# Optimizing a Trainium2 kernel written in Bass

```python
import numpy as np
import jax
import jax.numpy as jnp

def _softmax(x, axis=-1):
    return jax.nn.softmax(x, axis=axis)

def _gelu(x):
    return jax.nn.gelu(x, approximate=True)

def _silu(x):
    return jax.nn.silu(x)

def _sigmoid(x):
    return jax.nn.sigmoid(x)

def _layernorm(x, axis=-1, eps=1e-05):
    m = jnp.mean(x, axis=axis, keepdims=True)
    v = jnp.var(x, axis=axis, keepdims=True)
    return (x - m) / jnp.sqrt(v + eps)

def _scatter_add(tgt, idx, src, axis=0):
    return tgt.at[idx].add(src)

def _segment_sum(src, seg, n):
    return jax.ops.segment_sum(src, seg, n)
kernel_name = 'mk_pixart_resid_d1_seqx_r8_6f2fb1'

def setup_inputs(seed: int=0):
    np.random.seed(seed)
    _w = jnp.asarray

    def _rec_inputs():
        import jax
        import jax.numpy as jnp
        _rk = jax.random.key(seed)
        x = -0.0002928 + 1 * jax.random.normal(jax.random.fold_in(_rk, 1), (16, 128, 256), jnp.float32)
        _lenS = 128 - jax.random.randint(jax.random.fold_in(_rk, 7), (16,), 0, max(1, 128 // 4) + 1, jnp.int32)
        _lenS2 = 128 - jax.random.randint(jax.random.fold_in(_rk, 8), (16,), 0, max(1, 128 // 4) + 1, jnp.int32)
        _ctx_2048P = jax.random.normal(jax.random.fold_in(_rk, 11), (16, 16, 256), jnp.float32)
        _ctx_2048c = jax.random.dirichlet(jax.random.fold_in(_rk, 511), 0.3 * jnp.ones((16,), jnp.float32), (16, 128))
        _ctx_2048t = jnp.einsum('bsk,bkd->bsd', _ctx_2048c, _ctx_2048P)
        _ctx_2048t = _ctx_2048t * jax.lax.rsqrt(jnp.mean(jnp.square(_ctx_2048t)) + 1e-12) * 0.953939
        ctx_2048 = -1.39393e-06 + 0.999914 * (_ctx_2048t + 0.3 * jax.random.normal(jax.random.fold_in(_rk, 611), (16, 128, 256), jnp.float32))
        itok_B_779_1933 = jax.random.randint(jax.random.fold_in(_rk, 12), (16,), 779, 1934, jnp.int32)
        return (x, ctx_2048, itok_B_779_1933)
    x, ctx_2048, itok_B_779_1933 = _rec_inputs()

    def _L0_xcond_setup():
        import jax, jax.numpy as jnp
        import numpy as np
        NUM_HEADS = 8
        HEAD_DIM = 64
        AVG_K_LENGTH = 20
        SCALE = 1.0 / (HEAD_DIM ** 0.5 * float(np.log(AVG_K_LENGTH)))
        key = jax.random.key(seed)
        k1, k2, k3, k4 = jax.random.split(key, 4)
        B, HD, LQ, LK = (4, NUM_HEADS * HEAD_DIM, 256, 256)
        q = jax.random.normal(k1, (B, HD, LQ), dtype=jnp.float32)
        k = jax.random.normal(k2, (B, HD, LK), dtype=jnp.float32)
        v = jax.random.normal(k3, (B, HD, LK), dtype=jnp.float32)
        k_length = jax.random.randint(k4, (B,), 64, LK + 1, dtype=jnp.int32)
        return {'q': q, 'k': k, 'v': v, 'k_length': k_length}
    _L0_xcond_all = _L0_xcond_setup()
    _L0_xcond_in = {k: v for k, v in _L0_xcond_all.items() if k in ()}
    del _L0_xcond_all

    def _L0_ffn_setup():
        import jax, jax.numpy as jnp
        import numpy as np
        E, K = (12, 3)
        B, S, H, I = (2, 256, 256, 640)

        def _forward(x, Wr, br, w1, b1, w2, b2, Wp1, bp1, Wp2, bp2):
            logits = jnp.einsum('bsh,he->bse', x, Wr) + br
            probs = jax.nn.softmax(logits, axis=-1)
            top_vals, top_idx = jax.lax.top_k(probs, K)
            ew = jax.nn.softmax(top_vals, axis=-1)
            out = jnp.zeros_like(x)
            for e in range(E):
                sel = top_idx == e
                mask = sel.any(axis=-1)
                cnt = sel.sum()
                w_e = jnp.sum(jnp.where(sel, ew, 0.0)) / jnp.maximum(cnt, 1).astype(ew.dtype)
                h = jax.nn.relu(jnp.einsum('bsh,hi->bsi', x, w1[e]) + b1[e])
                h = jnp.einsum('bsi,ih->bsh', h, w2[e]) + b2[e]
                out = out + mask[..., None].astype(x.dtype) * (w_e * h)
            pooled = out.mean(axis=1)
            phi = jax.nn.sigmoid(jax.nn.relu(pooled @ Wp1 + bp1) @ Wp2 + bp2)
            phi_mask = (phi > 0.7).astype(out.dtype)[:, :, None]
            return out * (1.0 - phi_mask * 0.8)
        key = jax.random.key(seed)
        ks = jax.random.split(key, 8)
        sH = np.float32(1.0 / np.sqrt(H))
        sI = np.float32(1.0 / np.sqrt(I))
        sH2 = np.float32(1.0 / np.sqrt(H // 2))
        return {'hidden_states': jax.random.normal(ks[0], (B, S, H), jnp.float32), 'Wr': jax.random.normal(ks[1], (H, E), jnp.float32) * sH, 'br': jnp.zeros((E,), jnp.float32), 'w1': jax.random.normal(ks[2], (E, H, I), jnp.float32) * sH, 'b1': jnp.zeros((E, I), jnp.float32), 'w2': jax.random.normal(ks[3], (E, I, H), jnp.float32) * sI, 'b2': jnp.zeros((E, H), jnp.float32), 'Wp1': jax.random.normal(ks[4], (H, H // 2), jnp.float32) * sH, 'bp1': jnp.zeros((H // 2,), jnp.float32), 'Wp2': jax.random.normal(ks[5], (H // 2, 1), jnp.float32) * sH2, 'bp2': jnp.zeros((1,), jnp.float32)}
    _L0_ffn_all = _L0_ffn_setup()
    _L0_ffn_in = {k: v for k, v in _L0_ffn_all.items() if k in ('Wr', 'br', 'w1', 'b1', 'w2', 'b2', 'Wp1', 'bp1', 'Wp2', 'bp2')}
    del _L0_ffn_all
    return {'x': x, 'ctx_2048': ctx_2048, 'itok_B_779_1933': itok_B_779_1933, 'L0_ffn_Wr': _L0_ffn_in['Wr'], 'L0_ffn_br': _L0_ffn_in['br'], 'L0_ffn_w1': _L0_ffn_in['w1'], 'L0_ffn_b1': _L0_ffn_in['b1'], 'L0_ffn_w2': _L0_ffn_in['w2'], 'L0_ffn_b2': _L0_ffn_in['b2'], 'L0_ffn_Wp1': _L0_ffn_in['Wp1'], 'L0_ffn_bp1': _L0_ffn_in['bp1'], 'L0_ffn_Wp2': _L0_ffn_in['Wp2'], 'L0_ffn_bp2': _L0_ffn_in['bp2']}

def reference(x, ctx_2048, itok_B_779_1933, L0_ffn_Wr, L0_ffn_br, L0_ffn_w1, L0_ffn_b1, L0_ffn_w2, L0_ffn_b2, L0_ffn_Wp1, L0_ffn_bp1, L0_ffn_Wp2, L0_ffn_bp2):
    import jax
    import jax.numpy as jnp

    def _L0_xcond_ref(q, k, v, k_length):
        import jax, jax.numpy as jnp
        import numpy as np
        NUM_HEADS = 8
        HEAD_DIM = 64
        AVG_K_LENGTH = 20
        SCALE = 1.0 / (HEAD_DIM ** 0.5 * float(np.log(AVG_K_LENGTH)))
        b, hd, lq = q.shape
        lk = k.shape[-1]
        d = hd // NUM_HEADS
        qh = q.reshape(b, NUM_HEADS, d, lq)
        kh = k.reshape(b, NUM_HEADS, d, lk)
        vh = v.reshape(b, NUM_HEADS, d, lk)
        s = SCALE * jnp.log(k_length.astype(jnp.float32))[:, None, None, None]
        attn = jnp.einsum('bhdq,bhdk->bhqk', qh, kh)
        attn = jax.nn.softmax(s * attn, axis=-1)
        out = jnp.einsum('bhqk,bhdk->bhdq', attn, vh)
        return out.reshape(b, hd, lq)

    def _L0_ffn_ref(hidden_states, Wr, br, w1, b1, w2, b2, Wp1, bp1, Wp2, bp2):
        import jax, jax.numpy as jnp
        import numpy as np
        E, K = (12, 3)
        B, S, H, I = (2, 256, 256, 640)

        def _forward(x, Wr, br, w1, b1, w2, b2, Wp1, bp1, Wp2, bp2):
            logits = jnp.einsum('bsh,he->bse', x, Wr) + br
            probs = jax.nn.softmax(logits, axis=-1)
            top_vals, top_idx = jax.lax.top_k(probs, K)
            ew = jax.nn.softmax(top_vals, axis=-1)
            out = jnp.zeros_like(x)
            for e in range(E):
                sel = top_idx == e
                mask = sel.any(axis=-1)
                cnt = sel.sum()
                w_e = jnp.sum(jnp.where(sel, ew, 0.0)) / jnp.maximum(cnt, 1).astype(ew.dtype)
                h = jax.nn.relu(jnp.einsum('bsh,hi->bsi', x, w1[e]) + b1[e])
                h = jnp.einsum('bsi,ih->bsh', h, w2[e]) + b2[e]
                out = out + mask[..., None].astype(x.dtype) * (w_e * h)
            pooled = out.mean(axis=1)
            phi = jax.nn.sigmoid(jax.nn.relu(pooled @ Wp1 + bp1) @ Wp2 + bp2)
            phi_mask = (phi > 0.7).astype(out.dtype)[:, :, None]
            return out * (1.0 - phi_mask * 0.8)
        return _forward(hidden_states, Wr, br, w1, b1, w2, b2, Wp1, bp1, Wp2, bp2)
    x = x + _L0_xcond_ref(_layernorm(x, axis=-1), ctx_2048, ctx_2048, itok_B_779_1933)
    x = x + _L0_ffn_ref(_layernorm(x, axis=-1), L0_ffn_Wr, L0_ffn_br, L0_ffn_w1, L0_ffn_b1, L0_ffn_w2, L0_ffn_b2, L0_ffn_Wp1, L0_ffn_bp1, L0_ffn_Wp2, L0_ffn_bp2)
    return x

_drawn_inputs = setup_inputs


def setup_inputs(seed=0):
    import zlib

    import numpy as np

    out = dict(_drawn_inputs(seed))
    spreads = {'L0_ffn_br': (0.0, 0.1),
     'L0_ffn_b1': (0.0, 0.272),
     'L0_ffn_b2': (0.0, 0.1),
     'L0_ffn_bp1': (0.0, 0.1)}
    factors = {}
    for name, (base, spread) in spreads.items():
        noise = np.random.default_rng([zlib.crc32(name.encode()), seed]).standard_normal(out[name].shape)
        drawn = base * np.exp(spread * noise) if base else spread * noise
        out[name] = jnp.asarray(drawn.astype(out[name].dtype))
    for name, factor in factors.items():
        out[name] = (out[name] * factor).astype(out[name].dtype)
    return out
```

```python
import math

import concourse.bass as bass
from concourse import mybir
from contextlib import ExitStack

F32 = mybir.dt.float32
F16 = mybir.dt.float16
I32 = mybir.dt.int32
U16 = mybir.dt.uint16
ALU = mybir.AluOpType
ACT = mybir.ActivationFunctionType
AX = mybir.AxisListType

B, S, D = 16, 128, 256
HEADS, HD = 8, 16
PAIRS = HEADS // 2
E, TOPK, I = 12, 3, 640
KC, IC = D // 128, I // 128
EPS = 1e-5
SCALE = 1.0 / (64 ** 0.5 * math.log(20))
WS = 64.0
LEAD = 3
SLOTS = 128
TILES = B * S * TOPK // SLOTS + E - 1
CH = B * TOPK


def build(nc, x, ctx_in, klen, Wr, br, w1, b1, w2, b2, Wp1, bp1, Wp2, bp2, out):
    st = ExitStack()
    with st:
        def sb(name, shape, dt):
            return st.enter_context(nc.sbuf_tensor(name, shape, dt))

        def sem(name):
            return st.enter_context(nc.semaphore(name))

        parts_dram = nc.dram_tensor("qk_parts", (B, 2, 128, 4, D), F16, kind="Internal").ap()
        acc_dram = [nc.dram_tensor(f"acc{p}", (B * S + SLOTS, D), F32, kind="Internal").ap() for p in range(2)]
        xn2_dram = nc.dram_tensor("xn2", (B * S + 128, 2, D), F16, kind="Internal").ap()

        x_all = sb("x_all", [128, B, D], F32)
        w1s = sb("w1s", [128, E, 2, KC, I], F16)
        w2s = sb("w2s", [128, E, 2, IC, D], F16)
        ident = sb("ident", [128, 128], F32)
        ident16 = sb("ident16", [128, 128], F16)
        upper16 = sb("upper16", [128, 128], F16)
        ones16 = sb("ones16", [128, 128], F16)
        lg = sb("lg", [128, E], F32)
        lg_all = sb("lg_all", [128, B, E], F32)
        top8 = sb("top8", [128, 8], F32)
        top_all = sb("top_all", [128, B, TOPK], F32)
        idx8 = sb("idx8", [128, 8], U16)
        idx_all = sb("idx_all", [128, B, TOPK], F32)
        mask = sb("mask", [128, B, E], F16)
        seen = sb("seen", [128, B + 1, E], F16)
        iota_e = sb("iota_e", [128, E], F32)

        qkop = sb("qkop", [128, 2, 2, 2, PAIRS, D], F16)
        qop, kop = qkop[:, 0], qkop[:, 1]
        prob = sb("prob", [128, 2, PAIRS, KC, D], F32)
        vst = sb("vst", [128, 2, KC, PAIRS, 2, 32], F32)
        ones32 = sb("ones32", [128, 2, 32], F32)
        wstage = sb("wstage", [128, 2, KC * I], F32)
        parts = sb("parts", [128, 4, D], F16)
        qkf = sb("qkf", [128, 2, D], F32)
        ctx_k = sb("ctx_k", [128, 2, D], F32)
        ctx_v = sb("ctx_v", [128, 2, D], F32)
        att = sb("att", [128, D], F32)
        xn2 = sb("xn2s", [128, D], F32)
        xn2T = sb("xn2T", [128, KC, 128], F32)
        xn2hl = sb("xn2hl", [128, 2, D], F16)
        negm = sb("negm", [128, 2, PAIRS, 2], F16)
        negmT = sb("negmT", [8, 2, 128], F16)
        wr_s = sb("wr_s", [128, KC, E], F32)
        br_s = sb("br_s", [128, E], F32)
        klen_i = sb("klen_i", [128, B], I32)
        klen_f = sb("klen_f", [128, B], F32)
        lnk = sb("lnk", [128, B], F32)
        bn1 = sb("bn1", [128, 6], F32)
        mv1 = sb("mv1", [128, 2, 2], F32)
        rs1 = sb("rs1", [128, 2], F32)
        bn2 = sb("bn2", [128, 6], F32)
        mv2 = sb("mv2", [128, 2, 2], F32)
        rs2 = sb("rs2", [128, 2], F32)
        vpe = sb("vpe", [128, 2], F32)
        eps_s = sb("eps_s", [128, 1], F32)
        neghalf = sb("neghalf", [128, 1], F32)
        onehot = sb("onehot", [128, B, TOPK, E], F32)

        idx_tab = sb("idx_tab", [128, TILES + 1], I32)
        exp_tab = sb("exp_tab", [128, TILES + 1], I32)
        hid = sb("hid", [128, IC, SLOTS], F32)
        hid_lo = sb("hid_lo", [128, 2, IC, SLOTS], F16)
        pred = sb("pred", [128, 3], F32)
        zero_i = sb("zero_i", [128, 1], I32)
        row_of = sb("row_of", [128, 1], F32)
        b1T = sb("b1T", [128, E, IC], F32)
        w_e = sb("w_e", [128, 2, E], F32)
        tile_of = sb("tile_of", [128, CH], F32)
        slot_of = sb("slot_of", [128, CH], F32)
        gidx = [sb(f"gidx{p}", [128, 1], I32) for p in range(2)]
        sidx = [sb(f"sidx{p}", [128, 1], I32) for p in range(2)]

        def view(t, dt, first, shape, letters):
            dims = len(t.shape)
            names = " ".join("abcdefg"[:dims - 1])
            flat = t[:].rearrange(f"p {names} -> p ({names})") if dims > 2 else t[:]
            if dt != t.dtype:
                flat = flat.bitcast(dt)
            n = math.prod(shape)
            part = flat[:, first:first + n]
            if len(shape) == 1:
                return part
            names = " ".join(letters)
            return part.rearrange(f"p ({names}) -> p {names}", **dict(zip(letters[1:], shape[1:])))

        at_slot = view(prob, F16, 0, (CH, SLOTS), "ks")
        tile_cmp = view(prob, F32, CH * SLOTS // 2, (TILES + 1, E), "te")
        at_tile = view(wstage, F16, 0, (CH, TILES + 1), "kt")
        oh_val = view(wstage, F32, CH * (TILES + 1) // 2, (B, TOPK, E), "bce")
        lexp = view(parts, F32, 0, (B, E), "be")
        iota_s = view(parts, F16, 2 * 2 * B * E, (SLOTS,), "s")
        prefix = view(parts, F32, B * E, (B, E), "be")
        small = view(ctx_v, F32, 0, (10, CH), "nk")
        b2w = view(qkop, F32, 0, (E, D), "ed")
        xg = view(qkf, F16, 0, (2, 2, D), "rhf")
        xT = view(ctx_k, F16, 0, (2, 2 * KC, SLOTS), "rks")
        y = view(ctx_v, F32, 0, (2, D), "rf")
        hid_hi = view(vst, F16, 0, (2, IC, SLOTS), "ris")
        sum_w = view(xn2, F32, 0, (128,), "k")
        mean_w = view(xn2, F32, 128, (1,), "k")
        pooledT = view(xn2, F32, 132, (KC, B), "kb")
        z1T = view(xn2, F32, 164, (B,), "b")
        factor = view(xn2, F32, 180, (B,), "b")
        acc_s = [view(t, F32, 0, (B, D), "bd") for t in (prob, qkop)]
        wp1_s = xn2T
        b1s = att[0:E * IC, 0:128]
        zeros = hid[:].rearrange("p i s -> p (i s)")[:, 0:D]
        bank = [st.enter_context(nc.psum_tensor(f"bank{i}", [128, 512], F32)) for i in range(8)]
        sq = bank[0:2]
        sk = bank[2:4]
        av = bank[4:6]
        misc_a, misc_b = bank[6], bank[7]
        negm_ps = misc_a[:, 0:64].bitcast(F16)

        passed = sem("passed")
        pool_const, dve_const = sem("pool_const"), sem("dve_const")
        tables_loaded = sem("tables_loaded")
        x_first, x_rest = sem("x_first"), sem("x_rest")
        klen_float, lnk_ready = sem("klen_float"), sem("lnk_ready")
        ctxk_loaded = [sem("ctxk_even"), sem("ctxk_odd")]
        ctxv_loaded = [sem("ctxv_even"), sem("ctxv_odd")]
        bn1_ready, mv1_ready = sem("bn1_ready"), sem("mv1_ready")
        ve1_ready, rs1_ready = sem("ve1_ready"), sem("rs1_ready")
        qkf_ready, hi_ready, lo_ready = sem("qkf_ready"), sem("hi_ready"), sem("lo_ready")
        parts_stored = sem("parts_stored")
        qk_loaded = [[sem(f"qk_loaded{p}{g}") for g in range(2)] for p in range(2)]
        sq_ready, max_ready = sem("sq_ready"), sem("max_ready")
        negm_turned, negm_copied = sem("negm_turned"), sem("negm_copied")
        negm_loaded = [sem("negm_loaded0"), sem("negm_loaded1")]
        v_turned, v_ready = sem("v_turned"), sem("v_ready")
        sk_ready, prob_ready = sem("sk_ready"), sem("prob_ready")
        av_ready, rden_ready, att_ready = sem("av_ready"), sem("rden_ready"), sem("att_ready")
        x1_ready = sem("x1_ready")
        bn2_ready, mv2_ready = sem("bn2_ready"), sem("mv2_ready")
        ve2_ready, rs2_ready, xn2_ready = sem("ve2_ready"), sem("rs2_ready"), sem("xn2_ready")
        hi2_ready, lo2_ready, xn2_stored = sem("hi2_ready"), sem("lo2_ready"), sem("xn2_stored")
        xn2_turned, xn2T_ready = sem("xn2_turned"), sem("xn2T_ready")
        lg_summed, lg_ready, top_ready = sem("lg_summed"), sem("lg_ready"), sem("top_ready")
        idx_ready, idxf_ready, oh_ready = sem("idx_ready"), sem("idxf_ready"), sem("oh_ready")
        kept_ready = sem("kept_ready")
        mask_ready, seen_ready = sem("mask_ready"), sem("seen_ready")
        w_loaded = [sem("w_loaded0"), sem("w_loaded1")]
        whi_ready, wlo_ready = sem("whi_ready"), sem("wlo_ready")
        zeros_set, zeros_stored, pads_stored = sem("zeros_set"), sem("zeros_stored"), sem("pads_stored")
        counted, b1_loaded, b1_turned, b1T_ready = sem("counted"), sem("b1_loaded"), sem("b1_turned"), sem("b1T_ready")
        iotas_set, b2_loaded, pred_loaded = sem("iotas_set"), sem("b2_loaded"), sem("pred_loaded")
        table_made, tile_marked, table_summed = sem("table_made"), sem("tile_marked"), sem("table_summed")
        exp_made, weight_summed = sem("exp_made"), sem("weight_summed")
        gidx_ready, sidx_ready = sem("gidx_ready"), sem("sidx_ready")
        gathered = [sem("gathered_even"), sem("gathered_odd")]
        xg_turned, xT_ready = sem("xg_turned"), sem("xT_ready")
        h_summed, hid_ready, hid_hi_ready, hid_lo_ready = sem("h_summed"), sem("hid_ready"), sem("hid_hi_ready"), sem("hid_lo_ready")
        y_summed, y_ready = sem("y_summed"), sem("y_ready")
        scattered = [sem("scattered_even"), sem("scattered_odd")]
        acc_loaded = [sem(f"acc_loaded{q}") for q in range(4)]
        acc_summed = [sem(f"acc_summed{q}") for q in range(4)]
        pooled, pooledT_ready, z1_summed, z1_ready = sem("pooled"), sem("pooledT_ready"), sem("z1_summed"), sem("z1_ready")
        phi_summed, phi_exp, factor_ready = sem("phi_summed"), sem("phi_exp"), sem("factor_ready")
        scaled, out_stored = sem("scaled"), sem("out_stored")
        block = st.enter_context(nc.Block())

        def wait_some(eng, s, value):
            if not isinstance(value, int) or value > 0:
                eng.wait_ge(s, value)

        def wait_alone(eng, s, value):
            if not isinstance(value, int):
                eng.wait_ge(s, value)
                eng.sem_inc(passed, 1)
            elif value > 0:
                eng.wait_ge(s, value)

        def per_parity(b, par, n):
            return (b - par) * (n // 2) + n

        def batches(eng, iteration):
            for b in range(2):
                iteration(b, b % 2)
            with eng.Fori(1, E // 2 - 1) as two:
                iteration(two * 2, 0)
                iteration(two * 2 + 1, 1)
            for b in range(E - 2, B + LAST):
                iteration(b, b % 2)

        def has(b, lo=0, hi=B):
            return not isinstance(b, int) or lo <= b < hi

        STEPS = ["triangle", "cnt", "full", "tiles", "tri_tiles", "end", "base", "prefix", "oh_val", "pos", "pos_i",
                 "slot_i", "slot", "tile_i", "tile", "at_tile", "at_slot_1", "at_slot_2", "exp_cmp", "exp_sum", "exp_tab",
                 "idx_fill", "idx_tab", "l_sub", "top_sub", "z", "rz", "p3", "p3_sub", "ew_sum", "ew_rsum", "ew",
                 "oh_w", "w_part", "cnt_1", "cnt_r", "w_e", "w_e_ws", "b2w"]

        def made(step):
            return STEPS.index(step) + 1

        def tiles(eng, iteration):
            for t in range(2):
                iteration(t, t % 2)
            with eng.Fori(1, TILES // 2 - 1) as two:
                iteration(two * 2, 0)
                iteration(two * 2 + 1, 1)
            for t in range(TILES // 2 * 2 - 2, TILES + 1):
                iteration(t, t % 2)

        def tile_is(t, lo=0):
            return not isinstance(t, int) or lo <= t < TILES

        LAST = 2

        QB = B // 4

        def load_sums(eng, p):
            eng.wait_ge(y_ready, TILES)
            eng.wait_ge(scattered[p], 16 * ((TILES + 1 - p) // 2))
            for q in range(4):
                src = acc_dram[p][q * QB * S:(q + 1) * QB * S].rearrange("(b p) f -> p b f", p=S)
                eng.dma_start(acc_s[p][:, q * QB:(q + 1) * QB, :], src).then_inc(acc_loaded[q], 16)

        def store_out(eng, q):
            eng.wait_ge(scaled, QB * (q + 1))
            eng.dma_start(out[q * QB:(q + 1) * QB].rearrange("b p f -> p b f"),
                          acc_s[0][:, q * QB:(q + 1) * QB, :]).then_inc(out_stored, 16)

        @block.sync
        def _(sp):
            sp.dma_start(x_all[:, 0:2, :], x[0:2].rearrange("b p f -> p b f")).then_inc(x_first, 16)
            sp.dma_start(klen_i[:], klen.partition_broadcast(128)).then_inc(tables_loaded, 16)
            sp.dma_start(ctx_k[:, 0, :], ctx_in[0]).then_inc(ctxk_loaded[0], 16)
            sp.dma_start(ctx_k[:, 1, :], ctx_in[1]).then_inc(ctxk_loaded[1], 16)
            sp.dma_start(x_all[:, 2:B, :], x[2:B].rearrange("b p f -> p b f")).then_inc(x_rest, 16)
            sp.dma_start(ctx_v[:, 0, :], ctx_in[0]).then_inc(ctxv_loaded[0], 16)
            sp.dma_start(wr_s[:], Wr.rearrange("(c p) e -> p c e", p=128)).then_inc(tables_loaded, 16)
            sp.dma_start(br_s[:], br.partition_broadcast(128)).then_inc(tables_loaded, 16)

            def store_parts(b):
                wait_alone(sp, lo_ready, b + 1)
                sp.dma_start(parts_dram[b, 0].rearrange("p (r t) f -> p r (t f)", r=2),
                             parts[:, 0:2].rearrange("p t f -> p (t f)").unsqueeze(1).to_broadcast([128, 2, 2 * D])
                             ).then_inc(parts_stored, 16)
                sp.dma_start(parts_dram[b, 1, :, 0:2, :], parts[:, 2:4, :]).then_inc(parts_stored, 16)
                sp.dma_start(parts_dram[b, 1, :, 2:4, :], parts[:, 3:1:-1, :]).then_inc(parts_stored, 16)

            def load_ctx_k(b, par):
                wait_alone(sp, qkf_ready, 2 * b - 2)
                sp.dma_start(ctx_k[:, par, :], ctx_in[b]).then_inc(ctxk_loaded[par], 16)

            def load_qk(b, par, g):
                wait_alone(sp, parts_stored, 48 * b + 48)
                wait_alone(sp, sk_ready, 8 * (b - 2) + 4 * g + 4)
                for i, dst in ((0, qop), (1, kop)):
                    src = parts_dram[b, i].rearrange("(j g d) t f -> g (d t) j f", g=2, d=HD)[g]
                    sp.dma_start(dst[0:64, par, g], src).then_inc(qk_loaded[par][g], 16)

            def load_negm(b, par, g):
                wait_alone(sp, negm_copied, 2 * b + g + 1)
                sp.dma_start(qop[64:65, par, g].rearrange("o j (c q) -> o (j c) q", c=2),
                             negmT[0:8, g, :]).then_inc(negm_loaded[g], 16)

            def weights(b, i):
                wait_alone(sp, wlo_ready, 4 * (b - 1) + 2 * i + 2)
                src = (w1, w2)[i][bass.ds(b, 1)].rearrange("o (c p) i -> p (o c) i", p=128)
                sp.dma_start(wstage[:, i, :].rearrange("p (c i) -> p c i", c=(KC, IC)[i]), src).then_inc(w_loaded[i], 16)

            def iteration(b, par):
                if has(b):
                    load_negm(b, par, 1)
                if has(b + LEAD):
                    load_ctx_k(b + LEAD, 1 - par)
                if has(b + 1):
                    wait_alone(sp, v_turned, b)
                    sp.dma_start(ctx_v[:, 1 - par, :], ctx_in[b + 1]).then_inc(ctxv_loaded[1 - par], 16)
                if has(b + 2):
                    load_qk(b + 2, par, 0)
                if has(b + 1):
                    load_negm(b + 1, 1 - par, 0)
                if has(b + 1, 1, E):
                    weights(b + 1, 0)
                if has(b - 2):
                    wait_alone(sp, hi2_ready, b - 1)
                    wait_alone(sp, lo2_ready, b - 1)
                    sp.dma_start(xn2_dram[bass.ds((b - 2) * S, S)], xn2hl[:]).then_inc(xn2_stored, 16)
                if has(b + 2):
                    load_qk(b + 2, par, 1)
                if has(b + 1, 1, E):
                    weights(b + 1, 1)
                if has(b + LEAD):
                    store_parts(b + LEAD)
                if isinstance(b, int) and b == E:
                    sp.wait_ge(zeros_set, 2)
                    for a in acc_dram:
                        sp.dma_start(a.rearrange("(p r) f -> p r f", p=128),
                                     zeros.unsqueeze(1).to_broadcast([128, B + 1, D])).then_inc(zeros_stored, 16)
                    sp.dma_start(xn2_dram[B * S:B * S + SLOTS].rearrange("p h f -> p (h f)"),
                                 zeros.bitcast(F16)).then_inc(pads_stored, 16)
                    sp.dma_start(pred[:, 0:1], bp1.rearrange("(p o) -> p o", o=1)).then_inc(pred_loaded, 16)
                    sp.dma_start(pred[:, 1:2], Wp2).then_inc(pred_loaded, 16)
                    sp.dma_start(pred[:, 2:3], bp2.partition_broadcast(128)).then_inc(pred_loaded, 16)

            store_parts(0)
            for g in range(2):
                load_qk(0, 0, g)
            load_ctx_k(2, 0)
            store_parts(1)
            for g in range(2):
                load_qk(1, 1, g)
            load_negm(0, 0, 0)
            weights(0, 0)
            weights(0, 1)
            store_parts(2)
            batches(sp, iteration)
            sp.wait_ge(x1_ready, B)
            sp.dma_start(b1s, b1.rearrange("e (c i) -> (e c) i", i=128)).then_inc(b1_loaded, 16)
            sp.wait_ge(sk_ready, HEADS * B)
            sp.dma_start(b2w.rearrange("p e d -> p (e d)"),
                         b2.rearrange("e d -> (e d)").partition_broadcast(128)).then_inc(b2_loaded, 16)
            sp.wait_ge(lg_summed, B)
            sp.dma_start(wp1_s[:], Wp1.rearrange("(c p) j -> p c j", p=128)).then_inc(pred_loaded, 16)
            load_sums(sp, 0)
            for q in range(0, 4, 2):
                store_out(sp, q)
            sp.wait_ge(out_stored, 16 * 4)

        @block.gpsimd
        def _(pool):
            g = nc.gpsimd
            g.memset(neghalf[:], -0.5).then_inc(pool_const, 1)
            g.memset(eps_s[:], EPS).then_inc(pool_const, 1)
            for m, start in ((ident, 0.0), (ident16, 0.0), (upper16, 1.0)):
                g.memset(m[:], start).then_inc(pool_const, 1)
            g.memset(ones16[:], 1.0).then_inc(pool_const, 1)
            pool.wait_ge(pool_const, 6)
            g.memset(qop[64:128].bitcast(F32), 0.0).then_inc(pool_const, 1)
            pool.wait_ge(pool_const, 7)
            for m in (ident, ident16):
                g.affine_select(out=m[:], in_=m[:], compare_op=ALU.not_equal, fill=1.0, base=0,
                                pattern=[[-1, 128]], channel_multiplier=1).then_inc(pool_const, 1)
            g.affine_select(out=upper16[:], in_=upper16[:], compare_op=ALU.is_gt, fill=0.0, base=0,
                            pattern=[[1, 128]], channel_multiplier=-1).then_inc(pool_const, 1)
            g.iota(iota_e[:], pattern=[[1, E]], base=0, channel_multiplier=0,
                   allow_small_or_imprecise_dtypes=True).then_inc(pool_const, 1)

            g.iota(row_of[:], pattern=[[0, 1]], base=0, channel_multiplier=1,
                   allow_small_or_imprecise_dtypes=True).then_inc(pool_const, 1)
            g.memset(zeros, 0.0).then_inc(zeros_set, 1)
            g.memset(zero_i[:], 0).then_inc(zeros_set, 1)

            def rstd(mv, rs, b, par, mv_ready, ve_ready, rs_ready, k):
                wait_some(pool, rs_ready, b)
                pool.wait_ge(mv_ready, b + 1)
                g.tensor_tensor(vpe[:, k:k + 1], mv[:, par, 1:2], eps_s[:], ALU.add).then_inc(ve_ready, 1)
                pool.wait_ge(ve_ready, b + 1)
                g.tensor_tensor(rs[:, par:par + 1], vpe[:, k:k + 1], neghalf[:], ALU.pow).then_inc(rs_ready, 1)

            def low(b):
                pool.wait_ge(qkf_ready, 2 * b + 2)
                pool.wait_ge(hi_ready, b + 1)
                wait_some(pool, parts_stored, 48 * b)
                g.tensor_tensor(parts[:, 1:4:2, :], qkf[:], parts[:, 0:3:2, :], ALU.subtract).then_inc(lo_ready, 1)

            def iteration(b, par):
                if has(b - 1):
                    pool.wait_ge(att_ready, b)
                    g.tensor_tensor(x_all[:, bass.ds(b - 1, 1), :].squeeze(1), x_all[:, bass.ds(b - 1, 1), :].squeeze(1), att[:],
                                    ALU.add).then_inc(x1_ready, 1)
                    rstd(mv2, rs2, b - 1, 1 - par, mv2_ready, ve2_ready, rs2_ready, 1)
                    pool.wait_ge(xn2_ready, b)
                    pool.wait_ge(hi2_ready, b)
                    wait_some(pool, xn2_stored, 16 * (b - 1))
                    g.tensor_tensor(xn2hl[:, 1, :], xn2[:], xn2hl[:, 0, :], ALU.subtract).then_inc(lo2_ready, 1)
                if has(b + LEAD):
                    low(b + LEAD)
                if has(b + LEAD + 1):
                    rstd(mv1, rs1, b + LEAD + 1, par, mv1_ready, ve1_ready, rs1_ready, 0)

            rstd(mv1, rs1, 0, 0, mv1_ready, ve1_ready, rs1_ready, 0)
            rstd(mv1, rs1, 1, 1, mv1_ready, ve1_ready, rs1_ready, 0)
            low(0)
            low(1)
            rstd(mv1, rs1, 2, 0, mv1_ready, ve1_ready, rs1_ready, 0)
            low(2)
            rstd(mv1, rs1, 3, 1, mv1_ready, ve1_ready, rs1_ready, 0)
            batches(pool, iteration)

            pool.wait_ge(parts_stored, 48 * B)
            pool.wait_ge(v_turned, B)
            g.iota(iota_s, pattern=[[1, SLOTS]], base=0, channel_multiplier=0,
                   allow_small_or_imprecise_dtypes=True).then_inc(iotas_set, 1)
            g.iota(small[:, 9, :].rearrange("p (b c) -> p b c", c=TOPK), pattern=[[S, B], [0, TOPK]], base=-B * S,
                   channel_multiplier=1, allow_small_or_imprecise_dtypes=True).then_inc(iotas_set, 1)
            pool.wait_ge(lo2_ready, B)
            pool.wait_ge(xn2_turned, B)
            g.memset(sum_w, 1.0).then_inc(iotas_set, 1)
            g.memset(mean_w, 1.0 / S).then_inc(iotas_set, 1)
            pool.wait_ge(iotas_set, 4)
            pool.wait_ge(table_made, made("at_tile"))
            g.tensor_tensor(at_tile, at_tile, small[:, 9, :].unsqueeze(2).to_broadcast([128, CH, TILES + 1]),
                            ALU.mult).then_inc(tile_marked, 1)

            def gather(t, par):
                wait_alone(pool, gathered[par], (t - par) * 8)
                g.tensor_tensor(gidx[par][:], idx_tab[:, bass.ds(t, 1)], zero_i[:], ALU.add).then_inc(gidx_ready, 1)
                wait_alone(pool, gidx_ready, t + 1)
                wait_alone(pool, xg_turned, t - 1)
                g.indirect_dma_start(out=xg[:, par].rearrange("p h f -> p (h f)"), out_offset=None,
                                     in_=xn2_dram.rearrange("r h f -> r (h f)"),
                                     in_offset=bass.IndirectOffsetOnAxis(ap=gidx[par][:], axis=0),
                                     bounds_check=B * S + SLOTS - 1, oob_is_err=False).then_inc(gathered[par], 16)

            def scatter(t, par):
                wait_alone(pool, scattered[par], (t - par) * 8)
                g.tensor_tensor(sidx[par][:], idx_tab[:, bass.ds(t, 1)], zero_i[:], ALU.add).then_inc(sidx_ready, 1)
                wait_alone(pool, sidx_ready, t + 1)
                wait_alone(pool, y_ready, t + 1)
                g.indirect_dma_start(out=acc_dram[par], out_offset=bass.IndirectOffsetOnAxis(ap=sidx[par][:], axis=0),
                                     in_=y[:, par, :], in_offset=None, bounds_check=B * S + SLOTS - 1,
                                     oob_is_err=False, compute_op=ALU.add).then_inc(scattered[par], 16)

            pool.wait_ge(table_made, made("idx_tab"))
            pool.wait_ge(xn2_stored, 16 * B)
            pool.wait_ge(pads_stored, 16)
            pool.wait_ge(qkf_ready, 2 * B)
            for t in range(3):
                gather(t, t % 2)
            pool.wait_ge(zeros_stored, 32)

            def tile(t, par):
                if tile_is(t + 3):
                    gather(t + 3, 1 - par)
                if tile_is(t):
                    scatter(t, par)
            tiles(pool, tile)

            for q in range(1, 4, 2):
                pool.wait_ge(acc_loaded[q], 32)
                part = slice(q * QB, (q + 1) * QB)
                g.tensor_tensor(acc_s[0][:, part, :], acc_s[0][:, part, :], acc_s[1][:, part, :],
                                ALU.add).then_inc(acc_summed[q], 1)

        @block.scalar
        def _(act):
            a = nc.scalar
            act.wait_ge(klen_float, 1)
            a.activation(lnk[:], klen_f[:], ACT.Ln).then_inc(lnk_ready, 1)

            def high(b):
                act.wait_ge(qkf_ready, 2 * b + 2)
                wait_some(act, parts_stored, 48 * b)
                a.activation(parts[:, 0:3:2, :], qkf[:], ACT.Copy).then_inc(hi_ready, 1)

            def copy_negm(b, g):
                act.wait_ge(negm_turned, 2 * b + g + 1)
                wait_some(act, negm_loaded[g], 16 * b)
                a.activation(negmT[:, g, :], negm_ps[0:8, :], ACT.Copy).then_inc(negm_copied, 1)

            def copy_v(b, par):
                act.wait_ge(v_turned, b + 1)
                wait_some(act, av_ready, 2 * (b - 2) + 2)
                src = misc_a[:, 0:KC * 128].rearrange("p (c j g d) -> p c j g d", c=KC, g=2, d=HD)
                for g in range(2):
                    a.activation(vst[:, par, :, :, g, HD * g:HD * g + HD], src[:, :, :, g, :],
                                 ACT.Copy).then_inc(v_ready, 1)

            def exps(b, par, s):
                g, j = divmod(s, PAIRS)
                act.wait_ge(sk_ready, 8 * b + s + 1)
                if j == 0:
                    wait_some(act, av_ready, 2 * b + g - 1)
                a.activation(prob[:, g, j], sk[s % 2][:].rearrange("p (c q) -> p c q", c=KC),
                             ACT.Exp).then_inc(prob_ready, 1)

            def weight_hi(b, i, h):
                if h == 0:
                    act.wait_ge(w_loaded[i], 16 * b + 16)
                dst = (w1s, w2s)[i][:, bass.ds(b, 1), 0].rearrange("p o c n -> p (o c n)")
                n = KC * I // 2
                a.activation(dst[:, h * n:h * n + n], wstage[:, i, h * n:h * n + n], ACT.Copy,
                             scale=WS).then_inc(whi_ready, 1)

            def iteration(b, par):
                for s in range(HEADS):
                    if has(b):
                        exps(b, par, s)
                    if s == 0 and has(b - 2):
                        act.wait_ge(xn2_turned, b - 1)
                        a.activation(xn2T[:], misc_b[:, 0:256].rearrange("p (c t) -> p c t", c=KC),
                                     ACT.Copy).then_inc(xn2T_ready, 1)
                    if s == 2 and has(b):
                        copy_negm(b, 1)
                    if s == 6 and has(b + 1):
                        copy_negm(b + 1, 0)
                    if s == 7 and has(b + 1):
                        copy_v(b + 1, 1 - par)
                    if s in (1, 3, 4, 5) and has(b, 0, E):
                        k = (1, 3, 4, 5).index(s)
                        weight_hi(b, k // 2, k % 2)
                if has(b - 1):
                    act.wait_ge(xn2_ready, b)
                    wait_some(act, xn2_stored, 16 * (b - 1))
                    a.activation(xn2hl[:, 0, :], xn2[:], ACT.Copy).then_inc(hi2_ready, 1)
                if has(b + LEAD):
                    high(b + LEAD)

            high(0)
            high(1)
            copy_v(0, 0)
            copy_negm(0, 0)
            high(2)
            batches(act, iteration)

            act.wait_ge(b1_turned, 1)
            a.activation(b1T[:].rearrange("p e c -> p (e c)"), misc_b[:, 0:E * IC], ACT.Copy).then_inc(b1T_ready, 1)
            act.wait_ge(table_made, made("l_sub"))
            a.activation(lexp, lexp, ACT.Exp).then_inc(exp_made, 1)
            act.wait_ge(table_made, made("top_sub"))
            a.activation(small[:, 3, :], small[:, 3, :], ACT.Exp).then_inc(exp_made, 1)
            act.wait_ge(table_made, made("p3_sub"))
            a.activation(small[:, 4, :], small[:, 4, :], ACT.Exp).then_inc(exp_made, 1)
            act.wait_ge(b1T_ready, 1)
            act.wait_ge(zeros_stored, 32)
            act.wait_ge(pads_stored, 16)
            act.wait_ge(av_ready, 2 * B)

            def tile(t, par):
                if not tile_is(t):
                    return
                e = act.value_load(exp_tab[0:1, bass.ds(t, 1)], min_val=0, max_val=E - 1)
                for c in range(IC):
                    act.wait_ge(h_summed, IC * t + c + 1)
                    if c in (0, 3):
                        wait_some(act, hid_lo_ready, 2 * (t - 1) + (1 if c == 0 else 2))
                    a.activation(hid[:, c, :], bank[c][:, 0:SLOTS], ACT.Relu, bias=b1T[:, bass.ds(e, 1), c],
                                 scale=1.0 / WS).then_inc(hid_ready, 1)
                    if c in (2, 4):
                        first = 0 if c == 2 else 3
                        wait_alone(act, hid_ready, IC * t + c + 1)
                        wait_some(act, y_summed, t - 1)
                        a.activation(hid_hi[:, par, first:c + 1, :], hid[:, first:c + 1, :], ACT.Copy).then_inc(hid_hi_ready, 1)
            act.wait_ge(table_made, made("exp_tab"))
            tiles(act, tile)

            load_sums(act, 1)
            act.wait_ge(z1_summed, 1)
            a.activation(z1T, bank[0][:, 64:64 + B], ACT.Relu, bias=pred[:, 0:1]).then_inc(z1_ready, 1)
            act.wait_ge(phi_summed, 1)
            a.activation(factor, bank[0][:, 96:96 + B], ACT.Exp, bias=pred[:, 2:3], scale=-1.0).then_inc(phi_exp, 1)
            for q in range(1, 4, 2):
                store_out(act, q)

        @block.vector
        def _(dve):
            v = nc.vector
            v.memset(ones32[:], 0.0).then_inc(dve_const, 1)
            v.memset(vst[:], 0.0).then_inc(dve_const, 1)
            v.memset(seen[:, 0, :], 0.0).then_inc(dve_const, 1)
            v.memset(kop[64:128].bitcast(F32), 0.0).then_inc(dve_const, 1)
            dve.wait_ge(dve_const, 4)
            v.memset(ones32[:, 0, 0:HD], 1.0).then_inc(dve_const, 1)
            v.memset(ones32[:, 1, HD:2 * HD], 1.0).then_inc(dve_const, 1)
            v.memset(kop[64:65], 1.0).then_inc(dve_const, 1)
            dve.wait_ge(tables_loaded, 48)
            v.tensor_copy(klen_f[:], klen_i[:]).then_inc(klen_float, 1)

            def stats(b, par, bn, mv, bn_ready, mv_ready):
                wait_some(dve, mv_ready, b)
                v.bn_stats(bn[:], x_all[:, bass.ds(b, 1), :].squeeze(1)).then_inc(bn_ready, 1)
                wait_alone(dve, qkf_ready if bn is bn1 else xn2_ready, 2 * b - 3 if bn is bn1 else b - 1)
                wait_alone(dve, bn_ready, b + 1)
                v.bn_aggr(mv[:, par, :], bn[:]).then_inc(mv_ready, 1)

            def operands(b, par):
                dve.wait_ge(rs1_ready, b + 1)
                wait_some(dve, lo_ready, b)
                v.tensor_scalar(qkf[:, 0, :], x_all[:, bass.ds(b, 1), :].squeeze(1), mv1[:, par, 0:1], rs1[:, par:par + 1],
                                ALU.subtract, ALU.mult).then_inc(qkf_ready, 1)
                dve.wait_ge(ctxk_loaded[par], per_parity(b, par, 16))
                v.tensor_scalar(qkf[:, 1, :], ctx_k[:, par, :], lnk[:, bass.ds(b, 1)], SCALE,
                                ALU.mult, ALU.mult).then_inc(qkf_ready, 1)

            def maximum(b, s):
                g, j = divmod(s, PAIRS)
                dve.wait_ge(sq_ready, 8 * b + s + 1)
                if j == 0:
                    wait_some(dve, negm_turned, 2 * (b - 1) + g + 1)
                v.tensor_reduce(negm[:, g, j], sq[s % 2][:].rearrange("p (c k) -> p c k", c=2), AX.X, ALU.max,
                                negate=True).then_inc(max_ready, 1)

            def weight_lo(b, i, h):
                dve.wait_ge(whi_ready, 4 * b + 2 * i + h + 1)
                n = KC * I // 2
                t = (w1s, w2s)[i][:, bass.ds(b, 1)]
                hi = t[:, :, 0].rearrange("p o c n -> p (o c n)")[:, h * n:h * n + n]
                lo = t[:, :, 1].rearrange("p o c n -> p (o c n)")[:, h * n:h * n + n]
                v.scalar_tensor_tensor(lo, wstage[:, i, h * n:h * n + n], WS, hi, ALU.mult,
                                       ALU.subtract).then_inc(wlo_ready, 1)

            def route(b, step):
                bb = bass.ds(b, 1)
                if step == 0:
                    dve.wait_ge(lg_summed, b + 1)
                    wait_some(dve, kept_ready, 2 * b)
                    wait_some(dve, mask_ready, b)
                    v.tensor_tensor(lg[:], misc_b[:, 0:E], br_s[:], ALU.add).then_inc(lg_ready, 1)
                elif step == 1:
                    wait_alone(dve, lg_ready, b + 1)
                    v.max(top8[:], lg[:]).then_inc(top_ready, 1)
                elif step == 2:
                    wait_alone(dve, top_ready, b + 1)
                    v.max_index(idx8[:], top8[:], lg[:]).then_inc(idx_ready, 1)
                    v.tensor_scalar(lg_all[:, bb, :].squeeze(1), lg[:], 0.0, None, ALU.add).then_inc(kept_ready, 1)
                    v.tensor_scalar(top_all[:, bb, :].squeeze(1), top8[:, 0:TOPK], 0.0, None,
                                    ALU.add).then_inc(kept_ready, 1)
                elif step == 3:
                    dve.wait_ge(idx_ready, b + 1)
                    v.tensor_scalar(idx_all[:, bb, :].squeeze(1), idx8[:, 0:TOPK], 0.0, None,
                                    ALU.add).then_inc(idxf_ready, 1)
                elif step == 4:
                    dve.wait_ge(idxf_ready, b + 1)
                    v.tensor_tensor(onehot[:, bb].squeeze(1), iota_e[:].unsqueeze(1).to_broadcast([128, TOPK, E]),
                                    idx_all[:, bb, :].squeeze(1).unsqueeze(2).to_broadcast([128, TOPK, E]),
                                    ALU.is_equal).then_inc(oh_ready, 1)
                elif step == 5:
                    dve.wait_ge(oh_ready, b + 1)
                    with nc.allow_low_precision("zeros and ones are exact in float16"):
                        v.tensor_reduce(mask[:, bb, :].squeeze(1), onehot[:, bb].squeeze(1).rearrange("p c e -> p e c"), AX.X,
                                        ALU.add).then_inc(mask_ready, 1)
                elif step == 6:
                    dve.wait_ge(mask_ready, b + 1)
                    v.tensor_tensor(seen[:, bass.ds(b + 1, 1), :].squeeze(1), seen[:, bb, :].squeeze(1),
                                    mask[:, bb, :].squeeze(1), ALU.add).then_inc(seen_ready, 1)

            def iteration(b, par):
                for s in range(HEADS):
                    if has(b + 1):
                        maximum(b + 1, s)
                    if s >= 3 and has(b - 2):
                        route(b - 2, s - 3)
                    if s == 4 and has(b - 1):
                        dve.wait_ge(av_ready, 2 * b)
                        wait_some(dve, x1_ready, b - 1)
                        v.reciprocal(att[:], av[1 - par][:, D:2 * D]).then_inc(rden_ready, 1)
                        dve.wait_ge(rden_ready, b)
                        v.tensor_tensor(att[:], av[1 - par][:, 0:D], att[:], ALU.mult).then_inc(att_ready, 1)
                    if s == 6 and has(b - 1):
                        dve.wait_ge(x1_ready, b)
                        stats(b - 1, 1 - par, bn2, mv2, bn2_ready, mv2_ready)
                    if s in (1, 2, 4, 5) and has(b, 0, E):
                        k = (1, 2, 4, 5).index(s)
                        weight_lo(b, k // 2, k % 2)
                if has(b + LEAD):
                    operands(b + LEAD, 1 - par)
                if has(b - 2):
                    route(b - 2, 5)
                if has(b - 1):
                    dve.wait_ge(rs2_ready, b)
                    wait_some(dve, lo2_ready, b - 1)
                    wait_some(dve, xn2_turned, b - 1)
                    v.tensor_scalar(xn2[:], x_all[:, bass.ds(b - 1, 1), :].squeeze(1), mv2[:, 1 - par, 0:1],
                                    rs2[:, 1 - par:2 - par], ALU.subtract, ALU.mult).then_inc(xn2_ready, 1)
                if has(b + LEAD + 1):
                    stats(b + LEAD + 1, par, bn1, mv1, bn1_ready, mv1_ready)
                if has(b - 2):
                    route(b - 2, 6)

            dve.wait_ge(x_first, 16)
            stats(0, 0, bn1, mv1, bn1_ready, mv1_ready)
            stats(1, 1, bn1, mv1, bn1_ready, mv1_ready)
            dve.wait_ge(lnk_ready, 1)
            operands(0, 0)
            operands(1, 1)
            dve.wait_ge(x_rest, 16)
            stats(2, 0, bn1, mv1, bn1_ready, mv1_ready)
            stats(3, 1, bn1, mv1, bn1_ready, mv1_ready)
            for s in range(HEADS):
                maximum(0, s)
            operands(2, 0)
            batches(dve, iteration)

            def turned_rows(t, par):
                dve.wait_ge(xg_turned, t + 1)
                wait_some(dve, h_summed, IC * (t - 1))
                v.tensor_copy(xT[:, par].rearrange("p k s -> p (k s)"), bank[5][:].bitcast(F16)[:, 0:2 * KC * SLOTS]
                              ).then_inc(xT_ready, 1)

            done = [0]

            def step(name, op):
                assert STEPS[done[0]] == name
                done[0] += 1
                op.then_inc(table_made, 1)

            def after(name):
                dve.wait_ge(table_made, made(name))

            def tt(name, o, i0, i1, op):
                step(name, v.tensor_tensor(o, i0, i1, op))

            small_exp = prefix.rearrange("p b e -> p (b e)")[:, 0:TILES + 1]
            cnt_ps, prefix_ps = misc_a[:, B * E:B * E + E], misc_a[:, 0:B * E].rearrange("p (b e) -> p b e", e=E)
            tri = tile_cmp[:, 0:E, :]
            full = tile_cmp[:, E:2 * E + 4, :].rearrange("p t e -> p (t e)").rearrange("p (e k) -> p e k", k=B)
            num = small[:, :, 0:E]
            cnt, n_tiles, end, base = num[:, 5], num[:, 6], num[:, 7], num[:, 8]
            pos = small[:, 0, :]
            pos_i, cut_i, cut2_i = small[:, 1, :].bitcast(I32), small[:, 2, :].bitcast(I32), small[:, 3, :].bitcast(I32)
            dve.wait_ge(iotas_set, 4)
            dve.wait_ge(wlo_ready, 4 * E)
            dve.wait_ge(av_ready, 2 * B)
            tt("triangle", tri, iota_e[:].unsqueeze(2).to_broadcast([128, E, E]),
               iota_e[:].unsqueeze(1).to_broadcast([128, E, E]), ALU.is_ge)
            dve.wait_ge(counted, 1)
            step("cnt", v.tensor_scalar(cnt, cnt_ps, 1.0 / SLOTS, None, ALU.mult))
            after("cnt")
            tt("full", full, cnt.unsqueeze(2).to_broadcast([128, E, B]),
               iota_s[:, 0:B].unsqueeze(1).to_broadcast([128, E, B]), ALU.is_gt)
            after("full")
            step("tiles", v.tensor_reduce(n_tiles, full, AX.X, ALU.add))
            after("tiles")
            tt("tri_tiles", tri, tri, n_tiles.unsqueeze(1).to_broadcast([128, E, E]), ALU.mult)
            after("tri_tiles")
            step("end", v.tensor_reduce(end, tri, AX.X, ALU.add))
            after("end")
            tt("base", base, end, n_tiles, ALU.subtract)
            after("base")
            step("prefix", v.scalar_tensor_tensor(prefix, base.unsqueeze(1).to_broadcast([128, B, E]), float(SLOTS),
                                                  prefix_ps, ALU.mult, ALU.add))
            after("prefix")
            tt("oh_val", oh_val, onehot[:], prefix.unsqueeze(2).to_broadcast([128, B, TOPK, E]), ALU.mult)
            after("oh_val")
            step("pos", v.tensor_reduce(pos.rearrange("p (b c) -> p b c", c=TOPK), oh_val, AX.X, ALU.add))
            after("pos")
            step("pos_i", v.tensor_scalar(pos_i, pos, 0.0, None, ALU.add))
            after("pos_i")
            step("slot_i", v.tensor_scalar(cut_i, pos_i, SLOTS - 1, None, ALU.bitwise_and))
            after("slot_i")
            step("slot", v.tensor_scalar(slot_of[:], cut_i, 0.0, None, ALU.add))
            step("tile_i", v.tensor_scalar(cut2_i, pos_i, SLOTS.bit_length() - 1, None, ALU.arith_shift_right))
            after("tile_i")
            step("tile", v.tensor_scalar(tile_of[:], cut2_i, 0.0, None, ALU.add))
            after("tile")
            tt("at_tile", at_tile, iota_s[:, 0:TILES + 1].unsqueeze(1).to_broadcast([128, CH, TILES + 1]),
               tile_of[:].unsqueeze(2).to_broadcast([128, CH, TILES + 1]), ALU.is_equal)
            for h in range(2):
                k = slice(h * CH // 2, (h + 1) * CH // 2)
                tt(f"at_slot_{h + 1}", at_slot[:, k, :], iota_s.unsqueeze(1).to_broadcast([128, CH // 2, SLOTS]),
                   slot_of[:, k].unsqueeze(2).to_broadcast([128, CH // 2, SLOTS]), ALU.is_equal)
            tt("exp_cmp", tile_cmp, iota_s[:, 0:TILES + 1].unsqueeze(2).to_broadcast([128, TILES + 1, E]),
               end.unsqueeze(1).to_broadcast([128, TILES + 1, E]), ALU.is_ge)
            after("exp_cmp")
            step("exp_sum", v.tensor_reduce(small_exp, tile_cmp, AX.X, ALU.add))
            after("exp_sum")
            step("exp_tab", v.tensor_scalar(exp_tab[:], small_exp, float(E - 1), None, ALU.min))
            dve.wait_ge(table_summed, 1)
            T = misc_b[:, 64:64 + TILES + 1]
            fill = tile_cmp[:, 0:5, :].rearrange("p t e -> p (t e)")
            after("exp_sum")
            step("idx_fill", v.tensor_scalar(fill, T, 0.0, row_of[:], ALU.is_equal, ALU.mult))
            after("idx_fill")
            step("idx_tab", v.scalar_tensor_tensor(idx_tab[:], T, float(B * S), fill, ALU.add, ALU.add))

            def ch(k):
                return small[:, k, :].rearrange("p (b c) -> p b c", c=TOPK)

            s0, s1 = ch(3), ch(4)
            z, rz = small[:, 2, 0:B], small[:, 2, B:2 * B]
            def first(x):
                return x[:, :, 0:1].to_broadcast([128, B, x.shape[2]])
            tt("l_sub", lexp, lg_all[:], top_all[:, :, 0:1].to_broadcast([128, B, E]), ALU.subtract)
            tt("top_sub", s0, top_all[:], top_all[:, :, 0:1].to_broadcast([128, B, TOPK]), ALU.subtract)
            dve.wait_ge(exp_made, 1)
            step("z", v.tensor_reduce(z, lexp, AX.X, ALU.add))
            after("z")
            step("rz", v.reciprocal(rz, z))
            after("rz")
            dve.wait_ge(exp_made, 2)
            tt("p3", s0, s0, rz.unsqueeze(2).to_broadcast([128, B, TOPK]), ALU.mult)
            after("p3")
            tt("p3_sub", s1, s0, s0[:, :, 0:1].to_broadcast([128, B, TOPK]), ALU.subtract)
            dve.wait_ge(exp_made, 3)
            step("ew_sum", v.tensor_reduce(z, s1, AX.X, ALU.add))
            after("ew_sum")
            step("ew_rsum", v.reciprocal(rz, z))
            after("ew_rsum")
            tt("ew", s1, s1, rz.unsqueeze(2).to_broadcast([128, B, TOPK]), ALU.mult)
            after("ew")
            tt("oh_w", oh_val, onehot[:], s1.unsqueeze(3).to_broadcast([128, B, TOPK, E]), ALU.mult)
            after("oh_w")
            step("w_part", v.tensor_reduce(num[:, 7], oh_val.rearrange("p b c e -> p e (b c)"), AX.X, ALU.add))
            step("cnt_1", v.tensor_scalar(num[:, 1], cnt_ps, 1.0, None, ALU.max))
            after("cnt_1")
            step("cnt_r", v.reciprocal(num[:, 8], num[:, 1]))
            after("cnt_r")
            turned_rows(0, 0)
            dve.wait_ge(weight_summed, 1)
            tt("w_e", w_e[:, 0], misc_b[:, 128:128 + E], num[:, 8], ALU.mult)
            after("w_e")
            step("w_e_ws", v.tensor_scalar(w_e[:, 1], w_e[:, 0], 1.0 / WS, None, ALU.mult))
            dve.wait_ge(b2_loaded, 16)
            tt("b2w", b2w, b2w, w_e[:, 0].unsqueeze(2).to_broadcast([128, E, D]), ALU.mult)
            after("b2w")
            dve.wait_ge(pred_loaded, 64)
            v.tensor_scalar(pred[:, 2:3], pred[:, 2:3], -1.0, None, ALU.mult).then_inc(table_made, 1)

            def low_parts(t, par):
                for h, (first_c, last_c) in enumerate(((0, 3), (3, IC))):
                    wait_some(dve, y_summed, t - 1)
                    dve.wait_ge(hid_hi_ready, 2 * t + h + 1)
                    v.tensor_tensor(hid_lo[:, par, first_c:last_c, :], hid[:, first_c:last_c, :],
                                    hid_hi[:, par, first_c:last_c, :], ALU.subtract).then_inc(hid_lo_ready, 1)

            def output(t, par):
                e = dve.value_load(exp_tab[0:1, bass.ds(t, 1)], min_val=0, max_val=E - 1)
                wait_alone(dve, y_summed, t + 1)
                wait_alone(dve, scattered[par], (t - par) * 8)
                v.scalar_tensor_tensor(y[:, par, :], bank[6 + par][:, 0:D], w_e[:, 1, bass.ds(e, 1)],
                                       b2w[:, bass.ds(e, 1), :].squeeze(1), ALU.mult, ALU.add).then_inc(y_ready, 1)

            def tile(t, par):
                if tile_is(t):
                    low_parts(t, par)
                if tile_is(t - 1):
                    output(t - 1, 1 - par)
                if tile_is(t + 2):
                    turned_rows(t + 2, par)
            turned_rows(1, 1)
            tiles(dve, tile)

            for q in range(0, 4, 2):
                dve.wait_ge(acc_loaded[q], 32)
                part = slice(q * QB, (q + 1) * QB)
                v.tensor_tensor(acc_s[0][:, part, :], acc_s[0][:, part, :], acc_s[1][:, part, :],
                                ALU.add).then_inc(acc_summed[q], 1)
            dve.wait_ge(pooled, 1)
            v.tensor_copy(pooledT.rearrange("p k b -> p (k b)"), bank[0][:, 0:KC * B]).then_inc(pooledT_ready, 1)
            dve.wait_ge(phi_exp, 1)
            v.tensor_scalar(factor, factor, 1.0, None, ALU.add).then_inc(factor_ready, 1)
            dve.wait_ge(factor_ready, 1)
            v.reciprocal(factor, factor).then_inc(factor_ready, 1)
            dve.wait_ge(factor_ready, 2)
            v.tensor_scalar(factor, factor, 0.7, -0.8, ALU.is_gt, ALU.mult).then_inc(factor_ready, 1)
            dve.wait_ge(factor_ready, 3)
            v.tensor_scalar(factor, factor, 1.0, None, ALU.add).then_inc(factor_ready, 1)
            dve.wait_ge(factor_ready, 4)
            dve.wait_ge(acc_summed[1], 1)
            dve.wait_ge(acc_summed[3], 1)
            for b in range(B):
                v.scalar_tensor_tensor(acc_s[0][:, b, :], acc_s[0][:, b, :], factor[:, b:b + 1], x_all[:, b, :],
                                       ALU.mult, ALU.add).then_inc(scaled, 1)

        @block.tensor
        def _(pe):
            t = nc.tensor

            def scores_q(b, par, s):
                g, j = divmod(s, PAIRS)
                if j == 0:
                    pe.wait_ge(qk_loaded[par][g], per_parity(b, par, 32))
                wait_some(pe, max_ready, 8 * b + s - 1)
                for c in range(2):
                    mm = t.matmul(sq[s % 2][:, c * D:(c + 1) * D], qop[0:64, par, g, j, c * 128:(c + 1) * 128],
                                  kop[0:64, par, g, j, :], start=True, stop=True)
                mm.then_inc(sq_ready, 1)

            def scores_k(b, par, s):
                g, j = divmod(s, PAIRS)
                if j == 0:
                    pe.wait_ge(negm_loaded[g], 16 * b + 16)
                wait_some(pe, prob_ready, 8 * b + s - 1)
                for c in range(KC):
                    mm = t.matmul(sk[s % 2][:, c * D:(c + 1) * D], kop[:, par, g, j, c * 128:(c + 1) * 128],
                                  qop[:, par, g, j, :], start=True, stop=True)
                mm.then_inc(sk_ready, 1)

            def sums(b, par, g, quarter):
                c, what = divmod(quarter, 2)
                if quarter == 0:
                    pe.wait_ge(prob_ready, 8 * b + 4 * g + 4)
                    if g == 0:
                        pe.wait_ge(v_ready, 2 * b + 2)
                        wait_some(pe, att_ready, b - 1)
                for j in range(PAIRS):
                    lhs = vst[:, par, c, j, g, :] if what == 0 else ones32[:, g, :]
                    mm = t.matmul(av[par][32 * j:32 * j + 32, what * D:(what + 1) * D], lhs, prob[:, g, j, c, :],
                                  start=(g == 0 and quarter == 0), stop=(g == 1 and c == 1),
                                  skip_group_check=True)
                if quarter == 3:
                    mm.then_inc(av_ready, 1)

            def turn_negm(b, g):
                pe.wait_ge(max_ready, 8 * b + 4 * g + 4)
                if g == 1 or (isinstance(b, int) and b == 0):
                    pe.wait_ge(v_ready, 2 * b + 2)
                else:
                    pe.wait_ge(negm_copied, 2 * b)
                t.transpose(negm_ps[0:8, :], negm[:, g].rearrange("p j c -> p (j c)"),
                            ident16[:]).then_inc(negm_turned, 1)

            def turn_v(b, par):
                pe.wait_ge(ctxv_loaded[par], per_parity(b, par, 16))
                if not (isinstance(b, int) and b == 0):
                    pe.wait_ge(negm_copied, 2 * b + 1)
                for c in range(KC):
                    mm = t.transpose(misc_a[:, c * 128:(c + 1) * 128], ctx_v[:, par, c * 128:(c + 1) * 128], ident[:])
                mm.then_inc(v_turned, 1)

            def turn_xn2(b):
                pe.wait_ge(xn2_ready, b + 1)
                wait_some(pe, lg_ready, b)
                for c in range(KC):
                    mm = t.transpose(misc_b[:, c * 128:(c + 1) * 128], xn2[:, c * 128:(c + 1) * 128], ident[:])
                mm.then_inc(xn2_turned, 1)

            def router(b):
                pe.wait_ge(xn2T_ready, b + 1)
                for c in range(KC):
                    mm = t.matmul(misc_b[:, 0:E], xn2T[:, c, :], wr_s[:, c, :], start=(c == 0), stop=(c == KC - 1))
                mm.then_inc(lg_summed, 1)

            def iteration(b, par):
                for s in range(HEADS):
                    if has(b + 1):
                        scores_q(b + 1, 1 - par, s)
                    if has(b):
                        scores_k(b, par, s)
                    if s < 4 and has(b - 1):
                        sums(b - 1, 1 - par, 1, s)
                    if s >= 4 and has(b):
                        sums(b, par, 0, s - 4)
                    if s == 1 and has(b):
                        turn_negm(b, 1)
                    if s == 2 and has(b - 2):
                        router(b - 2)
                    if s == 5 and has(b + 1):
                        turn_negm(b + 1, 0)
                    if s == 6 and has(b + 1):
                        turn_v(b + 1, 1 - par)
                    if s == 7 and has(b - 1):
                        turn_xn2(b - 1)

            pe.wait_ge(pool_const, 11)
            pe.wait_ge(dve_const, 7)
            turn_v(0, 0)
            for s in range(HEADS):
                scores_q(0, 0, s)
            turn_negm(0, 0)
            batches(pe, iteration)

            pe.wait_ge(seen_ready, B)
            pe.wait_ge(negm_copied, 2 * B)
            pe.wait_ge(v_ready, 2 * B)
            pe.wait_ge(lg_ready, B)
            flat = "p b e -> p (b e)"
            t.matmul(misc_a[:, 0:B * E], upper16[:], mask[:].rearrange(flat), start=True, stop=False)
            t.matmul(misc_a[:, 0:B * E], ones16[:], seen[:, 0:B].rearrange(flat), start=False, stop=True)
            t.matmul(misc_a[:, B * E:B * E + E], ones16[:], seen[:, B, :], start=True, stop=True).then_inc(counted, 1)
            pe.wait_ge(b1_loaded, 16)
            t.transpose(misc_b[:, 0:E * IC], b1s, ident[0:E * IC, 0:E * IC]).then_inc(b1_turned, 1)
            pe.wait_ge(tile_marked, 1)
            pe.wait_ge(b1T_ready, 1)
            for k in range(CH):
                if k % (CH // 2) == 0:
                    pe.wait_ge(table_made, made("at_slot_1") + k // (CH // 2))
                mm = t.matmul(misc_b[:, 64:64 + TILES + 1], at_slot[:, k, :], at_tile[:, k, :], start=(k == 0),
                              stop=(k == CH - 1))
            mm.then_inc(table_summed, 1)

            def turn_rows(n, par):
                pe.wait_ge(gathered[par], (n - par) * 8 + 16)
                wait_some(pe, xT_ready, n)
                for k in range(2 * KC):
                    mm = t.transpose(bank[5][:].bitcast(F16)[:, k * SLOTS:(k + 1) * SLOTS],
                                     xg[:, par, k // KC, (k % KC) * 128:(k % KC) * 128 + 128], ident16[:])
                mm.then_inc(xg_turned, 1)

            def hidden(n, par):
                e = pe.value_load(exp_tab[0:1, bass.ds(n, 1)], min_val=0, max_val=E - 1)
                pe.wait_ge(xT_ready, n + 1)
                for c in range(IC):
                    wait_some(pe, hid_ready, IC * (n - 1) + c + 1)
                    dst = bank[c][:, 0:SLOTS]
                    terms = [(wp, xp, k) for k in range(KC) for wp, xp in ((0, 0), (0, 1), (1, 0))]
                    for i, (wp, xp, k) in enumerate(terms):
                        mm = t.matmul(dst, w1s[:, bass.ds(e, 1), wp, k, c * 128:(c + 1) * 128].squeeze(1),
                                      xT[:, par, xp * KC + k, :], start=(i == 0), stop=(i == len(terms) - 1))
                    mm.then_inc(h_summed, 1)

            def outputs(n, par):
                e = pe.value_load(exp_tab[0:1, bass.ds(n, 1)], min_val=0, max_val=E - 1)
                wait_some(pe, y_ready, n - 1)
                terms = [(c, hp, wp) for c in range(IC) for hp, wp in ((0, 0), (0, 1), (1, 0))]
                for i, (c, hp, wp) in enumerate(terms):
                    if i in (0, 9):
                        pe.wait_ge(hid_lo_ready, 2 * n + (1 if i == 0 else 2))
                    mm = t.matmul(bank[6 + par][:, 0:D], (hid_hi, hid_lo)[hp][:, par, c, :],
                                  w2s[:, bass.ds(e, 1), wp, c, :].squeeze(1), start=(i == 0), stop=(i == len(terms) - 1))
                mm.then_inc(y_summed, 1)

            turn_rows(0, 0)
            pe.wait_ge(table_made, made("w_part"))
            t.matmul(misc_b[:, 128:128 + E], sum_w, small[:, 7, 0:E], start=True, stop=True).then_inc(weight_summed, 1)
            turn_rows(1, 1)
            hidden(0, 0)
            pe.wait_ge(table_made, made("w_e"))

            def tile(n, par):
                if tile_is(n + 2):
                    turn_rows(n + 2, par)
                if tile_is(n + 1):
                    hidden(n + 1, 1 - par)
                if tile_is(n):
                    outputs(n, par)
            tiles(pe, tile)

            for b in range(B):
                if b % QB == 0:
                    pe.wait_ge(acc_summed[b // QB], 1)
                for k in range(KC):
                    mm = t.matmul(bank[0][:, k * B + b:k * B + b + 1], acc_s[0][:, b, k * 128:(k + 1) * 128], mean_w,
                                  start=True, stop=True)
            mm.then_inc(pooled, 1)
            pe.wait_ge(pooledT_ready, 1)
            for k in range(KC):
                mm = t.matmul(bank[0][:, 64:64 + B], wp1_s[:, k, :], pooledT[:, k, :], start=(k == 0), stop=(k == KC - 1))
            mm.then_inc(z1_summed, 1)
            pe.wait_ge(z1_ready, 1)
            t.matmul(bank[0][:, 96:96 + B], pred[:, 1:2].to_broadcast([128, 128]), z1T, start=True,
                     stop=True).then_inc(phi_summed, 1)


_INS = ["x", "ctx_2048", "itok_B_779_1933", "L0_ffn_Wr", "L0_ffn_br", "L0_ffn_w1", "L0_ffn_b1", "L0_ffn_w2",
        "L0_ffn_b2", "L0_ffn_Wp1", "L0_ffn_bp1", "L0_ffn_Wp2", "L0_ffn_bp2"]


def kernel(**inputs):
    import numpy as np
    import concourse.bacc as bacc
    from concourse.bass_utils import run_bass_kernel_spmd

    nc = bacc.Bacc("TRN2", target_bir_lowering=False, num_devices=1)
    arrays, args = {}, []
    for name in _INS:
        a = np.ascontiguousarray(inputs[name])
        arrays[name] = a
        args.append(nc.dram_tensor(name, a.shape, mybir.dt.from_np(a.dtype), kind="ExternalInput").ap())
    out = nc.dram_tensor("out", (B, S, D), F32, kind="ExternalOutput")
    build(nc, *args, out.ap())
    result = run_bass_kernel_spmd(nc, [arrays], core_ids=[0])
    return result.results[0]["out"]
```

```python
import math

import concourse.bass as bass
from concourse import mybir
from contextlib import ExitStack

F32 = mybir.dt.float32
F16 = mybir.dt.float16
I32 = mybir.dt.int32
U16 = mybir.dt.uint16
ALU = mybir.AluOpType
ACT = mybir.ActivationFunctionType
AX = mybir.AxisListType

B, S, D = 16, 128, 256
HEADS, HD = 8, 16
PAIRS = HEADS // 2
E, TOPK, I = 12, 3, 640
KC, IC = D // 128, I // 128
EPS = 1e-5
SCALE = 1.0 / (64 ** 0.5 * math.log(20))
WS = 64.0
LEAD = 3
HALF = 128
SLOTS = 2 * HALF
TILES = B * S * TOPK // SLOTS + E - 1
CH = B * TOPK


def build(nc, x, ctx_in, klen, Wr, br, w1, b1, w2, b2, Wp1, bp1, Wp2, bp2, out):
    st = ExitStack()
    with st:
        def sb(name, shape, dt):
            return st.enter_context(nc.sbuf_tensor(name, shape, dt))

        def sem(name):
            return st.enter_context(nc.semaphore(name))

        parts_dram = nc.dram_tensor("qk_parts", (B, 2, 128, 4, D), F16, kind="Internal").ap()
        acc_dram = [nc.dram_tensor(f"acc{p}", (B * S + HALF, D), F32, kind="Internal").ap() for p in range(2)]
        xn2_dram = nc.dram_tensor("xn2", (B * S + 128, 2, D), F16, kind="Internal").ap()

        x_all = sb("x_all", [128, B, D], F32)
        w1s = sb("w1s", [128, E, 2, KC, I], F16)
        w2s = sb("w2s", [128, E, IC, 2, D], F16)
        ident = sb("ident", [128, 128], F32)
        ident16 = sb("ident16", [128, 128], F16)
        upper16 = sb("upper16", [128, 128], F16)
        ones16 = sb("ones16", [128, 128], F16)
        lg = sb("lg", [128, E], F32)
        lg_all = sb("lg_all", [128, B, E], F32)
        top8 = sb("top8", [128, 8], F32)
        top_all = sb("top_all", [128, B, TOPK], F32)
        idx8 = sb("idx8", [128, 8], U16)
        idx_all = sb("idx_all", [128, B, TOPK], F32)
        mask = sb("mask", [128, B, E], F16)
        seen = sb("seen", [128, B + 1, E], F16)
        iota_e = sb("iota_e", [128, E], F32)

        def view(t, dt, first, shape, letters):
            dims = len(t.shape)
            names = " ".join("abcdefg"[:dims - 1])
            flat = t[:].rearrange(f"p {names} -> p ({names})") if dims > 2 else t[:]
            if dt != t.dtype:
                flat = flat.bitcast(dt)
            n = math.prod(shape)
            part = flat[:, first:first + n]
            if len(shape) == 1:
                return part
            letters = list(letters)
            names = " ".join(letters)
            return part.rearrange(f"p ({names}) -> p {names}", **dict(zip(letters[1:], shape[1:])))

        qkop = sb("qkop", [128, 2, 2, 2, PAIRS, D], F16)
        qop, kop = qkop[:, 0], qkop[:, 1]
        prob = sb("prob", [128, 2, PAIRS, KC, D], F32)
        mixed = sb("mixed", [128, 2 * KC * PAIRS * 64 + 2 * D], F32)
        vst = view(mixed, F32, 0, (2, KC, PAIRS, 2, 32), "rcjgd")
        qkf = view(mixed, F32, 2 * KC * PAIRS * 64, (2, D), "xf")
        ones32 = sb("ones32", [128, 2, 32], F32)
        wstage = sb("wstage", [128, 2, KC * I], F32)
        parts = sb("parts", [128, 4, D], F16)
        ctx_k = sb("ctx_k", [128, 2, D], F32)
        ctx_v = sb("ctx_v", [128, 2, D], F32)
        att = sb("att", [128, D], F32)
        xn2 = sb("xn2s", [128, D], F32)
        xn2T = sb("xn2T", [128, KC, 128], F32)
        xn2hl = sb("xn2hl", [128, 2, D], F16)
        negm = sb("negm", [128, 2, PAIRS, 2], F16)
        negmT = sb("negmT", [8, 2, 128], F16)
        wr_s = sb("wr_s", [128, KC, E], F32)
        br_s = sb("br_s", [128, E], F32)
        klen_i = sb("klen_i", [128, B], I32)
        klen_f = sb("klen_f", [128, B], F32)
        lnk = sb("lnk", [128, B], F32)
        bn1 = sb("bn1", [128, 6], F32)
        mv1 = sb("mv1", [128, 2, 2], F32)
        rs1 = sb("rs1", [128, 2], F32)
        bn2 = sb("bn2", [128, 6], F32)
        mv2 = sb("mv2", [128, 2, 2], F32)
        rs2 = sb("rs2", [128, 2], F32)
        vpe = sb("vpe", [128, 2], F32)
        eps_s = sb("eps_s", [128, 1], F32)
        neghalf = sb("neghalf", [128, 1], F32)
        onehot = sb("onehot", [128, B, TOPK, E], F32)

        idx_tab = sb("idx_tab", [128, 2 * TILES], I32)
        exp_tab = sb("exp_tab", [128, TILES + 1], I32)
        hid = sb("hid", [128, IC, SLOTS], F32)
        pred = sb("pred", [128, 3], F32)
        zero_i = sb("zero_i", [128, 2], I32)
        row_of = sb("row_of", [128, 1], F32)
        b1T = sb("b1T", [128, E, IC], F32)
        w_e = sb("w_e", [128, 2, E], F32)
        tile_of = sb("tile_of", [128, CH], F32)
        slot_of = sb("slot_of", [128, CH], F32)
        gidx = [sb(f"gidx{p}", [128, 2], I32) for p in range(2)]
        sidx = [sb(f"sidx{p}", [128, 2], I32) for p in range(2)]

        at_slot = view(prob, F16, 0, (CH, HALF), "ks")
        tile_cmp = view(prob, F32, CH * HALF // 2, (TILES + 1, E), "te")
        at_tile = view(wstage, F16, 0, (CH, 2 * TILES), "kt")
        oh_val = view(wstage, F32, CH * TILES, (B, TOPK, E), "bce")
        lexp = view(parts, F32, 0, (B, E), "be")
        iota_s = view(parts, F16, 2 * 2 * B * E, (HALF,), "s")
        prefix = view(parts, F32, B * E, (B, E), "be")
        small = view(ctx_v, F32, 0, (10, CH), "nk")
        b2w = view(qkop, F32, 0, (E, D), "ed")
        xg = view(prob, F16, 0, (2, 2, 2, D), "rvhf")
        xT = view(prob, F16, 8 * D, (2, 2 * KC, SLOTS), "rks")
        y = view(prob, F32, 4 * D + 2 * KC * SLOTS, (2, 2, D), "rvf")
        hid_hi = view(wstage, F16, 0, (2, IC, SLOTS), "ris")
        hid_lo = view(mixed, F16, 0, (2, IC, SLOTS), "ris")
        sum_w = view(xn2, F32, 0, (128,), "k")
        mean_w = view(xn2, F32, 128, (1,), "k")
        pooledT = view(xn2, F32, 132, (KC, B), "kb")
        z1T = view(xn2, F32, 164, (B,), "b")
        factor = view(xn2, F32, 180, (B,), "b")
        acc_s = [view(t, F32, 0, (B, D), "bd") for t in (prob, qkop)]
        wp1_s = xn2T
        b1s = att[0:E * IC, 0:128]
        zeros = hid[:].rearrange("p i s -> p (i s)")[:, 0:D]
        bank = [st.enter_context(nc.psum_tensor(f"bank{i}", [128, 512], F32)) for i in range(8)]
        sq = bank[0:2]
        sk = bank[2:4]
        av = bank[4:6]
        misc_a, misc_b = bank[6], bank[7]
        negm_ps = misc_a[:, 0:64].bitcast(F16)

        passed = sem("passed")
        pool_const, dve_const = sem("pool_const"), sem("dve_const")
        tables_loaded = sem("tables_loaded")
        x_first, x_rest = sem("x_first"), sem("x_rest")
        klen_float, lnk_ready = sem("klen_float"), sem("lnk_ready")
        ctxk_loaded = [sem("ctxk_even"), sem("ctxk_odd")]
        ctxv_loaded = [sem("ctxv_even"), sem("ctxv_odd")]
        bn1_ready, mv1_ready = sem("bn1_ready"), sem("mv1_ready")
        ve1_ready, rs1_ready = sem("ve1_ready"), sem("rs1_ready")
        qkf_ready, hi_ready, lo_ready = sem("qkf_ready"), sem("hi_ready"), sem("lo_ready")
        parts_stored = sem("parts_stored")
        qk_loaded = [[sem(f"qk_loaded{p}{g}") for g in range(2)] for p in range(2)]
        sq_ready, max_ready = sem("sq_ready"), sem("max_ready")
        negm_turned, negm_copied = sem("negm_turned"), sem("negm_copied")
        negm_loaded = [sem("negm_loaded0"), sem("negm_loaded1")]
        v_turned, v_ready = sem("v_turned"), sem("v_ready")
        sk_ready, prob_ready = sem("sk_ready"), sem("prob_ready")
        av_ready, rden_ready, att_ready = sem("av_ready"), sem("rden_ready"), sem("att_ready")
        x1_ready = sem("x1_ready")
        bn2_ready, mv2_ready = sem("bn2_ready"), sem("mv2_ready")
        ve2_ready, rs2_ready, xn2_ready = sem("ve2_ready"), sem("rs2_ready"), sem("xn2_ready")
        hi2_ready, lo2_ready, xn2_stored = sem("hi2_ready"), sem("lo2_ready"), sem("xn2_stored")
        xn2_turned, xn2T_ready = sem("xn2_turned"), sem("xn2T_ready")
        lg_summed, lg_ready, top_ready = sem("lg_summed"), sem("lg_ready"), sem("top_ready")
        idx_ready, idxf_ready, oh_ready = sem("idx_ready"), sem("idxf_ready"), sem("oh_ready")
        kept_ready = sem("kept_ready")
        mask_ready, seen_ready = sem("mask_ready"), sem("seen_ready")
        w_loaded = [sem("w_loaded0"), sem("w_loaded1")]
        whi_ready, wlo_ready = sem("whi_ready"), sem("wlo_ready")
        zeros_set, zeros_stored, pads_stored = sem("zeros_set"), sem("zeros_stored"), sem("pads_stored")
        counted, b1_loaded, b1_turned, b1T_ready = sem("counted"), sem("b1_loaded"), sem("b1_turned"), sem("b1T_ready")
        iotas_set, b2_loaded, pred_loaded = sem("iotas_set"), sem("b2_loaded"), sem("pred_loaded")
        table_made, tile_marked, table_summed = sem("table_made"), sem("tile_marked"), sem("table_summed")
        exp_made, weight_summed = sem("exp_made"), sem("weight_summed")
        gidx_ready, sidx_ready = sem("gidx_ready"), sem("sidx_ready")
        gathered = [sem("gathered_even"), sem("gathered_odd")]
        xg_turned, xT_ready = sem("xg_turned"), sem("xT_ready")
        h_summed, hid_ready, hid_hi_ready, hid_lo_ready = sem("h_summed"), sem("hid_ready"), sem("hid_hi_ready"), sem("hid_lo_ready")
        y_summed, y_half, y_ready = sem("y_summed"), sem("y_half"), sem("y_ready")
        scattered = [sem("scattered_first"), sem("scattered_second")]
        acc_loaded = [sem(f"acc_loaded{q}") for q in range(4)]
        acc_summed = [sem(f"acc_summed{q}") for q in range(4)]
        pooled, pooledT_ready, z1_summed, z1_ready = sem("pooled"), sem("pooledT_ready"), sem("z1_summed"), sem("z1_ready")
        phi_summed, phi_exp, factor_ready = sem("phi_summed"), sem("phi_exp"), sem("factor_ready")
        scaled, out_stored = sem("scaled"), sem("out_stored")
        block = st.enter_context(nc.Block())

        def wait_some(eng, s, value):
            if not isinstance(value, int) or value > 0:
                eng.wait_ge(s, value)

        def wait_alone(eng, s, value):
            if not isinstance(value, int):
                eng.wait_ge(s, value)
                eng.sem_inc(passed, 1)
            elif value > 0:
                eng.wait_ge(s, value)

        def per_parity(b, par, n):
            return (b - par) * (n // 2) + n

        def batches(eng, iteration):
            for b in range(2):
                iteration(b, b % 2)
            with eng.Fori(1, E // 2 - 1) as two:
                iteration(two * 2, 0)
                iteration(two * 2 + 1, 1)
            for b in range(E - 2, B + LAST):
                iteration(b, b % 2)

        def has(b, lo=0, hi=B):
            return not isinstance(b, int) or lo <= b < hi

        STEPS = ["triangle", "cnt", "full", "tiles", "tri_tiles", "end", "base", "prefix", "oh_val", "pos", "pos_i",
                 "slot_i", "slot", "tile_i", "tile", "at_tile", "at_slot_1", "at_slot_2", "exp_cmp", "exp_sum", "exp_tab",
                 "idx_fill", "idx_tab", "l_sub", "top_sub", "z", "rz", "p3", "p3_sub", "ew_sum", "ew_rsum", "ew",
                 "oh_w", "w_part", "cnt_1", "cnt_r", "w_e", "w_e_ws", "b2w"]

        def made(step):
            return STEPS.index(step) + 1

        def tiles(eng, iteration):
            for t in range(2):
                iteration(t, t % 2)
            with eng.Fori(1, TILES // 2 - 2) as two:
                iteration(two * 2, 0)
                iteration(two * 2 + 1, 1)
            for t in range(TILES // 2 * 2 - 4, TILES + 1):
                iteration(t, t % 2)

        def tile_is(t, lo=0):
            return not isinstance(t, int) or lo <= t < TILES

        LAST = 2

        def weight_parts(e, i, h):
            if i == 0:
                t = w1s[:, bass.ds(e, 1), :, h, :].squeeze(1)
                return t[:, 0], t[:, 1], wstage[:, 0, h * I:h * I + I]
            c = slice(0, IC // 2 + 1) if h == 0 else slice(IC // 2 + 1, IC)
            t = w2s[:, bass.ds(e, 1), c].squeeze(1)
            return t[:, :, 0], t[:, :, 1], wstage[:, 1].rearrange("p (c d) -> p c d", c=IC)[:, c]

        QB = B // 4

        def load_sums(eng, p):
            eng.wait_ge(y_ready, 2 * TILES)
            for s in scattered:
                eng.wait_ge(s, 16 * TILES)
            for q in range(4):
                src = acc_dram[p][q * QB * S:(q + 1) * QB * S].rearrange("(b p) f -> p b f", p=S)
                eng.dma_start(acc_s[p][:, q * QB:(q + 1) * QB, :], src).then_inc(acc_loaded[q], 16)

        def store_out(eng, q):
            eng.wait_ge(scaled, QB * (q + 1))
            eng.dma_start(out[q * QB:(q + 1) * QB].rearrange("b p f -> p b f"),
                          acc_s[0][:, q * QB:(q + 1) * QB, :]).then_inc(out_stored, 16)

        @block.sync
        def _(sp):
            sp.dma_start(x_all[:, 0:2, :], x[0:2].rearrange("b p f -> p b f")).then_inc(x_first, 16)
            sp.dma_start(klen_i[:], klen.partition_broadcast(128)).then_inc(tables_loaded, 16)
            sp.dma_start(ctx_k[:, 0, :], ctx_in[0]).then_inc(ctxk_loaded[0], 16)
            sp.dma_start(ctx_k[:, 1, :], ctx_in[1]).then_inc(ctxk_loaded[1], 16)
            sp.dma_start(x_all[:, 2:B, :], x[2:B].rearrange("b p f -> p b f")).then_inc(x_rest, 16)
            sp.dma_start(ctx_v[:, 0, :], ctx_in[0]).then_inc(ctxv_loaded[0], 16)
            sp.dma_start(wr_s[:], Wr.rearrange("(c p) e -> p c e", p=128)).then_inc(tables_loaded, 16)
            sp.dma_start(br_s[:], br.partition_broadcast(128)).then_inc(tables_loaded, 16)

            def store_parts(b):
                wait_alone(sp, lo_ready, b + 1)
                sp.dma_start(parts_dram[b, 0].rearrange("p (r t) f -> p r (t f)", r=2),
                             parts[:, 0:2].rearrange("p t f -> p (t f)").unsqueeze(1).to_broadcast([128, 2, 2 * D])
                             ).then_inc(parts_stored, 16)
                sp.dma_start(parts_dram[b, 1, :, 0:2, :], parts[:, 2:4, :]).then_inc(parts_stored, 16)
                sp.dma_start(parts_dram[b, 1, :, 2:4, :], parts[:, 3:1:-1, :]).then_inc(parts_stored, 16)

            def load_ctx_k(b, par):
                wait_alone(sp, qkf_ready, 2 * b - 2)
                sp.dma_start(ctx_k[:, par, :], ctx_in[b]).then_inc(ctxk_loaded[par], 16)

            def load_qk(b, par, g):
                wait_alone(sp, parts_stored, 48 * b + 48)
                wait_alone(sp, sk_ready, 8 * (b - 2) + 4 * g + 4)
                for i, dst in ((0, qop), (1, kop)):
                    src = parts_dram[b, i].rearrange("(j g d) t f -> g (d t) j f", g=2, d=HD)[g]
                    sp.dma_start(dst[0:64, par, g], src).then_inc(qk_loaded[par][g], 16)

            def load_negm(b, par, g):
                wait_alone(sp, negm_copied, 2 * b + g + 1)
                sp.dma_start(qop[64:65, par, g].rearrange("o j (c q) -> o (j c) q", c=2),
                             negmT[0:8, g, :]).then_inc(negm_loaded[g], 16)

            def weights(b, i):
                wait_alone(sp, wlo_ready, 4 * (b - 1) + 2 * i + 2)
                src = (w1, w2)[i][bass.ds(b, 1)].rearrange("o (c p) i -> p (o c) i", p=128)
                sp.dma_start(wstage[:, i, :].rearrange("p (c i) -> p c i", c=(KC, IC)[i]), src).then_inc(w_loaded[i], 16)

            def iteration(b, par):
                if has(b):
                    load_negm(b, par, 1)
                if has(b + LEAD):
                    load_ctx_k(b + LEAD, 1 - par)
                if has(b + 1):
                    wait_alone(sp, v_turned, b)
                    sp.dma_start(ctx_v[:, 1 - par, :], ctx_in[b + 1]).then_inc(ctxv_loaded[1 - par], 16)
                if has(b + 2):
                    load_qk(b + 2, par, 0)
                if has(b + 1):
                    load_negm(b + 1, 1 - par, 0)
                if has(b + 1, 1, E):
                    weights(b + 1, 0)
                if has(b - 2):
                    wait_alone(sp, hi2_ready, b - 1)
                    wait_alone(sp, lo2_ready, b - 1)
                    sp.dma_start(xn2_dram[bass.ds((b - 2) * S, S)], xn2hl[:]).then_inc(xn2_stored, 16)
                if has(b + 2):
                    load_qk(b + 2, par, 1)
                if has(b + 1, 1, E):
                    weights(b + 1, 1)
                if has(b + LEAD):
                    store_parts(b + LEAD)
                if isinstance(b, int) and b == E:
                    sp.wait_ge(zeros_set, 2)
                    for a in acc_dram:
                        sp.dma_start(a.rearrange("(p r) f -> p r f", p=128),
                                     zeros.unsqueeze(1).to_broadcast([128, B + 1, D])).then_inc(zeros_stored, 16)
                    sp.dma_start(xn2_dram[B * S:B * S + HALF].rearrange("p h f -> p (h f)"),
                                 zeros.bitcast(F16)).then_inc(pads_stored, 16)
                    sp.dma_start(pred[:, 0:1], bp1.rearrange("(p o) -> p o", o=1)).then_inc(pred_loaded, 16)
                    sp.dma_start(pred[:, 1:2], Wp2).then_inc(pred_loaded, 16)
                    sp.dma_start(pred[:, 2:3], bp2.partition_broadcast(128)).then_inc(pred_loaded, 16)

            store_parts(0)
            for g in range(2):
                load_qk(0, 0, g)
            load_ctx_k(2, 0)
            store_parts(1)
            for g in range(2):
                load_qk(1, 1, g)
            load_negm(0, 0, 0)
            weights(0, 0)
            weights(0, 1)
            store_parts(2)
            batches(sp, iteration)
            sp.wait_ge(x1_ready, B)
            sp.dma_start(b1s, b1.rearrange("e (c i) -> (e c) i", i=128)).then_inc(b1_loaded, 16)
            sp.wait_ge(sk_ready, HEADS * B)
            sp.dma_start(b2w.rearrange("p e d -> p (e d)"),
                         b2.rearrange("e d -> (e d)").partition_broadcast(128)).then_inc(b2_loaded, 16)
            sp.wait_ge(lg_summed, B)
            sp.dma_start(wp1_s[:], Wp1.rearrange("(c p) j -> p c j", p=128)).then_inc(pred_loaded, 16)
            load_sums(sp, 0)
            for q in range(0, 4, 2):
                store_out(sp, q)
            sp.wait_ge(out_stored, 16 * 4)

        @block.gpsimd
        def _(pool):
            g = nc.gpsimd
            g.memset(neghalf[:], -0.5).then_inc(pool_const, 1)
            g.memset(eps_s[:], EPS).then_inc(pool_const, 1)
            for m, start in ((ident, 0.0), (ident16, 0.0), (upper16, 1.0)):
                g.memset(m[:], start).then_inc(pool_const, 1)
            g.memset(ones16[:], 1.0).then_inc(pool_const, 1)
            pool.wait_ge(pool_const, 6)
            g.memset(qop[64:128].bitcast(F32), 0.0).then_inc(pool_const, 1)
            pool.wait_ge(pool_const, 7)
            for m in (ident, ident16):
                g.affine_select(out=m[:], in_=m[:], compare_op=ALU.not_equal, fill=1.0, base=0,
                                pattern=[[-1, 128]], channel_multiplier=1).then_inc(pool_const, 1)
            g.affine_select(out=upper16[:], in_=upper16[:], compare_op=ALU.is_gt, fill=0.0, base=0,
                            pattern=[[1, 128]], channel_multiplier=-1).then_inc(pool_const, 1)
            g.iota(iota_e[:], pattern=[[1, E]], base=0, channel_multiplier=0,
                   allow_small_or_imprecise_dtypes=True).then_inc(pool_const, 1)

            g.iota(row_of[:], pattern=[[0, 1]], base=0, channel_multiplier=1,
                   allow_small_or_imprecise_dtypes=True).then_inc(pool_const, 1)
            g.memset(zeros, 0.0).then_inc(zeros_set, 1)
            g.memset(zero_i[:], 0).then_inc(zeros_set, 1)

            def rstd(mv, rs, b, par, mv_ready, ve_ready, rs_ready, k):
                wait_some(pool, rs_ready, b)
                pool.wait_ge(mv_ready, b + 1)
                g.tensor_tensor(vpe[:, k:k + 1], mv[:, par, 1:2], eps_s[:], ALU.add).then_inc(ve_ready, 1)
                pool.wait_ge(ve_ready, b + 1)
                g.tensor_tensor(rs[:, par:par + 1], vpe[:, k:k + 1], neghalf[:], ALU.pow).then_inc(rs_ready, 1)

            def low(b):
                pool.wait_ge(qkf_ready, 2 * b + 2)
                pool.wait_ge(hi_ready, b + 1)
                wait_some(pool, parts_stored, 48 * b)
                g.tensor_tensor(parts[:, 1:4:2, :], qkf[:], parts[:, 0:3:2, :], ALU.subtract).then_inc(lo_ready, 1)

            def iteration(b, par):
                if has(b - 1):
                    pool.wait_ge(att_ready, b)
                    g.tensor_tensor(x_all[:, bass.ds(b - 1, 1), :].squeeze(1), x_all[:, bass.ds(b - 1, 1), :].squeeze(1), att[:],
                                    ALU.add).then_inc(x1_ready, 1)
                    rstd(mv2, rs2, b - 1, 1 - par, mv2_ready, ve2_ready, rs2_ready, 1)
                    pool.wait_ge(xn2_ready, b)
                    pool.wait_ge(hi2_ready, b)
                    wait_some(pool, xn2_stored, 16 * (b - 1))
                    g.tensor_tensor(xn2hl[:, 1, :], xn2[:], xn2hl[:, 0, :], ALU.subtract).then_inc(lo2_ready, 1)
                if has(b + LEAD):
                    low(b + LEAD)
                if has(b + LEAD + 1):
                    rstd(mv1, rs1, b + LEAD + 1, par, mv1_ready, ve1_ready, rs1_ready, 0)

            rstd(mv1, rs1, 0, 0, mv1_ready, ve1_ready, rs1_ready, 0)
            rstd(mv1, rs1, 1, 1, mv1_ready, ve1_ready, rs1_ready, 0)
            low(0)
            low(1)
            rstd(mv1, rs1, 2, 0, mv1_ready, ve1_ready, rs1_ready, 0)
            low(2)
            rstd(mv1, rs1, 3, 1, mv1_ready, ve1_ready, rs1_ready, 0)
            batches(pool, iteration)

            pool.wait_ge(parts_stored, 48 * B)
            pool.wait_ge(v_turned, B)
            g.iota(iota_s, pattern=[[1, HALF]], base=0, channel_multiplier=0,
                   allow_small_or_imprecise_dtypes=True).then_inc(iotas_set, 1)
            g.iota(small[:, 9, :].rearrange("p (b c) -> p b c", c=TOPK), pattern=[[S, B], [0, TOPK]], base=-B * S,
                   channel_multiplier=1, allow_small_or_imprecise_dtypes=True).then_inc(iotas_set, 1)
            pool.wait_ge(lo2_ready, B)
            pool.wait_ge(xn2_turned, B)
            g.memset(sum_w, 1.0).then_inc(iotas_set, 1)
            g.memset(mean_w, 1.0 / S).then_inc(iotas_set, 1)
            pool.wait_ge(iotas_set, 4)
            pool.wait_ge(table_made, made("at_tile"))
            g.tensor_tensor(at_tile, at_tile, small[:, 9, :].unsqueeze(2).to_broadcast([128, CH, 2 * TILES]),
                            ALU.mult).then_inc(tile_marked, 1)

            def gather(t, par):
                wait_alone(pool, gathered[par], (t - par) * 16)
                g.tensor_tensor(gidx[par][:], idx_tab[:, bass.ds(t * 2, 2)], zero_i[:], ALU.add).then_inc(gidx_ready, 1)
                wait_alone(pool, gidx_ready, t + 1)
                wait_alone(pool, xg_turned, t - 1)
                for h in range(2):
                    g.indirect_dma_start(out=xg[:, par, h].rearrange("p h f -> p (h f)"), out_offset=None,
                                         in_=xn2_dram.rearrange("r h f -> r (h f)"),
                                         in_offset=bass.IndirectOffsetOnAxis(ap=gidx[par][:, h:h + 1], axis=0),
                                         bounds_check=B * S + HALF - 1, oob_is_err=False).then_inc(gathered[par], 16)

            def scatter(t, par):
                for h in range(2):
                    wait_alone(pool, scattered[h], t * 16)
                g.tensor_tensor(sidx[par][:], idx_tab[:, bass.ds(t * 2, 2)], zero_i[:], ALU.add).then_inc(sidx_ready, 1)
                wait_alone(pool, sidx_ready, t + 1)
                for h in range(2):
                    wait_alone(pool, y_ready, 2 * t + h + 1)
                    g.indirect_dma_start(out=acc_dram[h],
                                         out_offset=bass.IndirectOffsetOnAxis(ap=sidx[par][:, h:h + 1], axis=0),
                                         in_=y[:, par, h, :], in_offset=None, bounds_check=B * S + HALF - 1,
                                         oob_is_err=False, compute_op=ALU.add).then_inc(scattered[h], 16)

            pool.wait_ge(table_made, made("idx_tab"))
            pool.wait_ge(xn2_stored, 16 * B)
            pool.wait_ge(pads_stored, 16)
            pool.wait_ge(qkf_ready, 2 * B)
            for t in range(4):
                gather(t, t % 2)
            pool.wait_ge(zeros_stored, 32)

            def tile(t, par):
                if tile_is(t + 4):
                    gather(t + 4, par)
                if tile_is(t):
                    scatter(t, par)
            tiles(pool, tile)

            for q in range(1, 4, 2):
                pool.wait_ge(acc_loaded[q], 32)
                part = slice(q * QB, (q + 1) * QB)
                g.tensor_tensor(acc_s[0][:, part, :], acc_s[0][:, part, :], acc_s[1][:, part, :],
                                ALU.add).then_inc(acc_summed[q], 1)

        @block.scalar
        def _(act):
            a = nc.scalar
            act.wait_ge(klen_float, 1)
            a.activation(lnk[:], klen_f[:], ACT.Ln).then_inc(lnk_ready, 1)

            def high(b):
                act.wait_ge(qkf_ready, 2 * b + 2)
                wait_some(act, parts_stored, 48 * b)
                a.activation(parts[:, 0:3:2, :], qkf[:], ACT.Copy).then_inc(hi_ready, 1)

            def copy_negm(b, g):
                act.wait_ge(negm_turned, 2 * b + g + 1)
                wait_some(act, negm_loaded[g], 16 * b)
                a.activation(negmT[:, g, :], negm_ps[0:8, :], ACT.Copy).then_inc(negm_copied, 1)

            def copy_v(b, par):
                act.wait_ge(v_turned, b + 1)
                wait_some(act, av_ready, 2 * (b - 2) + 2)
                src = misc_a[:, 0:KC * 128].rearrange("p (c j g d) -> p c j g d", c=KC, g=2, d=HD)
                for g in range(2):
                    a.activation(vst[:, par, :, :, g, HD * g:HD * g + HD], src[:, :, :, g, :],
                                 ACT.Copy).then_inc(v_ready, 1)

            def exps(b, par, s):
                g, j = divmod(s, PAIRS)
                act.wait_ge(sk_ready, 8 * b + s + 1)
                if j == 0:
                    wait_some(act, av_ready, 2 * b + g - 1)
                a.activation(prob[:, g, j], sk[s % 2][:].rearrange("p (c q) -> p c q", c=KC),
                             ACT.Exp).then_inc(prob_ready, 1)

            def weight_hi(b, i, h):
                if h == 0:
                    act.wait_ge(w_loaded[i], 16 * b + 16)
                hi, _, src = weight_parts(b, i, h)
                a.activation(hi, src, ACT.Copy, scale=WS).then_inc(whi_ready, 1)

            def iteration(b, par):
                for s in range(HEADS):
                    if has(b):
                        exps(b, par, s)
                    if s == 0 and has(b - 2):
                        act.wait_ge(xn2_turned, b - 1)
                        a.activation(xn2T[:], misc_b[:, 0:256].rearrange("p (c t) -> p c t", c=KC),
                                     ACT.Copy).then_inc(xn2T_ready, 1)
                    if s == 2 and has(b):
                        copy_negm(b, 1)
                    if s == 6 and has(b + 1):
                        copy_negm(b + 1, 0)
                    if s == 7 and has(b + 1):
                        copy_v(b + 1, 1 - par)
                    if s in (1, 3, 4, 5) and has(b, 0, E):
                        k = (1, 3, 4, 5).index(s)
                        weight_hi(b, k // 2, k % 2)
                if has(b - 1):
                    act.wait_ge(xn2_ready, b)
                    wait_some(act, xn2_stored, 16 * (b - 1))
                    a.activation(xn2hl[:, 0, :], xn2[:], ACT.Copy).then_inc(hi2_ready, 1)
                if has(b + LEAD):
                    high(b + LEAD)

            high(0)
            high(1)
            copy_v(0, 0)
            copy_negm(0, 0)
            high(2)
            batches(act, iteration)

            act.wait_ge(b1_turned, 1)
            a.activation(b1T[:].rearrange("p e c -> p (e c)"), misc_b[:, 0:E * IC], ACT.Copy).then_inc(b1T_ready, 1)
            act.wait_ge(table_made, made("l_sub"))
            a.activation(lexp, lexp, ACT.Exp).then_inc(exp_made, 1)
            act.wait_ge(table_made, made("top_sub"))
            a.activation(small[:, 3, :], small[:, 3, :], ACT.Exp).then_inc(exp_made, 1)
            act.wait_ge(table_made, made("p3_sub"))
            a.activation(small[:, 4, :], small[:, 4, :], ACT.Exp).then_inc(exp_made, 1)
            act.wait_ge(b1T_ready, 1)
            act.wait_ge(zeros_stored, 32)
            act.wait_ge(pads_stored, 16)
            act.wait_ge(av_ready, 2 * B)

            def tile(t, par):
                if not tile_is(t):
                    return
                e = act.value_load(exp_tab[0:1, bass.ds(t, 1)], min_val=0, max_val=E - 1)
                for c in range(IC):
                    act.wait_ge(h_summed, IC * t + c + 1)
                    if c in (0, 3):
                        wait_some(act, hid_lo_ready, 2 * (t - 1) + (1 if c == 0 else 2))
                    a.activation(hid[:, c, :], bank[c][:, 0:SLOTS], ACT.Relu, bias=b1T[:, bass.ds(e, 1), c],
                                 scale=1.0 / WS).then_inc(hid_ready, 1)
                    if c in (2, 4):
                        first = 0 if c == 2 else 3
                        wait_alone(act, hid_ready, IC * t + c + 1)
                        if c == 2:
                            wait_some(act, y_summed, 2 * t - 2)
                        a.activation(hid_hi[:, par, first:c + 1, :], hid[:, first:c + 1, :], ACT.Copy).then_inc(hid_hi_ready, 1)
            act.wait_ge(table_made, made("exp_tab"))
            tiles(act, tile)

            load_sums(act, 1)
            act.wait_ge(z1_summed, 1)
            a.activation(z1T, bank[0][:, 64:64 + B], ACT.Relu, bias=pred[:, 0:1]).then_inc(z1_ready, 1)
            act.wait_ge(phi_summed, 1)
            a.activation(factor, bank[0][:, 96:96 + B], ACT.Exp, bias=pred[:, 2:3], scale=-1.0).then_inc(phi_exp, 1)
            for q in range(1, 4, 2):
                store_out(act, q)

        @block.vector
        def _(dve):
            v = nc.vector
            v.memset(ones32[:], 0.0).then_inc(dve_const, 1)
            v.memset(vst[:], 0.0).then_inc(dve_const, 1)
            v.memset(seen[:, 0, :], 0.0).then_inc(dve_const, 1)
            v.memset(kop[64:128].bitcast(F32), 0.0).then_inc(dve_const, 1)
            dve.wait_ge(dve_const, 4)
            v.memset(ones32[:, 0, 0:HD], 1.0).then_inc(dve_const, 1)
            v.memset(ones32[:, 1, HD:2 * HD], 1.0).then_inc(dve_const, 1)
            v.memset(kop[64:65], 1.0).then_inc(dve_const, 1)
            dve.wait_ge(tables_loaded, 48)
            v.tensor_copy(klen_f[:], klen_i[:]).then_inc(klen_float, 1)

            def stats(b, par, bn, mv, bn_ready, mv_ready):
                wait_some(dve, mv_ready, b)
                v.bn_stats(bn[:], x_all[:, bass.ds(b, 1), :].squeeze(1)).then_inc(bn_ready, 1)
                wait_alone(dve, qkf_ready if bn is bn1 else xn2_ready, 2 * b - 3 if bn is bn1 else b - 1)
                wait_alone(dve, bn_ready, b + 1)
                v.bn_aggr(mv[:, par, :], bn[:]).then_inc(mv_ready, 1)

            def operands(b, par):
                dve.wait_ge(rs1_ready, b + 1)
                wait_some(dve, lo_ready, b)
                v.tensor_scalar(qkf[:, 0, :], x_all[:, bass.ds(b, 1), :].squeeze(1), mv1[:, par, 0:1], rs1[:, par:par + 1],
                                ALU.subtract, ALU.mult).then_inc(qkf_ready, 1)
                dve.wait_ge(ctxk_loaded[par], per_parity(b, par, 16))
                v.tensor_scalar(qkf[:, 1, :], ctx_k[:, par, :], lnk[:, bass.ds(b, 1)], SCALE,
                                ALU.mult, ALU.mult).then_inc(qkf_ready, 1)

            def maximum(b, s):
                g, j = divmod(s, PAIRS)
                dve.wait_ge(sq_ready, 8 * b + s + 1)
                if j == 0:
                    wait_some(dve, negm_turned, 2 * (b - 1) + g + 1)
                v.tensor_reduce(negm[:, g, j], sq[s % 2][:].rearrange("p (c k) -> p c k", c=2), AX.X, ALU.max,
                                negate=True).then_inc(max_ready, 1)

            def weight_lo(b, i, h):
                dve.wait_ge(whi_ready, 4 * b + 2 * i + h + 1)
                hi, lo, src = weight_parts(b, i, h)
                v.scalar_tensor_tensor(lo, src, WS, hi, ALU.mult, ALU.subtract).then_inc(wlo_ready, 1)

            def route(b, step):
                bb = bass.ds(b, 1)
                if step == 0:
                    dve.wait_ge(lg_summed, b + 1)
                    wait_some(dve, kept_ready, 2 * b)
                    wait_some(dve, mask_ready, b)
                    v.tensor_tensor(lg[:], misc_b[:, 0:E], br_s[:], ALU.add).then_inc(lg_ready, 1)
                elif step == 1:
                    wait_alone(dve, lg_ready, b + 1)
                    v.max(top8[:], lg[:]).then_inc(top_ready, 1)
                elif step == 2:
                    wait_alone(dve, top_ready, b + 1)
                    v.max_index(idx8[:], top8[:], lg[:]).then_inc(idx_ready, 1)
                    v.tensor_scalar(lg_all[:, bb, :].squeeze(1), lg[:], 0.0, None, ALU.add).then_inc(kept_ready, 1)
                    v.tensor_scalar(top_all[:, bb, :].squeeze(1), top8[:, 0:TOPK], 0.0, None,
                                    ALU.add).then_inc(kept_ready, 1)
                elif step == 3:
                    dve.wait_ge(idx_ready, b + 1)
                    v.tensor_scalar(idx_all[:, bb, :].squeeze(1), idx8[:, 0:TOPK], 0.0, None,
                                    ALU.add).then_inc(idxf_ready, 1)
                elif step == 4:
                    dve.wait_ge(idxf_ready, b + 1)
                    v.tensor_tensor(onehot[:, bb].squeeze(1), iota_e[:].unsqueeze(1).to_broadcast([128, TOPK, E]),
                                    idx_all[:, bb, :].squeeze(1).unsqueeze(2).to_broadcast([128, TOPK, E]),
                                    ALU.is_equal).then_inc(oh_ready, 1)
                elif step == 5:
                    dve.wait_ge(oh_ready, b + 1)
                    with nc.allow_low_precision("zeros and ones are exact in float16"):
                        v.tensor_reduce(mask[:, bb, :].squeeze(1), onehot[:, bb].squeeze(1).rearrange("p c e -> p e c"), AX.X,
                                        ALU.add).then_inc(mask_ready, 1)
                elif step == 6:
                    dve.wait_ge(mask_ready, b + 1)
                    v.tensor_tensor(seen[:, bass.ds(b + 1, 1), :].squeeze(1), seen[:, bb, :].squeeze(1),
                                    mask[:, bb, :].squeeze(1), ALU.add).then_inc(seen_ready, 1)

            def iteration(b, par):
                for s in range(HEADS):
                    if has(b + 1):
                        maximum(b + 1, s)
                    if s >= 3 and has(b - 2):
                        route(b - 2, s - 3)
                    if s == 4 and has(b - 1):
                        dve.wait_ge(av_ready, 2 * b)
                        wait_some(dve, x1_ready, b - 1)
                        v.reciprocal(att[:], av[1 - par][:, D:2 * D]).then_inc(rden_ready, 1)
                        dve.wait_ge(rden_ready, b)
                        v.tensor_tensor(att[:], av[1 - par][:, 0:D], att[:], ALU.mult).then_inc(att_ready, 1)
                    if s == 6 and has(b - 1):
                        dve.wait_ge(x1_ready, b)
                        stats(b - 1, 1 - par, bn2, mv2, bn2_ready, mv2_ready)
                    if s in (1, 2, 4, 5) and has(b, 0, E):
                        k = (1, 2, 4, 5).index(s)
                        weight_lo(b, k // 2, k % 2)
                if has(b + LEAD):
                    operands(b + LEAD, 1 - par)
                if has(b - 2):
                    route(b - 2, 5)
                if has(b - 1):
                    dve.wait_ge(rs2_ready, b)
                    wait_some(dve, lo2_ready, b - 1)
                    wait_some(dve, xn2_turned, b - 1)
                    v.tensor_scalar(xn2[:], x_all[:, bass.ds(b - 1, 1), :].squeeze(1), mv2[:, 1 - par, 0:1],
                                    rs2[:, 1 - par:2 - par], ALU.subtract, ALU.mult).then_inc(xn2_ready, 1)
                if has(b + LEAD + 1):
                    stats(b + LEAD + 1, par, bn1, mv1, bn1_ready, mv1_ready)
                if has(b - 2):
                    route(b - 2, 6)

            dve.wait_ge(x_first, 16)
            stats(0, 0, bn1, mv1, bn1_ready, mv1_ready)
            stats(1, 1, bn1, mv1, bn1_ready, mv1_ready)
            dve.wait_ge(lnk_ready, 1)
            operands(0, 0)
            operands(1, 1)
            dve.wait_ge(x_rest, 16)
            stats(2, 0, bn1, mv1, bn1_ready, mv1_ready)
            stats(3, 1, bn1, mv1, bn1_ready, mv1_ready)
            for s in range(HEADS):
                maximum(0, s)
            operands(2, 0)
            batches(dve, iteration)

            def turned_rows(t, par):
                dve.wait_ge(xg_turned, t + 1)
                wait_some(dve, h_summed, IC * (t - 1))
                v.tensor_copy(xT[:, par].rearrange("p k s -> p (k s)"), bank[5][:].bitcast(F16)).then_inc(xT_ready, 1)

            done = [0]

            def step(name, op):
                assert STEPS[done[0]] == name
                done[0] += 1
                op.then_inc(table_made, 1)

            def after(name):
                dve.wait_ge(table_made, made(name))

            def tt(name, o, i0, i1, op):
                step(name, v.tensor_tensor(o, i0, i1, op))

            small_exp = prefix.rearrange("p b e -> p (b e)")[:, 0:TILES + 1]
            cnt_ps, prefix_ps = misc_a[:, B * E:B * E + E], misc_a[:, 0:B * E].rearrange("p (b e) -> p b e", e=E)
            tri = tile_cmp[:, 0:E, :]
            full = tile_cmp[:, E:2 * E + 4, :].rearrange("p t e -> p (t e)").rearrange("p (e k) -> p e k", k=B)
            num = small[:, :, 0:E]
            cnt, n_tiles, end, base = num[:, 5], num[:, 6], num[:, 7], num[:, 8]
            pos = small[:, 0, :]
            pos_i, cut_i, cut2_i = small[:, 1, :].bitcast(I32), small[:, 2, :].bitcast(I32), small[:, 3, :].bitcast(I32)
            dve.wait_ge(iotas_set, 4)
            dve.wait_ge(wlo_ready, 4 * E)
            dve.wait_ge(av_ready, 2 * B)
            tt("triangle", tri, iota_e[:].unsqueeze(2).to_broadcast([128, E, E]),
               iota_e[:].unsqueeze(1).to_broadcast([128, E, E]), ALU.is_ge)
            dve.wait_ge(counted, 1)
            step("cnt", v.tensor_scalar(cnt, cnt_ps, 1.0 / SLOTS, None, ALU.mult))
            after("cnt")
            tt("full", full, cnt.unsqueeze(2).to_broadcast([128, E, B]),
               iota_s[:, 0:B].unsqueeze(1).to_broadcast([128, E, B]), ALU.is_gt)
            after("full")
            step("tiles", v.tensor_reduce(n_tiles, full, AX.X, ALU.add))
            after("tiles")
            tt("tri_tiles", tri, tri, n_tiles.unsqueeze(1).to_broadcast([128, E, E]), ALU.mult)
            after("tri_tiles")
            step("end", v.tensor_reduce(end, tri, AX.X, ALU.add))
            after("end")
            tt("base", base, end, n_tiles, ALU.subtract)
            after("base")
            step("prefix", v.scalar_tensor_tensor(prefix, base.unsqueeze(1).to_broadcast([128, B, E]), float(SLOTS),
                                                  prefix_ps, ALU.mult, ALU.add))
            after("prefix")
            tt("oh_val", oh_val, onehot[:], prefix.unsqueeze(2).to_broadcast([128, B, TOPK, E]), ALU.mult)
            after("oh_val")
            step("pos", v.tensor_reduce(pos.rearrange("p (b c) -> p b c", c=TOPK), oh_val, AX.X, ALU.add))
            after("pos")
            step("pos_i", v.tensor_scalar(pos_i, pos, 0.0, None, ALU.add))
            after("pos_i")
            step("slot_i", v.tensor_scalar(cut_i, pos_i, HALF - 1, None, ALU.bitwise_and))
            after("slot_i")
            step("slot", v.tensor_scalar(slot_of[:], cut_i, 0.0, None, ALU.add))
            step("tile_i", v.tensor_scalar(cut2_i, pos_i, HALF.bit_length() - 1, None, ALU.arith_shift_right))
            after("tile_i")
            step("tile", v.tensor_scalar(tile_of[:], cut2_i, 0.0, None, ALU.add))
            after("tile")
            tt("at_tile", at_tile, iota_s[:, 0:2 * TILES].unsqueeze(1).to_broadcast([128, CH, 2 * TILES]),
               tile_of[:].unsqueeze(2).to_broadcast([128, CH, 2 * TILES]), ALU.is_equal)
            for h in range(2):
                k = slice(h * CH // 2, (h + 1) * CH // 2)
                tt(f"at_slot_{h + 1}", at_slot[:, k, :], iota_s.unsqueeze(1).to_broadcast([128, CH // 2, HALF]),
                   slot_of[:, k].unsqueeze(2).to_broadcast([128, CH // 2, HALF]), ALU.is_equal)
            tt("exp_cmp", tile_cmp, iota_s[:, 0:TILES + 1].unsqueeze(2).to_broadcast([128, TILES + 1, E]),
               end.unsqueeze(1).to_broadcast([128, TILES + 1, E]), ALU.is_ge)
            after("exp_cmp")
            step("exp_sum", v.tensor_reduce(small_exp, tile_cmp, AX.X, ALU.add))
            after("exp_sum")
            step("exp_tab", v.tensor_scalar(exp_tab[:], small_exp, float(E - 1), None, ALU.min))
            dve.wait_ge(table_summed, 1)
            T = misc_b[:, 64:64 + 2 * TILES]
            fill = tile_cmp.rearrange("p t e -> p (t e)")[:, 0:2 * TILES]
            after("exp_sum")
            step("idx_fill", v.tensor_scalar(fill, T, 0.0, row_of[:], ALU.is_equal, ALU.mult))
            after("idx_fill")
            step("idx_tab", v.scalar_tensor_tensor(idx_tab[:], T, float(B * S), fill, ALU.add, ALU.add))

            def ch(k):
                return small[:, k, :].rearrange("p (b c) -> p b c", c=TOPK)

            s0, s1 = ch(3), ch(4)
            z, rz = small[:, 2, 0:B], small[:, 2, B:2 * B]
            def first(x):
                return x[:, :, 0:1].to_broadcast([128, B, x.shape[2]])
            tt("l_sub", lexp, lg_all[:], top_all[:, :, 0:1].to_broadcast([128, B, E]), ALU.subtract)
            tt("top_sub", s0, top_all[:], top_all[:, :, 0:1].to_broadcast([128, B, TOPK]), ALU.subtract)
            dve.wait_ge(exp_made, 1)
            step("z", v.tensor_reduce(z, lexp, AX.X, ALU.add))
            after("z")
            step("rz", v.reciprocal(rz, z))
            after("rz")
            dve.wait_ge(exp_made, 2)
            tt("p3", s0, s0, rz.unsqueeze(2).to_broadcast([128, B, TOPK]), ALU.mult)
            after("p3")
            tt("p3_sub", s1, s0, s0[:, :, 0:1].to_broadcast([128, B, TOPK]), ALU.subtract)
            dve.wait_ge(exp_made, 3)
            step("ew_sum", v.tensor_reduce(z, s1, AX.X, ALU.add))
            after("ew_sum")
            step("ew_rsum", v.reciprocal(rz, z))
            after("ew_rsum")
            tt("ew", s1, s1, rz.unsqueeze(2).to_broadcast([128, B, TOPK]), ALU.mult)
            after("ew")
            tt("oh_w", oh_val, onehot[:], s1.unsqueeze(3).to_broadcast([128, B, TOPK, E]), ALU.mult)
            after("oh_w")
            step("w_part", v.tensor_reduce(num[:, 7], oh_val.rearrange("p b c e -> p e (b c)"), AX.X, ALU.add))
            step("cnt_1", v.tensor_scalar(num[:, 1], cnt_ps, 1.0, None, ALU.max))
            after("cnt_1")
            step("cnt_r", v.reciprocal(num[:, 8], num[:, 1]))
            after("cnt_r")
            turned_rows(0, 0)
            dve.wait_ge(weight_summed, 1)
            tt("w_e", w_e[:, 0], misc_b[:, 256:256 + E], num[:, 8], ALU.mult)
            after("w_e")
            step("w_e_ws", v.tensor_scalar(w_e[:, 1], w_e[:, 0], 1.0 / WS, None, ALU.mult))
            dve.wait_ge(b2_loaded, 16)
            tt("b2w", b2w, b2w, w_e[:, 0].unsqueeze(2).to_broadcast([128, E, D]), ALU.mult)
            after("b2w")
            dve.wait_ge(pred_loaded, 64)
            v.tensor_scalar(pred[:, 2:3], pred[:, 2:3], -1.0, None, ALU.mult).then_inc(table_made, 1)

            def low_parts(t, par):
                for h, (first_c, last_c) in enumerate(((0, 3), (3, IC))):
                    dve.wait_ge(hid_hi_ready, 2 * t + h + 1)
                    v.tensor_tensor(hid_lo[:, par, first_c:last_c, :], hid[:, first_c:last_c, :],
                                    hid_hi[:, par, first_c:last_c, :], ALU.subtract).then_inc(hid_lo_ready, 1)

            def output(t, par):
                e = dve.value_load(exp_tab[0:1, bass.ds(t, 1)], min_val=0, max_val=E - 1)
                w = w_e[:, 1, bass.ds(e, 1)]
                for h in range(2):
                    wait_alone(dve, y_summed, 2 * t + h + 1)
                    wait_alone(dve, scattered[h], (t - 1) * 16)
                    v.scalar_tensor_tensor(y[:, par, h, :], bank[6 + h][:, 0:D], w, b2w[:, bass.ds(e, 1), :].squeeze(1),
                                           ALU.mult, ALU.add).then_inc(y_half, 1)
                for h in range(2):
                    wait_alone(dve, y_half, 2 * t + h + 1)
                    v.scalar_tensor_tensor(y[:, par, h, :], bank[6 + h][:, D:2 * D], w, y[:, par, h, :],
                                           ALU.mult, ALU.add).then_inc(y_ready, 1)

            def tile(t, par):
                if tile_is(t):
                    low_parts(t, par)
                if tile_is(t - 1):
                    output(t - 1, 1 - par)
                if tile_is(t + 2):
                    turned_rows(t + 2, par)
            turned_rows(1, 1)
            tiles(dve, tile)

            for q in range(0, 4, 2):
                dve.wait_ge(acc_loaded[q], 32)
                part = slice(q * QB, (q + 1) * QB)
                v.tensor_tensor(acc_s[0][:, part, :], acc_s[0][:, part, :], acc_s[1][:, part, :],
                                ALU.add).then_inc(acc_summed[q], 1)
            dve.wait_ge(pooled, 1)
            v.tensor_copy(pooledT.rearrange("p k b -> p (k b)"), bank[0][:, 0:KC * B]).then_inc(pooledT_ready, 1)
            dve.wait_ge(phi_exp, 1)
            v.tensor_scalar(factor, factor, 1.0, None, ALU.add).then_inc(factor_ready, 1)
            dve.wait_ge(factor_ready, 1)
            v.reciprocal(factor, factor).then_inc(factor_ready, 1)
            dve.wait_ge(factor_ready, 2)
            v.tensor_scalar(factor, factor, 0.7, -0.8, ALU.is_gt, ALU.mult).then_inc(factor_ready, 1)
            dve.wait_ge(factor_ready, 3)
            v.tensor_scalar(factor, factor, 1.0, None, ALU.add).then_inc(factor_ready, 1)
            dve.wait_ge(factor_ready, 4)
            dve.wait_ge(acc_summed[1], 1)
            dve.wait_ge(acc_summed[3], 1)
            for b in range(B):
                v.scalar_tensor_tensor(acc_s[0][:, b, :], acc_s[0][:, b, :], factor[:, b:b + 1], x_all[:, b, :],
                                       ALU.mult, ALU.add).then_inc(scaled, 1)

        @block.tensor
        def _(pe):
            t = nc.tensor

            def scores_q(b, par, s):
                g, j = divmod(s, PAIRS)
                if j == 0:
                    pe.wait_ge(qk_loaded[par][g], per_parity(b, par, 32))
                wait_some(pe, max_ready, 8 * b + s - 1)
                for c in range(2):
                    mm = t.matmul(sq[s % 2][:, c * D:(c + 1) * D], qop[0:64, par, g, j, c * 128:(c + 1) * 128],
                                  kop[0:64, par, g, j, :], start=True, stop=True)
                mm.then_inc(sq_ready, 1)

            def scores_k(b, par, s):
                g, j = divmod(s, PAIRS)
                if j == 0:
                    pe.wait_ge(negm_loaded[g], 16 * b + 16)
                wait_some(pe, prob_ready, 8 * b + s - 1)
                for c in range(KC):
                    mm = t.matmul(sk[s % 2][:, c * D:(c + 1) * D], kop[:, par, g, j, c * 128:(c + 1) * 128],
                                  qop[:, par, g, j, :], start=True, stop=True)
                mm.then_inc(sk_ready, 1)

            def sums(b, par, g, quarter):
                c, what = divmod(quarter, 2)
                if quarter == 0:
                    pe.wait_ge(prob_ready, 8 * b + 4 * g + 4)
                    if g == 0:
                        pe.wait_ge(v_ready, 2 * b + 2)
                        wait_some(pe, att_ready, b - 1)
                for j in range(PAIRS):
                    lhs = vst[:, par, c, j, g, :] if what == 0 else ones32[:, g, :]
                    mm = t.matmul(av[par][32 * j:32 * j + 32, what * D:(what + 1) * D], lhs, prob[:, g, j, c, :],
                                  start=(g == 0 and quarter == 0), stop=(g == 1 and c == 1),
                                  skip_group_check=True)
                if quarter == 3:
                    mm.then_inc(av_ready, 1)

            def turn_negm(b, g):
                pe.wait_ge(max_ready, 8 * b + 4 * g + 4)
                if g == 1 or (isinstance(b, int) and b == 0):
                    pe.wait_ge(v_ready, 2 * b + 2)
                else:
                    pe.wait_ge(negm_copied, 2 * b)
                t.transpose(negm_ps[0:8, :], negm[:, g].rearrange("p j c -> p (j c)"),
                            ident16[:]).then_inc(negm_turned, 1)

            def turn_v(b, par):
                pe.wait_ge(ctxv_loaded[par], per_parity(b, par, 16))
                if not (isinstance(b, int) and b == 0):
                    pe.wait_ge(negm_copied, 2 * b + 1)
                for c in range(KC):
                    mm = t.transpose(misc_a[:, c * 128:(c + 1) * 128], ctx_v[:, par, c * 128:(c + 1) * 128], ident[:])
                mm.then_inc(v_turned, 1)

            def turn_xn2(b):
                pe.wait_ge(xn2_ready, b + 1)
                wait_some(pe, lg_ready, b)
                for c in range(KC):
                    mm = t.transpose(misc_b[:, c * 128:(c + 1) * 128], xn2[:, c * 128:(c + 1) * 128], ident[:])
                mm.then_inc(xn2_turned, 1)

            def router(b):
                pe.wait_ge(xn2T_ready, b + 1)
                for c in range(KC):
                    mm = t.matmul(misc_b[:, 0:E], xn2T[:, c, :], wr_s[:, c, :], start=(c == 0), stop=(c == KC - 1))
                mm.then_inc(lg_summed, 1)

            def iteration(b, par):
                for s in range(HEADS):
                    if has(b + 1):
                        scores_q(b + 1, 1 - par, s)
                    if has(b):
                        scores_k(b, par, s)
                    if s < 4 and has(b - 1):
                        sums(b - 1, 1 - par, 1, s)
                    if s >= 4 and has(b):
                        sums(b, par, 0, s - 4)
                    if s == 1 and has(b):
                        turn_negm(b, 1)
                    if s == 2 and has(b - 2):
                        router(b - 2)
                    if s == 5 and has(b + 1):
                        turn_negm(b + 1, 0)
                    if s == 6 and has(b + 1):
                        turn_v(b + 1, 1 - par)
                    if s == 7 and has(b - 1):
                        turn_xn2(b - 1)

            pe.wait_ge(pool_const, 11)
            pe.wait_ge(dve_const, 7)
            turn_v(0, 0)
            for s in range(HEADS):
                scores_q(0, 0, s)
            turn_negm(0, 0)
            batches(pe, iteration)

            pe.wait_ge(seen_ready, B)
            pe.wait_ge(negm_copied, 2 * B)
            pe.wait_ge(v_ready, 2 * B)
            pe.wait_ge(lg_ready, B)
            flat = "p b e -> p (b e)"
            t.matmul(misc_a[:, 0:B * E], upper16[:], mask[:].rearrange(flat), start=True, stop=False)
            t.matmul(misc_a[:, 0:B * E], ones16[:], seen[:, 0:B].rearrange(flat), start=False, stop=True)
            t.matmul(misc_a[:, B * E:B * E + E], ones16[:], seen[:, B, :], start=True, stop=True).then_inc(counted, 1)
            pe.wait_ge(b1_loaded, 16)
            t.transpose(misc_b[:, 0:E * IC], b1s, ident[0:E * IC, 0:E * IC]).then_inc(b1_turned, 1)
            pe.wait_ge(tile_marked, 1)
            pe.wait_ge(b1T_ready, 1)
            for k in range(CH):
                if k % (CH // 2) == 0:
                    pe.wait_ge(table_made, made("at_slot_1") + k // (CH // 2))
                mm = t.matmul(misc_b[:, 64:64 + 2 * TILES], at_slot[:, k, :], at_tile[:, k, :], start=(k == 0),
                              stop=(k == CH - 1))
            mm.then_inc(table_summed, 1)

            def turn_rows(n, par):
                pe.wait_ge(gathered[par], (n - par) * 16 + 32)
                if isinstance(n, int) and n < 2:
                    wait_some(pe, xT_ready, n)
                for k in range(2 * KC):
                    for h in range(2):
                        at = k * SLOTS + h * HALF
                        mm = t.transpose(bank[5][:].bitcast(F16)[:, at:at + HALF],
                                         xg[:, par, h, k // KC, (k % KC) * 128:(k % KC) * 128 + 128], ident16[:])
                mm.then_inc(xg_turned, 1)

            def hidden(n, par):
                e = pe.value_load(exp_tab[0:1, bass.ds(n, 1)], min_val=0, max_val=E - 1)
                if isinstance(n, int) and n == 0:
                    pe.wait_ge(xT_ready, 1)
                wait_some(pe, hid_ready, IC * n)
                for c in range(IC):
                    dst = bank[c][:, 0:SLOTS]
                    terms = [(wp, xp, k) for k in range(KC) for wp, xp in ((0, 0), (0, 1), (1, 0))]
                    for i, (wp, xp, k) in enumerate(terms):
                        mm = t.matmul(dst, w1s[:, bass.ds(e, 1), wp, k, c * 128:(c + 1) * 128].squeeze(1),
                                      xT[:, par, xp * KC + k, :], start=(i == 0), stop=(i == len(terms) - 1))
                    mm.then_inc(h_summed, 1)
                return e

            def outputs(n, par, e=None):
                if e is None:
                    e = pe.value_load(exp_tab[0:1, bass.ds(n, 1)], min_val=0, max_val=E - 1)
                pe.wait_ge(hid_lo_ready, 2 * n + 2)
                wait_some(pe, y_ready, 2 * n)
                for c in range(IC):
                    w = w2s[:, bass.ds(e, 1), c].squeeze(1)
                    for h in range(2):
                        rows = slice(h * HALF, (h + 1) * HALF)
                        t.matmul(bank[6 + h][:], hid_hi[:, par, c, rows], w.rearrange("p h d -> p (h d)"),
                                 start=(c == 0), stop=False, skip_group_check=True)
                        mm = t.matmul(bank[6 + h][:, D:2 * D], hid_lo[:, par, c, rows], w[:, 0, :], start=False,
                                      stop=(c == IC - 1), skip_group_check=True)
                        if c == IC - 1:
                            mm.then_inc(y_summed, 1)

            turn_rows(0, 0)
            pe.wait_ge(table_made, made("w_part"))
            t.matmul(misc_b[:, 256:256 + E], sum_w, small[:, 7, 0:E], start=True, stop=True).then_inc(weight_summed, 1)
            turn_rows(1, 1)
            hidden(0, 0)
            pe.wait_ge(table_made, made("w_e"))

            expert = [None]

            def tile(n, par):
                mine = expert[0] if par else None
                if tile_is(n + 1):
                    pe.wait_ge(xT_ready, n + 2)
                if tile_is(n + 2):
                    turn_rows(n + 2, par)
                if tile_is(n + 1):
                    expert[0] = hidden(n + 1, 1 - par)
                if tile_is(n):
                    outputs(n, par, mine)
            tiles(pe, tile)

            for b in range(B):
                if b % QB == 0:
                    pe.wait_ge(acc_summed[b // QB], 1)
                for k in range(KC):
                    mm = t.matmul(bank[0][:, k * B + b:k * B + b + 1], acc_s[0][:, b, k * 128:(k + 1) * 128], mean_w,
                                  start=True, stop=True)
            mm.then_inc(pooled, 1)
            pe.wait_ge(pooledT_ready, 1)
            for k in range(KC):
                mm = t.matmul(bank[0][:, 64:64 + B], wp1_s[:, k, :], pooledT[:, k, :], start=(k == 0), stop=(k == KC - 1))
            mm.then_inc(z1_summed, 1)
            pe.wait_ge(z1_ready, 1)
            t.matmul(bank[0][:, 96:96 + B], pred[:, 1:2].to_broadcast([128, 128]), z1T, start=True,
                     stop=True).then_inc(phi_summed, 1)


_INS = ["x", "ctx_2048", "itok_B_779_1933", "L0_ffn_Wr", "L0_ffn_br", "L0_ffn_w1", "L0_ffn_b1", "L0_ffn_w2",
        "L0_ffn_b2", "L0_ffn_Wp1", "L0_ffn_bp1", "L0_ffn_Wp2", "L0_ffn_bp2"]


def kernel(**inputs):
    import numpy as np
    import concourse.bacc as bacc
    from concourse.bass_utils import run_bass_kernel_spmd

    nc = bacc.Bacc("TRN2", target_bir_lowering=False, num_devices=1)
    arrays, args = {}, []
    for name in _INS:
        a = np.ascontiguousarray(inputs[name])
        arrays[name] = a
        args.append(nc.dram_tensor(name, a.shape, mybir.dt.from_np(a.dtype), kind="ExternalInput").ap())
    out = nc.dram_tensor("out", (B, S, D), F32, kind="ExternalOutput")
    build(nc, *args, out.ap())
    result = run_bass_kernel_spmd(nc, [arrays], core_ids=[0])
    return result.results[0]["out"]
```

```python
import math

import concourse.bass as bass
from concourse import mybir
from contextlib import ExitStack

F32 = mybir.dt.float32
F16 = mybir.dt.float16
I32 = mybir.dt.int32
U16 = mybir.dt.uint16
ALU = mybir.AluOpType
ACT = mybir.ActivationFunctionType
AX = mybir.AxisListType

B, S, D = 16, 128, 256
HEADS, HD = 8, 16
PAIRS = HEADS // 2
E, TOPK, I = 12, 3, 640
KC, IC = D // 128, I // 128
EPS = 1e-5
SCALE = 1.0 / (64 ** 0.5 * math.log(20))
WS = 64.0
LEAD = 3
HALF = 128
SLOTS = 2 * HALF
TILES = B * S * TOPK // SLOTS + E - 1
CH = B * TOPK


def build(nc, x, ctx_in, klen, Wr, br, w1, b1, w2, b2, Wp1, bp1, Wp2, bp2, out):
    st = ExitStack()
    with st:
        def sb(name, shape, dt):
            return st.enter_context(nc.sbuf_tensor(name, shape, dt))

        def sem(name):
            return st.enter_context(nc.semaphore(name))

        parts_dram = nc.dram_tensor("qk_parts", (B, 2, 128, 4, D), F16, kind="Internal").ap()
        acc_dram = [nc.dram_tensor(f"acc{p}", (B * S + HALF, D), F32, kind="Internal").ap() for p in range(2)]
        xn2_dram = nc.dram_tensor("xn2", (B * S + 128, 2, D), F16, kind="Internal").ap()

        x_all = sb("x_all", [128, B, D], F32)
        w1s = sb("w1s", [128, E, 2, KC, I], F16)
        w2s = sb("w2s", [128, E, IC, 2, D], F16)
        ident = sb("ident", [128, 128], F32)
        ident16 = sb("ident16", [128, 128], F16)
        upper16 = sb("upper16", [128, 128], F16)
        ones16 = sb("ones16", [128, 128], F16)
        lg = sb("lg", [128, E], F32)
        lg_all = sb("lg_all", [128, B, E], F32)
        top8 = sb("top8", [128, 8], F32)
        top_all = sb("top_all", [128, B, TOPK], F32)
        idx8 = sb("idx8", [128, 8], U16)
        idx_all = sb("idx_all", [128, B, TOPK], F32)
        mask = sb("mask", [128, B, E], F16)
        seen = sb("seen", [128, B + 1, E], F16)
        iota_e = sb("iota_e", [128, E], F32)

        def view(t, dt, first, shape, letters):
            dims = len(t.shape)
            names = " ".join("abcdefg"[:dims - 1])
            flat = t[:].rearrange(f"p {names} -> p ({names})") if dims > 2 else t[:]
            if dt != t.dtype:
                flat = flat.bitcast(dt)
            n = math.prod(shape)
            part = flat[:, first:first + n]
            if len(shape) == 1:
                return part
            letters = list(letters)
            names = " ".join(letters)
            return part.rearrange(f"p ({names}) -> p {names}", **dict(zip(letters[1:], shape[1:])))

        qkop = sb("qkop", [128, 2, 2, 2, PAIRS, D], F16)
        qop, kop = qkop[:, 0], qkop[:, 1]
        prob = sb("prob", [128, 2, PAIRS, KC, D], F32)
        mixed = sb("mixed", [128, 2 * KC * PAIRS * 64 + 2 * D], F32)
        vst = view(mixed, F32, 0, (2, KC, PAIRS, 2, 32), "rcjgd")
        qkf = view(mixed, F32, 2 * KC * PAIRS * 64, (2, D), "xf")
        ones32 = sb("ones32", [128, 2, 32], F32)
        wstage = sb("wstage", [128, 2, KC * I], F32)
        parts = sb("parts", [128, 4, D], F16)
        ctx_k = sb("ctx_k", [128, 2, D], F32)
        ctx_v = sb("ctx_v", [128, 2, D], F32)
        att = sb("att", [128, D], F32)
        xn2 = sb("xn2s", [128, D], F32)
        xn2T = sb("xn2T", [128, KC, 128], F32)
        xn2hl = sb("xn2hl", [128, 2, D], F16)
        negm = sb("negm", [128, 2, PAIRS, 2], F16)
        negmT = sb("negmT", [8, 2, 128], F16)
        wr_s = sb("wr_s", [128, KC, E], F32)
        br_s = sb("br_s", [128, E], F32)
        klen_i = sb("klen_i", [128, B], I32)
        klen_f = sb("klen_f", [128, B], F32)
        lnk = sb("lnk", [128, B], F32)
        bn1 = sb("bn1", [128, 6], F32)
        mv1 = sb("mv1", [128, 2, 2], F32)
        rs1 = sb("rs1", [128, 2], F32)
        bn2 = sb("bn2", [128, 6], F32)
        mv2 = sb("mv2", [128, 2, 2], F32)
        rs2 = sb("rs2", [128, 2], F32)
        vpe = sb("vpe", [128, 2], F32)
        eps_s = sb("eps_s", [128, 1], F32)
        neghalf = sb("neghalf", [128, 1], F32)
        onehot = sb("onehot", [128, B, TOPK, E], F32)

        idx_tab = sb("idx_tab", [128, 2 * TILES], I32)
        exp_tab = sb("exp_tab", [128, TILES + 1], I32)
        hid = sb("hid", [128, IC, SLOTS], F32)
        pred = sb("pred", [128, 3], F32)
        zero_i = sb("zero_i", [128, 2], I32)
        row_of = sb("row_of", [128, 1], F32)
        b1T = sb("b1T", [128, E, IC], F32)
        w_e = sb("w_e", [128, 2, E], F32)
        tile_of = sb("tile_of", [128, CH], F32)
        slot_of = sb("slot_of", [128, CH], F32)
        gidx = [sb(f"gidx{p}", [128, 2], I32) for p in range(2)]
        sidx = [sb(f"sidx{p}", [128, 2], I32) for p in range(2)]

        at_slot = view(prob, F16, 0, (CH, HALF), "ks")
        tile_cmp = view(prob, F32, CH * HALF // 2, (TILES + 1, E), "te")
        at_tile = view(wstage, F16, 0, (CH, 2 * TILES), "kt")
        oh_val = view(wstage, F32, CH * TILES, (B, TOPK, E), "bce")
        lexp = view(parts, F32, 0, (B, E), "be")
        iota_s = view(parts, F16, 2 * 2 * B * E, (HALF,), "s")
        prefix = view(parts, F32, B * E, (B, E), "be")
        small = view(ctx_v, F32, 0, (10, CH), "nk")
        b2w = view(qkop, F32, 0, (E, D), "ed")
        xg = view(prob, F16, 0, (2, 2, 2, D), "rvhf")
        xT = view(prob, F16, 8 * D, (2, 2 * KC, SLOTS), "rks")
        y = view(prob, F32, 4 * D + 2 * KC * SLOTS, (2, 2, D), "rvf")
        hid_hi = view(wstage, F16, 0, (2, IC, SLOTS), "ris")
        hid_lo = view(mixed, F16, 0, (2, IC, SLOTS), "ris")
        sum_w = view(xn2, F32, 0, (128,), "k")
        mean_w = view(xn2, F32, 128, (2 * B - 1,), "k")
        pooledT = view(xn2, F32, 160, (KC, B), "kb")
        z1T = view(xn2, F32, 192, (B,), "b")
        factor = view(xn2, F32, 208, (B,), "b")
        pooled_s = view(xn2T, F32, 0, (D,), "f")
        acc_s = [view(t, F32, 0, (B, D), "bd") for t in (prob, qkop)]
        wp1_s = view(parts, F32, 0, (KC, 128), "kj")
        b1s = att[0:E * IC, 0:128]
        zeros = hid[:].rearrange("p i s -> p (i s)")[:, 0:D]
        bank = [st.enter_context(nc.psum_tensor(f"bank{i}", [128, 512], F32)) for i in range(8)]
        sq = bank[0:2]
        sk = bank[2:4]
        av = bank[4:6]
        misc_a, misc_b = bank[6], bank[7]
        negm_ps = misc_a[:, 0:64].bitcast(F16)

        passed = sem("passed")
        pool_const, dve_const = sem("pool_const"), sem("dve_const")
        klen_loaded, tables_loaded = sem("klen_loaded"), sem("tables_loaded")
        exp_warm = sem("exp_warm")
        x_first, x_rest = sem("x_first"), sem("x_rest")
        klen_float, lnk_ready = sem("klen_float"), sem("lnk_ready")
        ctxk_loaded = [sem("ctxk_even"), sem("ctxk_odd")]
        ctxv_loaded = [sem("ctxv_even"), sem("ctxv_odd")]
        bn1_ready, mv1_ready = sem("bn1_ready"), sem("mv1_ready")
        ve1_ready, rs1_ready = sem("ve1_ready"), sem("rs1_ready")
        qkf_ready, hi_ready, lo_ready = sem("qkf_ready"), sem("hi_ready"), sem("lo_ready")
        parts_stored = sem("parts_stored")
        qk_loaded = [[sem(f"qk_loaded{p}{g}") for g in range(2)] for p in range(2)]
        sq_ready, max_ready = sem("sq_ready"), sem("max_ready")
        negm_turned, negm_copied = sem("negm_turned"), sem("negm_copied")
        negm_loaded = [sem("negm_loaded0"), sem("negm_loaded1")]
        v_turned, v_ready = sem("v_turned"), sem("v_ready")
        sk_ready, prob_ready = sem("sk_ready"), sem("prob_ready")
        av_ready, rden_ready, att_ready = sem("av_ready"), sem("rden_ready"), sem("att_ready")
        x1_ready = sem("x1_ready")
        bn2_ready, mv2_ready = sem("bn2_ready"), sem("mv2_ready")
        ve2_ready, rs2_ready, xn2_ready = sem("ve2_ready"), sem("rs2_ready"), sem("xn2_ready")
        hi2_ready, lo2_ready, xn2_stored = sem("hi2_ready"), sem("lo2_ready"), sem("xn2_stored")
        xn2_turned, xn2T_ready = sem("xn2_turned"), sem("xn2T_ready")
        lg_summed, lg_ready, top_ready = sem("lg_summed"), sem("lg_ready"), sem("top_ready")
        idx_ready, idxf_ready, oh_ready = sem("idx_ready"), sem("idxf_ready"), sem("oh_ready")
        kept_ready = sem("kept_ready")
        mask_ready, seen_ready = sem("mask_ready"), sem("seen_ready")
        w_loaded = [sem("w_loaded0"), sem("w_loaded1")]
        wscaled, whi_ready = sem("wscaled"), sem("whi_ready")
        wlo_ready = [sem("w1lo_ready"), sem("w2lo_ready")]
        zeros_set, zeros_stored, pads_stored = sem("zeros_set"), sem("zeros_stored"), sem("pads_stored")
        counted, b1_loaded, b1_turned, b1T_ready = sem("counted"), sem("b1_loaded"), sem("b1_turned"), sem("b1T_ready")
        iotas_set, b2_loaded, pred_loaded = sem("iotas_set"), sem("b2_loaded"), sem("pred_loaded")
        table_made, tile_marked, table_summed = sem("table_made"), sem("tile_marked"), sem("table_summed")
        exp_made, weight_summed = sem("exp_made"), sem("weight_summed")
        gidx_ready, sidx_ready = sem("gidx_ready"), sem("sidx_ready")
        gathered = [sem("gathered_even"), sem("gathered_odd")]
        xg_turned, xT_ready = sem("xg_turned"), sem("xT_ready")
        h_summed, hid_ready, hid_hi_ready, hid_lo_ready = sem("h_summed"), sem("hid_ready"), sem("hid_hi_ready"), sem("hid_lo_ready")
        y_summed, y_half, y_ready = sem("y_summed"), sem("y_half"), sem("y_ready")
        scattered = [sem("scattered_first"), sem("scattered_second")]
        acc_loaded = [sem(f"acc_loaded{q}") for q in range(4)]
        acc_summed = [sem(f"acc_summed{q}") for q in range(4)]
        pooled, pooledT_ready, z1_summed, z1_ready = sem("pooled"), sem("pooledT_ready"), sem("z1_summed"), sem("z1_ready")
        phi_summed, phi_exp, factor_ready = sem("phi_summed"), sem("phi_exp"), sem("factor_ready")
        pooled_copied, pooled_turned = sem("pooled_copied"), sem("pooled_turned")
        acc_scaled, scaled_late = sem("acc_scaled"), sem("scaled_late")
        scaled, out_stored = sem("scaled"), sem("out_stored")
        block = st.enter_context(nc.Block())

        def wait_some(eng, s, value):
            if not isinstance(value, int) or value > 0:
                eng.wait_ge(s, value)

        def wait_alone(eng, s, value):
            if not isinstance(value, int):
                eng.wait_ge(s, value)
                eng.sem_inc(passed, 1)
            elif value > 0:
                eng.wait_ge(s, value)

        def per_parity(b, par, n):
            return (b - par) * (n // 2) + n

        def batches(eng, iteration):
            for b in range(2):
                iteration(b, b % 2)
            with eng.Fori(1, E // 2 - 1) as two:
                iteration(two * 2, 0)
                iteration(two * 2 + 1, 1)
            for b in range(E - 2, B + LAST):
                iteration(b, b % 2)

        def has(b, lo=0, hi=B):
            return not isinstance(b, int) or lo <= b < hi

        STEPS = ["triangle", "cnt", "full", "tiles", "tri_tiles", "end", "base", "prefix", "oh_val", "pos", "pos_i",
                 "slot_i", "slot", "tile_i", "tile", "at_tile_1", "at_tile_2", "at_slot_1", "at_slot_2", "exp_cmp", "exp_sum", "exp_tab",
                 "idx_fill", "idx_tab", "l_sub", "top_sub", "z", "rz", "p3", "p3_sub", "ew_sum", "ew_rsum", "ew",
                 "oh_w", "w_part", "cnt_1", "cnt_r", "w_e", "w_e_ws", "b2w"]

        def made(step):
            return STEPS.index(step) + 1

        def tiles(eng, iteration):
            for t in range(2):
                iteration(t, t % 2)
            with eng.Fori(1, TILES // 2 - 2) as two:
                iteration(two * 2, 0)
                iteration(two * 2 + 1, 1)
            for t in range(TILES // 2 * 2 - 4, TILES + 1):
                iteration(t, t % 2)

        def tile_is(t, lo=0):
            return not isinstance(t, int) or lo <= t < TILES

        LAST = 2

        ROUTE_AT = [(), (), (), (), (0,), (1,), (2,), (3, 4, 5, 6)]
        BY_POOL = (0,)

        def weight_parts(e, i, h):
            if i == 0:
                t = w1s[:, bass.ds(e, 1), :, h, :].squeeze(1)
                return t[:, 0], t[:, 1], wstage[:, 0, h * I:h * I + I]
            c = slice(0, IC // 2 + 1) if h == 0 else slice(IC // 2 + 1, IC)
            t = w2s[:, bass.ds(e, 1), c].squeeze(1)
            return t[:, :, 0], t[:, :, 1], wstage[:, 1].rearrange("p (c d) -> p c d", c=IC)[:, c]

        BY_ACT = 6
        QB = B // 4

        def load_sums(eng, p):
            eng.wait_ge(y_ready, 2 * TILES)
            for s in scattered:
                eng.wait_ge(s, 16 * TILES)
            for q in range(4):
                src = acc_dram[p][q * QB * S:(q + 1) * QB * S].rearrange("(b p) f -> p b f", p=S)
                eng.dma_start(acc_s[p][:, q * QB:(q + 1) * QB, :], src).then_inc(acc_loaded[q], 16)

        def store_out(eng, q):
            eng.wait_ge(scaled, min(QB * (q + 1), B - BY_ACT))
            wait_some(eng, scaled_late, max(QB * (q + 1) - (B - BY_ACT), 0))
            eng.dma_start(out[q * QB:(q + 1) * QB].rearrange("b p f -> p b f"),
                          acc_s[0][:, q * QB:(q + 1) * QB, :]).then_inc(out_stored, 16)

        @block.sync
        def _(sp):
            sp.dma_start(x_all[:, 0:2, :], x[0:2].rearrange("b p f -> p b f")).then_inc(x_first, 16)
            sp.dma_start(klen_i[:], klen.partition_broadcast(128)).then_inc(klen_loaded, 16)
            sp.dma_start(ctx_k[:, 0, :], ctx_in[0]).then_inc(ctxk_loaded[0], 16)
            sp.dma_start(ctx_k[:, 1, :], ctx_in[1]).then_inc(ctxk_loaded[1], 16)
            sp.dma_start(ctx_v[:, 0, :], ctx_in[0]).then_inc(ctxv_loaded[0], 16)
            sp.dma_start(ctx_v[:, 1, :], ctx_in[1]).then_inc(ctxv_loaded[1], 16)
            sp.dma_start(wr_s[:], Wr.rearrange("(c p) e -> p c e", p=128)).then_inc(tables_loaded, 16)
            sp.dma_start(br_s[:], br.partition_broadcast(128)).then_inc(tables_loaded, 16)
            sp.dma_start(x_all[:, 2:B, :], x[2:B].rearrange("b p f -> p b f")).then_inc(x_rest, 16)

            def store_parts(b, maxima_of=None):
                wait_alone(sp, lo_ready, b + 1)
                sp.dma_start(parts_dram[b, 0].rearrange("p (r t) f -> p r (t f)", r=2),
                             parts[:, 0:2].rearrange("p t f -> p (t f)").unsqueeze(1).to_broadcast([128, 2, 2 * D])
                             ).then_inc(parts_stored, 16)
                sp.dma_start(parts_dram[b, 1, :, 0:2, :], parts[:, 2:4, :]).then_inc(parts_stored, 16)
                if maxima_of:
                    load_negm(*maxima_of, 0)
                sp.dma_start(parts_dram[b, 1, :, 2:4, :], parts[:, 3:1:-1, :]).then_inc(parts_stored, 16)

            def load_ctx_k(b, par):
                wait_alone(sp, qkf_ready, 2 * b - 2)
                sp.dma_start(ctx_k[:, par, :], ctx_in[b]).then_inc(ctxk_loaded[par], 16)

            def load_qk(b, par, g):
                wait_alone(sp, parts_stored, 48 * b + 48)
                wait_alone(sp, sk_ready, 8 * (b - 2) + 4 * g + 4)
                for i, dst in ((0, qop), (1, kop)):
                    src = parts_dram[b, i].rearrange("(j g d) t f -> g (d t) j f", g=2, d=HD)[g]
                    sp.dma_start(dst[0:64, par, g], src).then_inc(qk_loaded[par][g], 16)

            def load_negm(b, par, g):
                wait_alone(sp, negm_copied, 2 * b + g + 1)
                sp.dma_start(qop[64:65, par, g].rearrange("o j (c q) -> o (j c) q", c=2),
                             negmT[0:8, g, :]).then_inc(negm_loaded[g], 16)

            def weights(b, i):
                wait_alone(sp, wlo_ready[i], 2 * b)
                src = (w1, w2)[i][bass.ds(b, 1)].rearrange("o (c p) i -> p (o c) i", p=128)
                sp.dma_start(wstage[:, i, :].rearrange("p (c i) -> p c i", c=(KC, IC)[i]), src).then_inc(w_loaded[i], 16)

            def iteration(b, par):
                if has(b + LEAD + 1):
                    load_ctx_k(b + LEAD + 1, par)
                if has(b + 2):
                    wait_alone(sp, v_turned, b + 1)
                    sp.dma_start(ctx_v[:, par, :], ctx_in[b + 2]).then_inc(ctxv_loaded[par], 16)
                if has(b):
                    load_negm(b, par, 1)
                if has(b + 1, 1, E):
                    weights(b + 1, 0)
                if has(b + 2):
                    load_qk(b + 2, par, 0)
                if has(b - 2):
                    wait_alone(sp, hi2_ready, b - 1)
                    wait_alone(sp, lo2_ready, b - 1)
                    sp.dma_start(xn2_dram[bass.ds((b - 2) * S, S)], xn2hl[:]).then_inc(xn2_stored, 16)
                if has(b + LEAD):
                    store_parts(b + LEAD, (b + 1, 1 - par))
                elif has(b + 1):
                    load_negm(b + 1, 1 - par, 0)
                if has(b + 1, 1, E):
                    weights(b + 1, 1)
                if has(b + 2):
                    load_qk(b + 2, par, 1)
                if has(b, 0, B + 1):
                    for a in acc_dram:
                        sp.dma_start(a[bass.ds(b * HALF, HALF)], zeros).then_inc(zeros_stored, 16)
                if isinstance(b, int) and b == E:
                    sp.dma_start(xn2_dram[B * S:B * S + HALF].rearrange("p h f -> p (h f)"),
                                 zeros.bitcast(F16)).then_inc(pads_stored, 16)
                    sp.dma_start(pred[:, 0:1], bp1.rearrange("(p o) -> p o", o=1)).then_inc(pred_loaded, 16)
                    sp.dma_start(pred[:, 1:2], Wp2).then_inc(pred_loaded, 16)
                    sp.dma_start(pred[:, 2:3], bp2.partition_broadcast(128)).then_inc(pred_loaded, 16)

            store_parts(0)
            for g in range(2):
                load_qk(0, 0, g)
            sp.wait_ge(zeros_set, 2)
            load_ctx_k(2, 0)
            store_parts(1)
            load_ctx_k(3, 1)
            for g in range(2):
                load_qk(1, 1, g)
            load_negm(0, 0, 0)
            weights(0, 0)
            weights(0, 1)
            store_parts(2)
            batches(sp, iteration)
            sp.wait_ge(x1_ready, B)
            sp.dma_start(b1s, b1.rearrange("e (c i) -> (e c) i", i=128)).then_inc(b1_loaded, 16)
            sp.wait_ge(sk_ready, HEADS * B)
            sp.dma_start(b2w.rearrange("p e d -> p (e d)"),
                         b2.rearrange("e d -> (e d)").partition_broadcast(128)).then_inc(b2_loaded, 16)
            sp.wait_ge(table_made, made("b2w"))
            sp.dma_start(wp1_s, Wp1.rearrange("(c p) j -> p c j", p=128)).then_inc(pred_loaded, 16)
            load_sums(sp, 0)
            for q in range(0, 4, 2):
                store_out(sp, q)
            sp.wait_ge(out_stored, 16 * 4)

        @block.gpsimd
        def _(pool):
            g = nc.gpsimd
            g.memset(neghalf[:], -0.5).then_inc(pool_const, 1)
            g.memset(eps_s[:], EPS).then_inc(pool_const, 1)
            for m, start in ((ident, 0.0), (ident16, 0.0), (upper16, 1.0)):
                g.memset(m[:], start).then_inc(pool_const, 1)
            g.memset(ones16[:], 1.0).then_inc(pool_const, 1)
            pool.wait_ge(pool_const, 6)
            g.memset(qop[64:128].bitcast(F32), 0.0).then_inc(pool_const, 1)
            pool.wait_ge(pool_const, 7)
            for m in (ident, ident16):
                g.affine_select(out=m[:], in_=m[:], compare_op=ALU.not_equal, fill=1.0, base=0,
                                pattern=[[-1, 128]], channel_multiplier=1).then_inc(pool_const, 1)
            g.affine_select(out=upper16[:], in_=upper16[:], compare_op=ALU.is_gt, fill=0.0, base=0,
                            pattern=[[1, 128]], channel_multiplier=-1).then_inc(pool_const, 1)
            g.iota(iota_e[:], pattern=[[1, E]], base=0, channel_multiplier=0,
                   allow_small_or_imprecise_dtypes=True).then_inc(pool_const, 1)

            g.iota(row_of[:], pattern=[[0, 1]], base=0, channel_multiplier=1,
                   allow_small_or_imprecise_dtypes=True).then_inc(pool_const, 1)
            g.memset(zeros, 0.0).then_inc(zeros_set, 1)
            g.memset(zero_i[:], 0).then_inc(zeros_set, 1)

            def rstd(mv, rs, b, par, mv_ready, ve_ready, rs_ready, k):
                wait_some(pool, rs_ready, b)
                pool.wait_ge(mv_ready, b + 1)
                g.tensor_tensor(vpe[:, k:k + 1], mv[:, par, 1:2], eps_s[:], ALU.add).then_inc(ve_ready, 1)
                pool.wait_ge(ve_ready, b + 1)
                g.tensor_tensor(rs[:, par:par + 1], vpe[:, k:k + 1], neghalf[:], ALU.pow).then_inc(rs_ready, 1)

            def weight_low(b, i, h):
                pool.wait_ge(whi_ready, 4 * b + 2 * i + h + 1)
                hi, lo, src = weight_parts(b, i, h)
                g.tensor_tensor(lo, src, hi, ALU.subtract).then_inc(wlo_ready[i], 1)

            def low(b):
                pool.wait_ge(qkf_ready, 2 * b + 2)
                pool.wait_ge(hi_ready, b + 1)
                wait_some(pool, parts_stored, 48 * b)
                g.tensor_tensor(parts[:, 1:4:2, :], qkf[:], parts[:, 0:3:2, :], ALU.subtract).then_inc(lo_ready, 1)

            def iteration(b, par):
                if has(b, 0, E):
                    weight_low(b, 0, 0)
                if has(b, 0, E):
                    weight_low(b, 0, 1)
                if has(b - 2):
                    pool.wait_ge(hi2_ready, b - 1)
                    wait_some(pool, xn2_stored, 16 * (b - 2))
                    g.tensor_tensor(xn2hl[:, 1, :], xn2[:], xn2hl[:, 0, :], ALU.subtract).then_inc(lo2_ready, 1)
                if has(b + LEAD):
                    low(b + LEAD)
                if has(b - 1):
                    pool.wait_ge(att_ready, b)
                    g.tensor_tensor(x_all[:, bass.ds(b - 1, 1), :].squeeze(1), x_all[:, bass.ds(b - 1, 1), :].squeeze(1), att[:],
                                    ALU.add).then_inc(x1_ready, 1)
                    rstd(mv2, rs2, b - 1, 1 - par, mv2_ready, ve2_ready, rs2_ready, 1)
                if has(b + LEAD + 1):
                    rstd(mv1, rs1, b + LEAD + 1, par, mv1_ready, ve1_ready, rs1_ready, 0)

            rstd(mv1, rs1, 0, 0, mv1_ready, ve1_ready, rs1_ready, 0)
            rstd(mv1, rs1, 1, 1, mv1_ready, ve1_ready, rs1_ready, 0)
            low(0)
            low(1)
            rstd(mv1, rs1, 2, 0, mv1_ready, ve1_ready, rs1_ready, 0)
            low(2)
            rstd(mv1, rs1, 3, 1, mv1_ready, ve1_ready, rs1_ready, 0)
            batches(pool, iteration)

            pool.wait_ge(parts_stored, 48 * B)
            pool.wait_ge(v_turned, B)
            g.iota(iota_s, pattern=[[1, HALF]], base=0, channel_multiplier=0,
                   allow_small_or_imprecise_dtypes=True).then_inc(iotas_set, 1)
            g.iota(small[:, 9, :].rearrange("p (b c) -> p b c", c=TOPK), pattern=[[S, B], [0, TOPK]], base=-B * S,
                   channel_multiplier=1, allow_small_or_imprecise_dtypes=True).then_inc(iotas_set, 1)
            pool.wait_ge(lo2_ready, B)
            pool.wait_ge(xn2_turned, B)
            g.memset(sum_w, 1.0).then_inc(iotas_set, 1)
            g.memset(mean_w, 0.0).then_inc(iotas_set, 1)
            pool.wait_ge(iotas_set, 4)
            g.memset(mean_w[:, B - 1:B], 1.0 / S).then_inc(iotas_set, 1)
            for h in range(2):
                k = slice(h * CH // 2, (h + 1) * CH // 2)
                pool.wait_ge(table_made, made(f"at_tile_{h + 1}"))
                g.tensor_tensor(at_tile[:, k], at_tile[:, k], small[:, 9, k].unsqueeze(2).to_broadcast([128, CH // 2, 2 * TILES]),
                                ALU.mult).then_inc(tile_marked, 1)

            def gather(t, par):
                wait_alone(pool, gathered[par], (t - par) * 16)
                g.tensor_tensor(gidx[par][:], idx_tab[:, bass.ds(t * 2, 2)], zero_i[:], ALU.add).then_inc(gidx_ready, 1)
                wait_alone(pool, gidx_ready, t + 1)
                wait_alone(pool, xg_turned, t - 1)
                for h in range(2):
                    g.indirect_dma_start(out=xg[:, par, h].rearrange("p h f -> p (h f)"), out_offset=None,
                                         in_=xn2_dram.rearrange("r h f -> r (h f)"),
                                         in_offset=bass.IndirectOffsetOnAxis(ap=gidx[par][:, h:h + 1], axis=0),
                                         bounds_check=B * S + HALF - 1, oob_is_err=False).then_inc(gathered[par], 16)

            def scatter(t, par):
                for h in range(2):
                    wait_alone(pool, scattered[h], t * 16)
                g.tensor_tensor(sidx[par][:], idx_tab[:, bass.ds(t * 2, 2)], zero_i[:], ALU.add).then_inc(sidx_ready, 1)
                wait_alone(pool, sidx_ready, t + 1)
                for h in range(2):
                    wait_alone(pool, y_ready, 2 * t + h + 1)
                    g.indirect_dma_start(out=acc_dram[h],
                                         out_offset=bass.IndirectOffsetOnAxis(ap=sidx[par][:, h:h + 1], axis=0),
                                         in_=y[:, par, h, :], in_offset=None, bounds_check=B * S + HALF - 1,
                                         oob_is_err=False, compute_op=ALU.add).then_inc(scattered[h], 16)

            pool.wait_ge(table_made, made("idx_tab"))
            pool.wait_ge(xn2_stored, 16 * B)
            pool.wait_ge(pads_stored, 16)
            pool.wait_ge(qkf_ready, 2 * B)
            for t in range(4):
                gather(t, t % 2)
            pool.wait_ge(zeros_stored, 32 * (B + 1))

            def tile(t, par):
                if tile_is(t + 4):
                    gather(t + 4, par)
                if tile_is(t):
                    scatter(t, par)
            tiles(pool, tile)

            for b in range(B - BY_ACT, B):
                pool.wait_ge(acc_scaled, b - (B - BY_ACT) + 1)
                g.tensor_tensor(acc_s[0][:, b, :], acc_s[0][:, b, :], x_all[:, b, :], ALU.add).then_inc(scaled_late, 1)

        @block.scalar
        def _(act):
            a = nc.scalar
            act.wait_ge(klen_float, 1)
            a.activation(lnk[:], klen_f[:], ACT.Ln).then_inc(lnk_ready, 1)
            act.wait_ge(pool_const, 2)
            a.activation(rs2[:, 0:1], eps_s[:], ACT.Exp).then_inc(exp_warm, 1)

            def high(b):
                act.wait_ge(qkf_ready, 2 * b + 2)
                wait_some(act, parts_stored, 48 * b)
                a.activation(parts[:, 0:3:2, :], qkf[:], ACT.Copy).then_inc(hi_ready, 1)

            def copy_negm(b, g):
                act.wait_ge(negm_turned, 2 * b + g + 1)
                wait_some(act, negm_loaded[g], 16 * b)
                a.activation(negmT[:, g, :], negm_ps[0:8, :], ACT.Copy).then_inc(negm_copied, 1)

            def copy_v(b, par):
                act.wait_ge(v_turned, b + 1)
                wait_some(act, av_ready, 2 * (b - 2) + 2)
                src = misc_a[:, 0:KC * 128].rearrange("p (c j g d) -> p c j g d", c=KC, g=2, d=HD)
                for g in range(2):
                    a.activation(vst[:, par, :, :, g, HD * g:HD * g + HD], src[:, :, :, g, :],
                                 ACT.Copy).then_inc(v_ready, 1)

            def exps(b, par, s):
                g, j = divmod(s, PAIRS)
                act.wait_ge(sk_ready, 8 * b + s + 1)
                if j == 0:
                    wait_some(act, av_ready, 2 * b + g - 1)
                a.activation(prob[:, g, j], sk[s % 2][:].rearrange("p (c q) -> p c q", c=KC),
                             ACT.Exp).then_inc(prob_ready, 1)

            def weight_hi(b, i, h):
                if h == 0:
                    act.wait_ge(w_loaded[i], 16 * b + 16)
                hi, _, src = weight_parts(b, i, h)
                if i in BY_POOL:
                    if h == 0:
                        a.activation(wstage[:, i], wstage[:, i], ACT.Copy, scale=WS).then_inc(wscaled, 1)
                        act.wait_ge(wscaled, len(BY_POOL) * b + len(BY_POOL[:i]) + 1)
                    a.activation(hi, src, ACT.Copy).then_inc(whi_ready, 1)
                else:
                    a.activation(hi, src, ACT.Copy, scale=WS).then_inc(whi_ready, 1)

            def iteration(b, par):
                for s in range(HEADS):
                    if has(b):
                        exps(b, par, s)
                    if s == 2 and has(b - 2):
                        act.wait_ge(xn2_turned, b - 1)
                        a.activation(xn2T[:], misc_b[:, 0:256].rearrange("p (c t) -> p c t", c=KC),
                                     ACT.Copy).then_inc(xn2T_ready, 1)
                        wait_some(act, xn2_stored, 16 * (b - 2))
                        a.activation(xn2hl[:, 0, :], xn2[:], ACT.Copy).then_inc(hi2_ready, 1)
                    if s == 1 and has(b):
                        copy_negm(b, 1)
                    if s == 5 and has(b + 1):
                        copy_negm(b + 1, 0)
                    if s == 6 and has(b + 1):
                        copy_v(b + 1, 1 - par)
                    if s in (0, 1, 3, 4) and has(b, 0, E):
                        k = (0, 1, 3, 4).index(s)
                        weight_hi(b, k // 2, k % 2)
                    if s == 2 and has(b + LEAD):
                        high(b + LEAD)

            high(0)
            high(1)
            act.wait_ge(dve_const, 1)
            copy_v(0, 0)
            copy_negm(0, 0)
            high(2)
            batches(act, iteration)

            act.wait_ge(b1_turned, 1)
            a.activation(b1T[:].rearrange("p e c -> p (e c)"), misc_b[:, 0:E * IC], ACT.Copy).then_inc(b1T_ready, 1)
            act.wait_ge(table_made, made("l_sub"))
            a.activation(lexp, lexp, ACT.Exp).then_inc(exp_made, 1)
            act.wait_ge(table_made, made("top_sub"))
            a.activation(small[:, 3, :], small[:, 3, :], ACT.Exp).then_inc(exp_made, 1)
            act.wait_ge(table_made, made("p3_sub"))
            a.activation(small[:, 4, :], small[:, 4, :], ACT.Exp).then_inc(exp_made, 1)
            act.wait_ge(b1T_ready, 1)
            act.wait_ge(zeros_stored, 32 * (B + 1))
            act.wait_ge(pads_stored, 16)
            act.wait_ge(av_ready, 2 * B)

            def tile(t, par):
                if not tile_is(t):
                    return
                e = act.value_load(exp_tab[0:1, bass.ds(t, 1)], min_val=0, max_val=E - 1)
                for c in range(IC):
                    act.wait_ge(h_summed, IC * t + c + 1)
                    if c in (0, 3):
                        wait_some(act, hid_lo_ready, 2 * (t - 1) + (1 if c == 0 else 2))
                    a.activation(hid[:, c, :], bank[c][:, 0:SLOTS], ACT.Relu, bias=b1T[:, bass.ds(e, 1), c],
                                 scale=1.0 / WS).then_inc(hid_ready, 1)
                    if c in (2, 4):
                        first = 0 if c == 2 else 3
                        wait_alone(act, hid_ready, IC * t + c + 1)
                        if c == 2:
                            wait_some(act, y_summed, 2 * t - 2)
                        a.activation(hid_hi[:, par, first:c + 1, :], hid[:, first:c + 1, :], ACT.Copy).then_inc(hid_hi_ready, 1)
            act.wait_ge(table_made, made("exp_tab"))
            tiles(act, tile)

            load_sums(act, 1)
            act.wait_ge(z1_summed, 1)
            a.activation(z1T, bank[1][:, 64:64 + B], ACT.Relu, bias=pred[:, 0:1]).then_inc(z1_ready, 1)
            act.wait_ge(phi_summed, 1)
            a.activation(factor, bank[1][:, 96:96 + B], ACT.Exp, bias=pred[:, 2:3], scale=-1.0).then_inc(phi_exp, 1)
            act.wait_ge(factor_ready, 4)
            for q in range(4):
                act.wait_ge(acc_summed[q], 1)
            for b in range(B - BY_ACT, B):
                a.activation(acc_s[0][:, b, :], acc_s[0][:, b, :], ACT.Copy, scale=factor[:, b:b + 1]).then_inc(acc_scaled, 1)
            for q in range(1, 4, 2):
                store_out(act, q)

        @block.vector
        def _(dve):
            v = nc.vector
            dve.wait_ge(klen_loaded, 16)
            v.tensor_copy(klen_f[:], klen_i[:]).then_inc(klen_float, 1)

            def stats(b, par, bn, mv, bn_ready, mv_ready):
                wait_some(dve, mv_ready, b)
                v.bn_stats(bn[:], x_all[:, bass.ds(b, 1), :].squeeze(1)).then_inc(bn_ready, 1)
                wait_alone(dve, qkf_ready if bn is bn1 else xn2_ready, 2 * b - 3 if bn is bn1 else b - 1)
                wait_alone(dve, bn_ready, b + 1)
                v.bn_aggr(mv[:, par, :], bn[:]).then_inc(mv_ready, 1)

            def operands(b, par):
                dve.wait_ge(rs1_ready, b + 1)
                wait_some(dve, lo_ready, b)
                v.tensor_scalar(qkf[:, 0, :], x_all[:, bass.ds(b, 1), :].squeeze(1), mv1[:, par, 0:1], rs1[:, par:par + 1],
                                ALU.subtract, ALU.mult).then_inc(qkf_ready, 1)
                dve.wait_ge(ctxk_loaded[par], per_parity(b, par, 16))
                v.tensor_scalar(qkf[:, 1, :], ctx_k[:, par, :], lnk[:, bass.ds(b, 1)], SCALE,
                                ALU.mult, ALU.mult).then_inc(qkf_ready, 1)

            def maximum(b, s):
                g, j = divmod(s, PAIRS)
                dve.wait_ge(sq_ready, 8 * b + s + 1)
                if j == 0:
                    wait_some(dve, negm_turned, 2 * (b - 1) + g + 1)
                v.tensor_reduce(negm[:, g, j], sq[s % 2][:].rearrange("p (c k) -> p c k", c=2), AX.X, ALU.max,
                                negate=True).then_inc(max_ready, 1)

            def weight_lo(b, i, h):
                dve.wait_ge(whi_ready, 4 * b + 2 * i + h + 1)
                hi, lo, src = weight_parts(b, i, h)
                v.scalar_tensor_tensor(lo, src, WS, hi, ALU.mult, ALU.subtract).then_inc(wlo_ready[i], 1)

            def route(b, step):
                bb = bass.ds(b, 1)
                if step == 0:
                    dve.wait_ge(lg_summed, b + 1)
                    wait_some(dve, kept_ready, 2 * b)
                    wait_some(dve, mask_ready, b)
                    v.tensor_tensor(lg[:], misc_b[:, 0:E], br_s[:], ALU.add).then_inc(lg_ready, 1)
                elif step == 1:
                    wait_alone(dve, lg_ready, b + 1)
                    v.max(top8[:], lg[:]).then_inc(top_ready, 1)
                elif step == 2:
                    wait_alone(dve, top_ready, b + 1)
                    v.max_index(idx8[:], top8[:], lg[:]).then_inc(idx_ready, 1)
                    v.tensor_scalar(lg_all[:, bb, :].squeeze(1), lg[:], 0.0, None, ALU.add).then_inc(kept_ready, 1)
                    v.tensor_scalar(top_all[:, bb, :].squeeze(1), top8[:, 0:TOPK], 0.0, None,
                                    ALU.add).then_inc(kept_ready, 1)
                elif step == 3:
                    dve.wait_ge(idx_ready, b + 1)
                    v.tensor_scalar(idx_all[:, bb, :].squeeze(1), idx8[:, 0:TOPK], 0.0, None,
                                    ALU.add).then_inc(idxf_ready, 1)
                elif step == 4:
                    dve.wait_ge(idxf_ready, b + 1)
                    v.tensor_tensor(onehot[:, bb].squeeze(1), iota_e[:].unsqueeze(1).to_broadcast([128, TOPK, E]),
                                    idx_all[:, bb, :].squeeze(1).unsqueeze(2).to_broadcast([128, TOPK, E]),
                                    ALU.is_equal).then_inc(oh_ready, 1)
                elif step == 5:
                    dve.wait_ge(oh_ready, b + 1)
                    with nc.allow_low_precision("zeros and ones are exact in float16"):
                        v.tensor_reduce(mask[:, bb, :].squeeze(1), onehot[:, bb].squeeze(1).rearrange("p c e -> p e c"), AX.X,
                                        ALU.add).then_inc(mask_ready, 1)
                elif step == 6:
                    dve.wait_ge(mask_ready, b + 1)
                    v.tensor_tensor(seen[:, bass.ds(b + 1, 1), :].squeeze(1), seen[:, bb, :].squeeze(1),
                                    mask[:, bb, :].squeeze(1), ALU.add).then_inc(seen_ready, 1)

            def iteration(b, par):
                for s in range(HEADS):
                    if has(b + 1):
                        maximum(b + 1, s)
                    if s == 1 and has(b - 2):
                        dve.wait_ge(rs2_ready, b - 1)
                        wait_some(dve, lo2_ready, b - 2)
                        wait_some(dve, xn2_turned, b - 2)
                        v.tensor_scalar(xn2[:], x_all[:, bass.ds(b - 2, 1), :].squeeze(1), mv2[:, par, 0:1],
                                        rs2[:, par:par + 1], ALU.subtract, ALU.mult).then_inc(xn2_ready, 1)
                    if s == 2 and has(b + LEAD):
                        operands(b + LEAD, 1 - par)
                    if s == 2 and has(b + LEAD + 1):
                        stats(b + LEAD + 1, par, bn1, mv1, bn1_ready, mv1_ready)
                    if s == 3 and has(b - 1):
                        dve.wait_ge(av_ready, 2 * b)
                        wait_some(dve, x1_ready, b - 1)
                    if s in (3, 4) and has(b - 1):
                        q = slice(0, D // 2) if s == 3 else slice(D // 2, D)
                        v.reciprocal(att[:, q], av[1 - par][:, D:2 * D][:, q]).then_inc(rden_ready, 1)
                    if s == 4 and has(b - 1):
                        dve.wait_ge(rden_ready, 2 * b)
                        v.tensor_tensor(att[:], av[1 - par][:, 0:D], att[:], ALU.mult).then_inc(att_ready, 1)
                    if s in (5, 6) and has(b, 0, E):
                        weight_lo(b, 1, (5, 6).index(s))
                    if s == 7 and has(b - 1):
                        dve.wait_ge(x1_ready, b)
                        stats(b - 1, 1 - par, bn2, mv2, bn2_ready, mv2_ready)
                    if has(b - 2):
                        for step in ROUTE_AT[s]:
                            route(b - 2, step)

            dve.wait_ge(x_first, 16)
            stats(0, 0, bn1, mv1, bn1_ready, mv1_ready)
            stats(1, 1, bn1, mv1, bn1_ready, mv1_ready)
            dve.wait_ge(lnk_ready, 1)
            dve.wait_ge(exp_warm, 1)
            operands(0, 0)
            operands(1, 1)
            v.memset(vst[:], 0.0).then_inc(dve_const, 1)
            v.memset(ones32[:], 0.0).then_inc(dve_const, 1)
            v.memset(seen[:, 0, :], 0.0).then_inc(dve_const, 1)
            v.memset(kop[64:128].bitcast(F32), 0.0).then_inc(dve_const, 1)
            dve.wait_ge(dve_const, 4)
            v.memset(ones32[:, 0, 0:HD], 1.0).then_inc(dve_const, 1)
            v.memset(ones32[:, 1, HD:2 * HD], 1.0).then_inc(dve_const, 1)
            v.memset(kop[64:65], 1.0).then_inc(dve_const, 1)
            dve.wait_ge(x_rest, 16)
            stats(2, 0, bn1, mv1, bn1_ready, mv1_ready)
            stats(3, 1, bn1, mv1, bn1_ready, mv1_ready)
            for s in range(HEADS):
                maximum(0, s)
            operands(2, 0)
            batches(dve, iteration)

            def turned_rows(t, par):
                dve.wait_ge(xg_turned, t + 1)
                wait_some(dve, h_summed, IC * (t - 1))
                v.tensor_copy(xT[:, par].rearrange("p k s -> p (k s)"), bank[5][:].bitcast(F16)).then_inc(xT_ready, 1)

            done = [0]

            def step(name, op):
                assert STEPS[done[0]] == name
                done[0] += 1
                op.then_inc(table_made, 1)

            def after(name):
                dve.wait_ge(table_made, made(name))

            def tt(name, o, i0, i1, op):
                step(name, v.tensor_tensor(o, i0, i1, op))

            small_exp = prefix.rearrange("p b e -> p (b e)")[:, 0:TILES + 1]
            cnt_ps, prefix_ps = misc_a[:, B * E:B * E + E], misc_a[:, 0:B * E].rearrange("p (b e) -> p b e", e=E)
            tri = tile_cmp[:, 0:E, :]
            full = tile_cmp[:, E:2 * E + 4, :].rearrange("p t e -> p (t e)").rearrange("p (e k) -> p e k", k=B)
            num = small[:, :, 0:E]
            cnt, n_tiles, end, base = num[:, 5], num[:, 6], num[:, 7], num[:, 8]
            pos = small[:, 0, :]
            pos_i, cut_i, cut2_i = small[:, 1, :].bitcast(I32), small[:, 2, :].bitcast(I32), small[:, 3, :].bitcast(I32)
            dve.wait_ge(iotas_set, 4)
            for lo_ready_i in wlo_ready:
                dve.wait_ge(lo_ready_i, 2 * E)
            dve.wait_ge(av_ready, 2 * B)
            tt("triangle", tri, iota_e[:].unsqueeze(2).to_broadcast([128, E, E]),
               iota_e[:].unsqueeze(1).to_broadcast([128, E, E]), ALU.is_ge)
            dve.wait_ge(counted, 1)
            step("cnt", v.tensor_scalar(cnt, cnt_ps, 1.0 / SLOTS, None, ALU.mult))
            after("cnt")
            tt("full", full, cnt.unsqueeze(2).to_broadcast([128, E, B]),
               iota_s[:, 0:B].unsqueeze(1).to_broadcast([128, E, B]), ALU.is_gt)
            after("full")
            step("tiles", v.tensor_reduce(n_tiles, full, AX.X, ALU.add))
            after("tiles")
            tt("tri_tiles", tri, tri, n_tiles.unsqueeze(1).to_broadcast([128, E, E]), ALU.mult)
            after("tri_tiles")
            step("end", v.tensor_reduce(end, tri, AX.X, ALU.add))
            after("end")
            tt("base", base, end, n_tiles, ALU.subtract)
            after("base")
            step("prefix", v.scalar_tensor_tensor(prefix, base.unsqueeze(1).to_broadcast([128, B, E]), float(SLOTS),
                                                  prefix_ps, ALU.mult, ALU.add))
            after("prefix")
            tt("oh_val", oh_val, onehot[:], prefix.unsqueeze(2).to_broadcast([128, B, TOPK, E]), ALU.mult)
            after("oh_val")
            step("pos", v.tensor_reduce(pos.rearrange("p (b c) -> p b c", c=TOPK), oh_val, AX.X, ALU.add))
            after("pos")
            step("pos_i", v.tensor_scalar(pos_i, pos, 0.0, None, ALU.add))
            after("pos_i")
            step("slot_i", v.tensor_scalar(cut_i, pos_i, HALF - 1, None, ALU.bitwise_and))
            after("slot_i")
            step("slot", v.tensor_scalar(slot_of[:], cut_i, 0.0, None, ALU.add))
            step("tile_i", v.tensor_scalar(cut2_i, pos_i, HALF.bit_length() - 1, None, ALU.arith_shift_right))
            after("tile_i")
            step("tile", v.tensor_scalar(tile_of[:], cut2_i, 0.0, None, ALU.add))
            after("tile")
            for h in range(2):
                k = slice(h * CH // 2, (h + 1) * CH // 2)
                tt(f"at_tile_{h + 1}", at_tile[:, k], iota_s[:, 0:2 * TILES].unsqueeze(1).to_broadcast([128, CH // 2, 2 * TILES]),
                   tile_of[:, k].unsqueeze(2).to_broadcast([128, CH // 2, 2 * TILES]), ALU.is_equal)
            for h in range(2):
                k = slice(h * CH // 2, (h + 1) * CH // 2)
                tt(f"at_slot_{h + 1}", at_slot[:, k, :], iota_s.unsqueeze(1).to_broadcast([128, CH // 2, HALF]),
                   slot_of[:, k].unsqueeze(2).to_broadcast([128, CH // 2, HALF]), ALU.is_equal)
            tt("exp_cmp", tile_cmp, iota_s[:, 0:TILES + 1].unsqueeze(2).to_broadcast([128, TILES + 1, E]),
               end.unsqueeze(1).to_broadcast([128, TILES + 1, E]), ALU.is_ge)
            after("exp_cmp")
            step("exp_sum", v.tensor_reduce(small_exp, tile_cmp, AX.X, ALU.add))
            after("exp_sum")
            step("exp_tab", v.tensor_scalar(exp_tab[:], small_exp, float(E - 1), None, ALU.min))
            dve.wait_ge(table_summed, 1)
            T = misc_b[:, 64:64 + 2 * TILES]
            fill = tile_cmp.rearrange("p t e -> p (t e)")[:, 0:2 * TILES]
            after("exp_sum")
            step("idx_fill", v.tensor_scalar(fill, T, 0.0, row_of[:], ALU.is_equal, ALU.mult))
            after("idx_fill")
            step("idx_tab", v.scalar_tensor_tensor(idx_tab[:], T, float(B * S), fill, ALU.add, ALU.add))

            def ch(k):
                return small[:, k, :].rearrange("p (b c) -> p b c", c=TOPK)

            s0, s1 = ch(3), ch(4)
            z, rz = small[:, 2, 0:B], small[:, 2, B:2 * B]
            tt("l_sub", lexp, lg_all[:], top_all[:, :, 0:1].to_broadcast([128, B, E]), ALU.subtract)
            tt("top_sub", s0, top_all[:], top_all[:, :, 0:1].to_broadcast([128, B, TOPK]), ALU.subtract)
            dve.wait_ge(exp_made, 1)
            step("z", v.tensor_reduce(z, lexp, AX.X, ALU.add))
            after("z")
            step("rz", v.reciprocal(rz, z))
            after("rz")
            dve.wait_ge(exp_made, 2)
            tt("p3", s0, s0, rz.unsqueeze(2).to_broadcast([128, B, TOPK]), ALU.mult)
            after("p3")
            tt("p3_sub", s1, s0, s0[:, :, 0:1].to_broadcast([128, B, TOPK]), ALU.subtract)
            dve.wait_ge(exp_made, 3)
            step("ew_sum", v.tensor_reduce(z, s1, AX.X, ALU.add))
            after("ew_sum")
            step("ew_rsum", v.reciprocal(rz, z))
            after("ew_rsum")
            tt("ew", s1, s1, rz.unsqueeze(2).to_broadcast([128, B, TOPK]), ALU.mult)
            after("ew")
            tt("oh_w", oh_val, onehot[:], s1.unsqueeze(3).to_broadcast([128, B, TOPK, E]), ALU.mult)
            after("oh_w")
            step("w_part", v.tensor_reduce(num[:, 7], oh_val.rearrange("p b c e -> p e (b c)"), AX.X, ALU.add))
            step("cnt_1", v.tensor_scalar(num[:, 1], cnt_ps, 1.0, None, ALU.max))
            after("cnt_1")
            step("cnt_r", v.reciprocal(num[:, 8], num[:, 1]))
            after("cnt_r")
            turned_rows(0, 0)
            dve.wait_ge(weight_summed, 1)
            tt("w_e", w_e[:, 0], misc_b[:, 256:256 + E], num[:, 8], ALU.mult)
            after("w_e")
            step("w_e_ws", v.tensor_scalar(w_e[:, 1], w_e[:, 0], 1.0 / WS, None, ALU.mult))

            def low_parts(t, par):
                for h, (first_c, last_c) in enumerate(((0, 3), (3, IC))):
                    dve.wait_ge(hid_hi_ready, 2 * t + h + 1)
                    v.tensor_tensor(hid_lo[:, par, first_c:last_c, :], hid[:, first_c:last_c, :],
                                    hid_hi[:, par, first_c:last_c, :], ALU.subtract).then_inc(hid_lo_ready, 1)

            def output(t, par):
                e = dve.value_load(exp_tab[0:1, bass.ds(t, 1)], min_val=0, max_val=E - 1)
                w = w_e[:, 1, bass.ds(e, 1)]
                for h in range(2):
                    wait_alone(dve, y_summed, 2 * t + h + 1)
                    wait_alone(dve, scattered[h], (t - 1) * 16)
                    v.scalar_tensor_tensor(y[:, par, h, :], bank[6 + h][:, 0:D], w, b2w[:, bass.ds(e, 1), :].squeeze(1),
                                           ALU.mult, ALU.add).then_inc(y_half, 1)
                for h in range(2):
                    wait_alone(dve, y_half, 2 * t + h + 1)
                    v.scalar_tensor_tensor(y[:, par, h, :], bank[6 + h][:, D:2 * D], w, y[:, par, h, :],
                                           ALU.mult, ALU.add).then_inc(y_ready, 1)

            def tile(t, par):
                if tile_is(t):
                    low_parts(t, par)
                if tile_is(t - 1):
                    output(t - 1, 1 - par)
                if tile_is(t + 2):
                    turned_rows(t + 2, par)
            turned_rows(1, 1)
            dve.wait_ge(b2_loaded, 16)
            tt("b2w", b2w, b2w, w_e[:, 0].unsqueeze(2).to_broadcast([128, E, D]), ALU.mult)
            after("b2w")
            dve.wait_ge(pred_loaded, 48)
            v.tensor_scalar(pred[:, 2:3], pred[:, 2:3], -1.0, None, ALU.mult).then_inc(table_made, 1)
            tiles(dve, tile)

            for q in range(4):
                dve.wait_ge(acc_loaded[q], 32)
                part = slice(q * QB, (q + 1) * QB)
                v.tensor_tensor(acc_s[0][:, part, :], acc_s[0][:, part, :], acc_s[1][:, part, :],
                                ALU.add).then_inc(acc_summed[q], 1)
            dve.wait_ge(pooled, 1)
            v.tensor_copy(pooled_s[0:B, :], bank[0][0:B, 0:D]).then_inc(pooled_copied, 1)
            dve.wait_ge(pooled_turned, 1)
            v.tensor_copy(pooledT.rearrange("p k b -> p (k b)"), bank[1][:, 0:KC * B]).then_inc(pooledT_ready, 1)
            dve.wait_ge(phi_exp, 1)
            v.tensor_scalar(factor, factor, 1.0, None, ALU.add).then_inc(factor_ready, 1)
            dve.wait_ge(factor_ready, 1)
            v.reciprocal(factor, factor).then_inc(factor_ready, 1)
            dve.wait_ge(factor_ready, 2)
            v.tensor_scalar(factor, factor, 0.7, -0.8, ALU.is_gt, ALU.mult).then_inc(factor_ready, 1)
            dve.wait_ge(factor_ready, 3)
            v.tensor_scalar(factor, factor, 1.0, None, ALU.add).then_inc(factor_ready, 1)
            dve.wait_ge(factor_ready, 4)
            for q in range(4):
                dve.wait_ge(acc_summed[q], 1)
            for b in range(B - BY_ACT):
                v.scalar_tensor_tensor(acc_s[0][:, b, :], acc_s[0][:, b, :], factor[:, b:b + 1], x_all[:, b, :],
                                       ALU.mult, ALU.add).then_inc(scaled, 1)

        @block.tensor
        def _(pe):
            t = nc.tensor

            def scores_q(b, par, s):
                g, j = divmod(s, PAIRS)
                if j == 0:
                    pe.wait_ge(qk_loaded[par][g], per_parity(b, par, 32))
                wait_some(pe, max_ready, 8 * b + s - 1)
                for c in range(2):
                    mm = t.matmul(sq[s % 2][:, c * D:(c + 1) * D], qop[0:64, par, g, j, c * 128:(c + 1) * 128],
                                  kop[0:64, par, g, j, :], start=True, stop=True)
                mm.then_inc(sq_ready, 1)

            def scores_k(b, par, s):
                g, j = divmod(s, PAIRS)
                if j == 0:
                    pe.wait_ge(negm_loaded[g], 16 * b + 16)
                wait_some(pe, prob_ready, 8 * b + s - 1)
                for c in range(KC):
                    mm = t.matmul(sk[s % 2][:, c * D:(c + 1) * D], kop[:, par, g, j, c * 128:(c + 1) * 128],
                                  qop[:, par, g, j, :], start=True, stop=True)
                mm.then_inc(sk_ready, 1)

            def sums(b, par, g, quarter):
                c, what = divmod(quarter, 2)
                if quarter == 0:
                    pe.wait_ge(prob_ready, 8 * b + 4 * g + 4)
                    if g == 0:
                        pe.wait_ge(v_ready, 2 * b + 2)
                        wait_some(pe, att_ready, b - 1)
                for j in range(PAIRS):
                    lhs = vst[:, par, c, j, g, :] if what == 0 else ones32[:, g, :]
                    mm = t.matmul(av[par][32 * j:32 * j + 32, what * D:(what + 1) * D], lhs, prob[:, g, j, c, :],
                                  start=(g == 0 and quarter == 0), stop=(g == 1 and c == 1),
                                  skip_group_check=True)
                if quarter == 3:
                    mm.then_inc(av_ready, 1)

            def turn_negm(b, g):
                pe.wait_ge(max_ready, 8 * b + 4 * g + 4)
                if g == 1 or (isinstance(b, int) and b == 0):
                    pe.wait_ge(v_ready, 2 * b + 2)
                else:
                    pe.wait_ge(negm_copied, 2 * b)
                t.transpose(negm_ps[0:8, :], negm[:, g].rearrange("p j c -> p (j c)"),
                            ident16[:]).then_inc(negm_turned, 1)

            def turn_v(b, par):
                pe.wait_ge(ctxv_loaded[par], per_parity(b, par, 16))
                if not (isinstance(b, int) and b == 0):
                    pe.wait_ge(negm_copied, 2 * b + 1)
                for c in range(KC):
                    mm = t.transpose(misc_a[:, c * 128:(c + 1) * 128], ctx_v[:, par, c * 128:(c + 1) * 128], ident[:])
                mm.then_inc(v_turned, 1)

            def turn_xn2(b):
                pe.wait_ge(xn2_ready, b + 1)
                wait_some(pe, lg_ready, b)
                for c in range(KC):
                    mm = t.transpose(misc_b[:, c * 128:(c + 1) * 128], xn2[:, c * 128:(c + 1) * 128], ident[:])
                mm.then_inc(xn2_turned, 1)

            def router(b):
                pe.wait_ge(xn2T_ready, b + 1)
                for c in range(KC):
                    mm = t.matmul(misc_b[:, 0:E], xn2T[:, c, :], wr_s[:, c, :], start=(c == 0), stop=(c == KC - 1))
                mm.then_inc(lg_summed, 1)

            def iteration(b, par):
                for s in range(HEADS):
                    if has(b + 1):
                        scores_q(b + 1, 1 - par, s)
                    if has(b):
                        scores_k(b, par, s)
                    for quarter in ((0,), (1,), (2, 3), ())[s % 4]:
                        if s < 4 and has(b - 1):
                            sums(b - 1, 1 - par, 1, quarter)
                        if s >= 4 and has(b):
                            sums(b, par, 0, quarter)
                    if s == 1 and has(b):
                        turn_negm(b, 1)
                    if s == 3 and has(b - 2):
                        router(b - 2)
                    if s == 5 and has(b + 1):
                        turn_negm(b + 1, 0)
                    if s == 6 and has(b + 1):
                        turn_v(b + 1, 1 - par)
                    if s == 2 and has(b - 2):
                        turn_xn2(b - 2)

            pe.wait_ge(pool_const, 11)
            turn_v(0, 0)
            for s in range(HEADS):
                scores_q(0, 0, s)
            turn_negm(0, 0)
            pe.wait_ge(dve_const, 7)
            pe.wait_ge(tables_loaded, 32)
            batches(pe, iteration)

            pe.wait_ge(seen_ready, B)
            pe.wait_ge(negm_copied, 2 * B)
            pe.wait_ge(v_ready, 2 * B)
            pe.wait_ge(lg_ready, B)
            flat = "p b e -> p (b e)"
            t.matmul(misc_a[:, 0:B * E], upper16[:], mask[:].rearrange(flat), start=True, stop=False)
            t.matmul(misc_a[:, 0:B * E], ones16[:], seen[:, 0:B].rearrange(flat), start=False, stop=True)
            t.matmul(misc_a[:, B * E:B * E + E], ones16[:], seen[:, B, :], start=True, stop=True).then_inc(counted, 1)
            pe.wait_ge(b1_loaded, 16)
            t.transpose(misc_b[:, 0:E * IC], b1s, ident[0:E * IC, 0:E * IC]).then_inc(b1_turned, 1)
            pe.wait_ge(b1T_ready, 1)
            for k in range(CH):
                if k % (CH // 2) == 0:
                    pe.wait_ge(table_made, made("at_slot_1") + k // (CH // 2))
                    pe.wait_ge(tile_marked, 1 + k // (CH // 2))
                mm = t.matmul(misc_b[:, 64:64 + 2 * TILES], at_slot[:, k, :], at_tile[:, k, :], start=(k == 0),
                              stop=(k == CH - 1))
            mm.then_inc(table_summed, 1)

            def turn_rows(n, par):
                pe.wait_ge(gathered[par], (n - par) * 16 + 32)
                if isinstance(n, int) and n < 2:
                    wait_some(pe, xT_ready, n)
                for k in range(2 * KC):
                    for h in range(2):
                        at = k * SLOTS + h * HALF
                        mm = t.transpose(bank[5][:].bitcast(F16)[:, at:at + HALF],
                                         xg[:, par, h, k // KC, (k % KC) * 128:(k % KC) * 128 + 128], ident16[:])
                mm.then_inc(xg_turned, 1)

            def hidden(n, par):
                e = pe.value_load(exp_tab[0:1, bass.ds(n, 1)], min_val=0, max_val=E - 1)
                if isinstance(n, int) and n == 0:
                    pe.wait_ge(xT_ready, 1)
                wait_some(pe, hid_ready, IC * n)
                for c in range(IC):
                    dst = bank[c][:, 0:SLOTS]
                    terms = [(wp, xp, k) for k in range(KC) for wp, xp in ((0, 0), (0, 1), (1, 0))]
                    for i, (wp, xp, k) in enumerate(terms):
                        mm = t.matmul(dst, w1s[:, bass.ds(e, 1), wp, k, c * 128:(c + 1) * 128].squeeze(1),
                                      xT[:, par, xp * KC + k, :], start=(i == 0), stop=(i == len(terms) - 1))
                    mm.then_inc(h_summed, 1)
                return e

            def outputs(n, par, e=None):
                if e is None:
                    e = pe.value_load(exp_tab[0:1, bass.ds(n, 1)], min_val=0, max_val=E - 1)
                pe.wait_ge(hid_lo_ready, 2 * n + 2)
                wait_some(pe, y_ready, 2 * n)
                for c in range(IC):
                    w = w2s[:, bass.ds(e, 1), c].squeeze(1)
                    for h in range(2):
                        rows = slice(h * HALF, (h + 1) * HALF)
                        t.matmul(bank[6 + h][:], hid_hi[:, par, c, rows], w.rearrange("p h d -> p (h d)"),
                                 start=(c == 0), stop=False, skip_group_check=True)
                        mm = t.matmul(bank[6 + h][:, D:2 * D], hid_lo[:, par, c, rows], w[:, 0, :], start=False,
                                      stop=(c == IC - 1), skip_group_check=True)
                        if c == IC - 1:
                            mm.then_inc(y_summed, 1)

            turn_rows(0, 0)
            pe.wait_ge(table_made, made("w_part"))
            t.matmul(misc_b[:, 256:256 + E], sum_w, small[:, 7, 0:E], start=True, stop=True).then_inc(weight_summed, 1)
            turn_rows(1, 1)
            hidden(0, 0)
            pe.wait_ge(table_made, made("w_e"))

            expert = [None]

            def tile(n, par):
                mine = expert[0] if par else None
                if tile_is(n + 1):
                    pe.wait_ge(xT_ready, n + 2)
                if tile_is(n + 2):
                    turn_rows(n + 2, par)
                if tile_is(n + 1):
                    expert[0] = hidden(n + 1, 1 - par)
                if tile_is(n):
                    outputs(n, par, mine)
            tiles(pe, tile)

            for b in range(B):
                if b % QB == 0:
                    pe.wait_ge(acc_summed[b // QB], 1)
                mm = t.matmul(bank[0][0:B, 0:D], mean_w[:, B - 1 - b:2 * B - 1 - b], acc_s[0][:, b, :],
                              start=(b == 0), stop=(b == B - 1))
            mm.then_inc(pooled, 1)
            pe.wait_ge(pooled_copied, 1)
            for k in range(KC):
                mm = t.transpose(bank[1][:, k * B:(k + 1) * B], pooled_s[0:B, k * 128:(k + 1) * 128], ident[0:B, 0:B])
            mm.then_inc(pooled_turned, 1)
            pe.wait_ge(pooledT_ready, 1)
            pe.wait_ge(pred_loaded, 64)
            for k in range(KC):
                mm = t.matmul(bank[1][:, 64:64 + B], wp1_s[:, k, :], pooledT[:, k, :], start=(k == 0), stop=(k == KC - 1))
            mm.then_inc(z1_summed, 1)
            pe.wait_ge(z1_ready, 1)
            t.matmul(bank[1][:, 96:96 + B], pred[:, 1:2].to_broadcast([128, 128]), z1T, start=True,
                     stop=True).then_inc(phi_summed, 1)


_INS = ["x", "ctx_2048", "itok_B_779_1933", "L0_ffn_Wr", "L0_ffn_br", "L0_ffn_w1", "L0_ffn_b1", "L0_ffn_w2",
        "L0_ffn_b2", "L0_ffn_Wp1", "L0_ffn_bp1", "L0_ffn_Wp2", "L0_ffn_bp2"]


def kernel(**inputs):
    import numpy as np
    import concourse.bacc as bacc
    from concourse.bass_utils import run_bass_kernel_spmd

    nc = bacc.Bacc("TRN2", target_bir_lowering=False, num_devices=1)
    arrays, args = {}, []
    for name in _INS:
        a = np.ascontiguousarray(inputs[name])
        arrays[name] = a
        args.append(nc.dram_tensor(name, a.shape, mybir.dt.from_np(a.dtype), kind="ExternalInput").ap())
    out = nc.dram_tensor("out", (B, S, D), F32, kind="ExternalOutput")
    build(nc, *args, out.ap())
    result = run_bass_kernel_spmd(nc, [arrays], core_ids=[0])
    return result.results[0]["out"]
```
